# Optimizing a Trainium2 kernel written in Bass

```python
import numpy as np
import jax
import jax.numpy as jnp

def _softmax(x, axis=-1):
    return jax.nn.softmax(x, axis=axis)

def _gelu(x):
    return jax.nn.gelu(x, approximate=True)

def _silu(x):
    return jax.nn.silu(x)

def _sigmoid(x):
    return jax.nn.sigmoid(x)

def _layernorm(x, axis=-1, eps=1e-05):
    m = jnp.mean(x, axis=axis, keepdims=True)
    v = jnp.var(x, axis=axis, keepdims=True)
    return (x - m) / jnp.sqrt(v + eps)

def _scatter_add(tgt, idx, src, axis=0):
    return tgt.at[idx].add(src)

def _segment_sum(src, seg, n):
    return jax.ops.segment_sum(src, seg, n)
kernel_name = 'mk_xattn_ffn_d2_seqx_r4_db55a1'

def setup_inputs(seed: int=0):
    np.random.seed(seed)
    _w = jnp.asarray

    def _rec_inputs():
        import jax
        import jax.numpy as jnp
        _rk = jax.random.key(seed)
        x = 7.22e-05 + 1 * jax.random.normal(jax.random.fold_in(_rk, 1), (4, 1024, 256), jnp.float32)
        _lenS = 1024 - jax.random.randint(jax.random.fold_in(_rk, 7), (4,), 0, max(1, 1024 // 4) + 1, jnp.int32)
        _lenS2 = 77 - jax.random.randint(jax.random.fold_in(_rk, 8), (4,), 0, max(1, 77 // 4) + 1, jnp.int32)
        _ctx_1024P = jax.random.normal(jax.random.fold_in(_rk, 11), (4, 16, 256), jnp.float32)
        _ctx_1024c = jax.random.dirichlet(jax.random.fold_in(_rk, 511), 0.3 * jnp.ones((16,), jnp.float32), (4, 77))
        _ctx_1024t = jnp.einsum('bsk,bkd->bsd', _ctx_1024c, _ctx_1024P)
        _ctx_1024t = _ctx_1024t * jax.lax.rsqrt(jnp.mean(jnp.square(_ctx_1024t)) + 1e-12) * 0.953939
        ctx_1024 = 4.13588e-05 + 0.999923 * (_ctx_1024t + 0.3 * jax.random.normal(jax.random.fold_in(_rk, 611), (4, 77, 256), jnp.float32))
        return (x, ctx_1024)
    x, ctx_1024 = _rec_inputs()

    def _L0_xattn_setup():
        import jax, jax.numpy as jnp
        import numpy as np
        B, TQ, TK, DIM = (4, 512, 512, 256)
        key = jax.random.key(seed)
        k1, k2, k3, k4 = jax.random.split(key, 4)
        inputs = jax.random.normal(k1, (B, TQ, DIM), dtype=jnp.float32)
        context = jax.random.normal(k2, (B, TK, DIM), dtype=jnp.float32)
        scale = 1.0 / np.sqrt(DIM)
        Wg = jax.random.normal(k3, (DIM, DIM), dtype=jnp.float32) * scale
        bg = jnp.zeros((DIM,), dtype=jnp.float32)
        Wo = jax.random.normal(k4, (DIM, DIM), dtype=jnp.float32) * scale
        bo = jnp.zeros((DIM,), dtype=jnp.float32)
        return {'inputs': inputs, 'context': context, 'Wg': Wg, 'bg': bg, 'Wo': Wo, 'bo': bo}
    _L0_xattn_all = _L0_xattn_setup()
    _L0_xattn_in = {k: v for k, v in _L0_xattn_all.items() if k in ('Wg', 'bg', 'Wo', 'bo')}
    del _L0_xattn_all

    def _L0_ffn_setup():
        import jax, jax.numpy as jnp
        import numpy as np
        NUM_OPS, B, T, D = (8, 8, 128, 256)
        key = jax.random.key(seed)
        k1, k2, k3, k4 = jax.random.split(key, 4)
        x = jax.random.normal(k1, (B, T, D), dtype=jnp.float32)
        W = jax.random.normal(k2, (NUM_OPS, D, D), dtype=jnp.float32) * 0.02
        b = jnp.zeros((NUM_OPS, D), dtype=jnp.float32)
        logits = 0.001 * jax.random.normal(k3, (NUM_OPS,), dtype=jnp.float32)
        u = jax.random.uniform(k4, (NUM_OPS,), dtype=jnp.float32, minval=1e-06, maxval=1.0 - 1e-06)
        return {'x': x, 'W': W, 'b': b, 'logits': logits, 'u': u}
    _L0_ffn_all = _L0_ffn_setup()
    _L0_ffn_in = {k: v for k, v in _L0_ffn_all.items() if k in ('W', 'b', 'logits', 'u')}
    del _L0_ffn_all

    def _L1_xattn_setup():
        import jax, jax.numpy as jnp
        import numpy as np
        NUM_HEADS = 16
        HEAD_SIZE = 64
        key = jax.random.key(seed)
        ks = jax.random.split(key, 6)
        B, S, CH = (2, 1024, 256)
        N, CD = (256, 256)
        x = jax.random.normal(ks[0], (B, S, CH), dtype=jnp.float32)
        c = jax.random.normal(ks[1], (B, N, CD), dtype=jnp.float32)
        c = c.at[:, N - 128:, :].set(0.0)
        sd = 1.0 / np.sqrt(CH)
        Wq = jax.random.normal(ks[2], (CH, NUM_HEADS * HEAD_SIZE), dtype=jnp.float32) * sd
        Wk = jax.random.normal(ks[3], (CD, NUM_HEADS * HEAD_SIZE), dtype=jnp.float32) * sd
        Wv = jax.random.normal(ks[4], (CD, NUM_HEADS * HEAD_SIZE), dtype=jnp.float32) * sd
        Wo = jax.random.normal(ks[5], (NUM_HEADS * HEAD_SIZE, CH), dtype=jnp.float32) * sd
        return {'x': x, 'c': c, 'Wq': Wq, 'Wk': Wk, 'Wv': Wv, 'Wo': Wo}
    _L1_xattn_all = _L1_xattn_setup()
    _L1_xattn_in = {k: v for k, v in _L1_xattn_all.items() if k in ('Wq', 'Wk', 'Wv', 'Wo')}
    del _L1_xattn_all

    def _L1_ffn_setup():
        import jax, jax.numpy as jnp
        import numpy as np
        HIDDEN = 256
        INNER = 1024

        def _weight_quant(w):
            scale = 1.0 / jnp.clip(jnp.mean(jnp.abs(w)), 1e-05)
            wq = jnp.clip(jnp.round(w * scale), -1.0, 1.0) / scale
            return w + jax.lax.stop_gradient(wq - w)

        def _act_quant(x):
            scale = 127.0 / jnp.clip(jnp.max(jnp.abs(x), axis=-1, keepdims=True), 1e-05)
            xq = jnp.clip(jnp.round(x * scale), -128.0, 127.0) / scale
            return x + jax.lax.stop_gradient(xq - x)

        def _bitlinear(x, w):
            return jnp.einsum('bsi,oi->bso', _act_quant(x), _weight_quant(w))
        key = jax.random.key(seed)
        k0, k1, k2, k3 = jax.random.split(key, 4)
        x = jax.random.normal(k0, (4, 512, HIDDEN), dtype=jnp.float32)
        w_gate = jax.random.normal(k1, (INNER, HIDDEN), dtype=jnp.float32) / np.sqrt(HIDDEN)
        w_up = jax.random.normal(k2, (INNER, HIDDEN), dtype=jnp.float32) / np.sqrt(HIDDEN)
        w_down = jax.random.normal(k3, (HIDDEN, INNER), dtype=jnp.float32) / np.sqrt(INNER)
        return {'x': x, 'w_gate': w_gate, 'w_up': w_up, 'w_down': w_down}
    _L1_ffn_all = _L1_ffn_setup()
    _L1_ffn_in = {k: v for k, v in _L1_ffn_all.items() if k in ('w_gate', 'w_up', 'w_down')}
    del _L1_ffn_all
    return {'x': x, 'ctx_1024': ctx_1024, 'L0_xattn_Wg': _L0_xattn_in['Wg'], 'L0_xattn_bg': _L0_xattn_in['bg'], 'L0_xattn_Wo': _L0_xattn_in['Wo'], 'L0_xattn_bo': _L0_xattn_in['bo'], 'L0_ffn_W': _L0_ffn_in['W'], 'L0_ffn_b': _L0_ffn_in['b'], 'L0_ffn_logits': _L0_ffn_in['logits'], 'L0_ffn_u': _L0_ffn_in['u'], 'L1_xattn_Wq': _L1_xattn_in['Wq'], 'L1_xattn_Wk': _L1_xattn_in['Wk'], 'L1_xattn_Wv': _L1_xattn_in['Wv'], 'L1_xattn_Wo': _L1_xattn_in['Wo'], 'L1_ffn_w_gate': _L1_ffn_in['w_gate'], 'L1_ffn_w_up': _L1_ffn_in['w_up'], 'L1_ffn_w_down': _L1_ffn_in['w_down']}

def reference(x, ctx_1024, L0_xattn_Wg, L0_xattn_bg, L0_xattn_Wo, L0_xattn_bo, L0_ffn_W, L0_ffn_b, L0_ffn_logits, L0_ffn_u, L1_xattn_Wq, L1_xattn_Wk, L1_xattn_Wv, L1_xattn_Wo, L1_ffn_w_gate, L1_ffn_w_up, L1_ffn_w_down):
    import jax
    import jax.numpy as jnp

    def _L0_xattn_ref(inputs, context, Wg, bg, Wo, bo):
        import jax, jax.numpy as jnp
        import numpy as np
        B, TQ, TK, DIM = (4, 512, 512, 256)
        gate_signal = jnp.einsum('bkd,de->bke', context, Wg) + bg
        attn = jnp.einsum('bkd,bqd->bkq', gate_signal, inputs)
        attn = jax.nn.softmax(attn, axis=1)
        out = jnp.einsum('bkq,bkd->bqd', attn, context)
        return jnp.einsum('bqd,de->bqe', out, Wo) + bo

    def _L0_ffn_ref(x, W, b, logits, u):
        import jax, jax.numpy as jnp
        import numpy as np
        NUM_OPS, B, T, D = (8, 8, 128, 256)
        gumbel = -jnp.log(-jnp.log(u))
        idx = jnp.argmax(jax.nn.log_softmax(logits) + gumbel)
        out = jnp.einsum('btd,de->bte', x, W[idx]) + b[idx]
        return out

    def _L1_xattn_ref(x, c, Wq, Wk, Wv, Wo):
        import jax, jax.numpy as jnp
        import numpy as np
        NUM_HEADS = 16
        HEAD_SIZE = 64
        H, D = (NUM_HEADS, HEAD_SIZE)
        B, S = (x.shape[0], x.shape[1])
        N = c.shape[1]
        scale = D ** (-0.5)
        q = (x @ Wq).reshape(B, S, H, D).transpose(0, 2, 1, 3)
        k = (c @ Wk).reshape(B, N, D, H).transpose(0, 3, 2, 1)
        v = (c @ Wv).reshape(B, N, D, H).transpose(0, 3, 1, 2)
        mask = jnp.all(c == 0, axis=-1)[:, None, None, :]
        scores = jnp.einsum('bhsd,bhdn->bhsn', q, k) * scale
        scores = jnp.where(mask, -jnp.inf, scores)
        att = jax.nn.softmax(scores, axis=-1)
        out = jnp.einsum('bhsn,bhnd->bhsd', att, v)
        out = out.transpose(0, 2, 1, 3).reshape(B, S, H * D)
        return out @ Wo

    def _L1_ffn_ref(x, w_gate, w_up, w_down):
        import jax, jax.numpy as jnp
        import numpy as np
        HIDDEN = 256
        INNER = 1024

        def _weight_quant(w):
            scale = 1.0 / jnp.clip(jnp.mean(jnp.abs(w)), 1e-05)
            wq = jnp.clip(jnp.round(w * scale), -1.0, 1.0) / scale
            return w + jax.lax.stop_gradient(wq - w)

        def _act_quant(x):
            scale = 127.0 / jnp.clip(jnp.max(jnp.abs(x), axis=-1, keepdims=True), 1e-05)
            xq = jnp.clip(jnp.round(x * scale), -128.0, 127.0) / scale
            return x + jax.lax.stop_gradient(xq - x)

        def _bitlinear(x, w):
            return jnp.einsum('bsi,oi->bso', _act_quant(x), _weight_quant(w))
        gate = jax.nn.silu(_bitlinear(x, w_gate))
        up = _bitlinear(x, w_up)
        return _bitlinear(gate * up, w_down)
    x = x + _L0_xattn_ref(_layernorm(x, axis=-1), ctx_1024, L0_xattn_Wg, L0_xattn_bg, L0_xattn_Wo, L0_xattn_bo)
    x = x + _L0_ffn_ref(_layernorm(x, axis=-1), L0_ffn_W, L0_ffn_b, L0_ffn_logits, L0_ffn_u)
    x = x + _L1_xattn_ref(_layernorm(x, axis=-1), ctx_1024, L1_xattn_Wq, L1_xattn_Wk, L1_xattn_Wv, L1_xattn_Wo)
    x = x + _L1_ffn_ref(_layernorm(x, axis=-1), L1_ffn_w_gate, L1_ffn_w_up, L1_ffn_w_down)
    return x

_drawn_inputs = setup_inputs


def setup_inputs(seed=0):
    import zlib

    import numpy as np

    out = dict(_drawn_inputs(seed))
    spreads = {'L0_xattn_bg': (0.0, 0.1), 'L0_xattn_bo': (0.0, 0.1), 'L0_ffn_b': (0.0, 0.1)}
    factors = {}
    for name, (base, spread) in spreads.items():
        noise = np.random.default_rng([zlib.crc32(name.encode()), seed]).standard_normal(out[name].shape)
        drawn = base * np.exp(spread * noise) if base else spread * noise
        out[name] = jnp.asarray(drawn.astype(out[name].dtype))
    for name, factor in factors.items():
        out[name] = (out[name] * factor).astype(out[name].dtype)
    return out
```

```python
from contextlib import ExitStack

import concourse.bass as bass
from concourse import mybir

F32 = mybir.dt.float32
F32R = mybir.dt.float32r
BF16 = mybir.dt.bfloat16
U32 = mybir.dt.uint32
ALU = mybir.AluOpType
ACT = mybir.ActivationFunctionType
AX = mybir.AxisListType.X

P = 128
B, S, D = 4, 1024, 256
DC = D // P
NB = B * S // P
BPB = S // P
KEYS = 77
H, HD = 16, 64
HK = H * KEYS
NCH = -(-HK // P)
PAIRS = H // 2
BANK = 512
HEAD_GROUPS = ((0, 6), (6, 12), (12, 16))
T_GROUPS = ((0, 4), (4, 8), (8, 10))
OPS = 8
INNER = 1024
IC = INNER // P
EPS = 1e-5
MASKED = -3.0e38
MAGIC = 1.5 * 2.0 ** 23
QMAX = 127.0
CLIP = 1e-5
PADV = P - 1


def wait(eng, sem, count):
    if not (isinstance(count, int) and count <= 0):
        eng.wait_ge(sem, count)


def overlaps(j):
    return [p for p in range(PAIRS) if 2 * KEYS * p < P * (j + 1) and 2 * KEYS * (p + 1) > P * j]


def build(nc, x, cT_in, a_wg, a_bg, a_wo, a_bo, f_w, f_b, f_logits, f_u,
          b_wqT, b_wk, b_wv, b_wo, w_gateT, w_upT, w_downT, out):
    ctx = ExitStack()
    with ctx:
        def sem(name):
            return ctx.enter_context(nc.semaphore(name))

        def alloc(stack, name, shape, dt=F32):
            return stack.enter_context(nc.sbuf_tensor(name, shape, dt))

        xs = alloc(ctx, "xs", [P, NB, D])
        ident = alloc(ctx, "ident", [P, P])
        ident_b = alloc(ctx, "ident_b", [P, P], BF16)
        mhalf = alloc(ctx, "mhalf", [P, 1])
        ones_b = alloc(ctx, "ones_b", [P, P], BF16)
        ones = alloc(ctx, "ones", [P, P])
        stats = alloc(ctx, "stats", [P, 2, 6])
        meanvar = alloc(ctx, "meanvar", [P, 2, 2])
        var_eps = alloc(ctx, "var_eps", [P, 2, 1])
        rstd = alloc(ctx, "rstd", [P, 2, 1])
        xn = alloc(ctx, "xn", [P, 2, D])
        xT_hi = alloc(ctx, "xT_hi", [P, 2, DC, P], F32R)
        xT_lo = alloc(ctx, "xT_lo", [P, 2, DC, P], F32R)

        ab = ExitStack()
        vT = alloc(ab, "vT", [P, PAIRS, B, KEYS])
        wo1 = alloc(ab, "wo1", [P, PAIRS, D])
        m_hi = alloc(ab, "m_hi", [P, B, DC, HK], F32R)
        m_lo = alloc(ab, "m_lo", [P, B, DC, HK], F32R)
        mask_row = alloc(ab, "mask_row", [1, B, KEYS], BF16)

        pa = ExitStack()
        cT = alloc(pa, "cT", [P, DC, B * KEYS])
        nonzero = alloc(pa, "nonzero", [P, DC, B * KEYS], BF16)
        wg0 = alloc(pa, "wg0", [P, DC, D])
        wo0 = alloc(pa, "wo0", [P, DC, D])
        bg = alloc(pa, "bg", [P, DC])
        bo = alloc(pa, "bo", [KEYS, D])
        wv = alloc(pa, "wv", [P, DC, H * HD])
        wqT = alloc(pa, "wqT", [P, PAIRS, D])
        kT = alloc(pa, "kT", [P, PAIRS, B * KEYS])
        gate = alloc(pa, "gate", [P, DC, B * KEYS])
        gate_hi = alloc(pa, "gate_hi", [P, B, DC, KEYS + 1], F32R)
        gate_lo = alloc(pa, "gate_lo", [P, B, DC, KEYS + 1], F32R)
        cwo = alloc(pa, "cwo", [KEYS, D])
        cwo_hi = alloc(pa, "cwo_hi", [KEYS, B, D], F32R)
        cwo_lo = alloc(pa, "cwo_lo", [KEYS, B, D], F32R)
        logit = alloc(pa, "logit", [1, OPS])
        uni = alloc(pa, "uni", [1, OPS])
        pick = alloc(pa, "pick", [1, 8, OPS])
        picked = alloc(pa, "picked", [1, OPS], U32)
        wsel = alloc(pa, "wsel", [P, DC, D])
        wsel_hi = alloc(pa, "wsel_hi", [P, DC, D], F32R)
        wsel_lo = alloc(pa, "wsel_lo", [P, DC, D], F32R)
        bsel = alloc(pa, "bsel", [P, D])
        with ExitStack() as key_weights:
            wk = alloc(key_weights, "wk", [P, DC, H * HD])
        stats2 = alloc(pa, "stats2", [P, 2, 6])
        meanvar2 = alloc(pa, "meanvar2", [P, 2, 2])
        var_eps2 = alloc(pa, "var_eps2", [P, 2, 1])
        rstd2 = alloc(pa, "rstd2", [P, 2, 1])
        xn2 = alloc(pa, "xn2", [P, 2, D])
        x2T_hi = alloc(pa, "x2T_hi", [P, 2, DC, P], F32R)
        x2T_lo = alloc(pa, "x2T_lo", [P, 2, DC, P], F32R)
        nmax0 = alloc(pa, "nmax0", [P, 2, 1])
        den0 = alloc(pa, "den0", [P, 2, 1])
        rden0 = alloc(pa, "rden0", [P, 2, 1])
        e0 = alloc(pa, "e0", [P, 2, KEYS])
        e0T_hi = alloc(pa, "e0T_hi", [KEYS, 2, P], F32R)
        e0T_lo = alloc(pa, "e0T_lo", [KEYS, 2, P], F32R)
        pa.close()

        pb = ExitStack()
        pair_vT = alloc(pb, "pair_vT", [P, PAIRS, 2 * KEYS + 2 * PADV])
        vwo_hi = alloc(pb, "vwo_hi", [P, NCH, D], F32R)
        vwo_lo = alloc(pb, "vwo_lo", [P, NCH, D], F32R)
        e = alloc(pb, "e", [P, 2, NCH * P])
        nmax = alloc(pb, "nmax", [P, 2, H])
        den = alloc(pb, "den", [P, 2, H])
        rden = alloc(pb, "rden", [P, 2, H])
        pT_hi = alloc(pb, "pT_hi", [P, NCH, P], F32R)
        pT_lo = alloc(pb, "pT_lo", [P, NCH, P], F32R)
        pb.close()
        ab.close()

        raw = {n: alloc(ctx, f"raw_{n}", [P, 2 * INNER]) for n in ("g", "u", "d")}
        wq_b = {n: alloc(ctx, f"wq_{n}", [P, 2 * INNER], BF16) for n in ("g", "u", "d")}
        wtmp = alloc(ctx, "wtmp", [P, 2 * INNER])
        wtmp_b = alloc(ctx, "wtmp_b", [P, 2 * INNER], BF16)
        abs_sum = alloc(ctx, "abs_sum", [P, 4])
        w_mean = alloc(ctx, "w_mean", [P, 4])
        w_inv = alloc(ctx, "w_inv", [P, 4])
        up_127 = alloc(ctx, "up_127", [P, 1])
        q_f = alloc(ctx, "q_f", [P, 2, D])
        q_b = alloc(ctx, "q_b", [P, 2, D], BF16)
        qT = alloc(ctx, "qT", [P, 2, DC, P], BF16)
        amax = alloc(ctx, "amax", [P, 2, 1])
        c1 = alloc(ctx, "c1", [P, 2, 1])
        r1 = alloc(ctx, "r1", [P, 2, 1])
        s_gate = alloc(ctx, "s_gate", [P, 2, 1])
        s_up = alloc(ctx, "s_up", [P, 4, 1])
        s_up127 = alloc(ctx, "s_up127", [P, 4, 1])
        silu = alloc(ctx, "silu", [P, 2, INNER])
        h = alloc(ctx, "h", [P, 2, INNER])
        hmax = alloc(ctx, "hmax", [P, 2, 1])
        c2 = alloc(ctx, "c2", [P, 2, 1])
        r2 = alloc(ctx, "r2", [P, 2, 1])
        s_h = alloc(ctx, "s_h", [P, 2, 1])
        s_y = alloc(ctx, "s_y", [P, 4, 1])
        hq_f = alloc(ctx, "hq_f", [P, 2, INNER])
        hq_b = alloc(ctx, "hq_b", [P, 2, INNER], BF16)
        hqT = alloc(ctx, "hqT", [P, IC, P], BF16)
        y = alloc(ctx, "y", [P, 2, D])

        bank = [ctx.enter_context(nc.psum_tensor(f"bank{i}", [P, BANK], F32)) for i in range(8)]

        ld_c, ld_a, ld_pick, ld_k, ld_q, ld_v, ld_wo, ld_sel, ld_ffn = (
            sem(n) for n in ("ld_c", "ld_a", "ld_pick", "ld_k", "ld_q", "ld_v", "ld_wo", "ld_sel", "ld_ffn"))
        st_out = [sem("st_even"), sem("st_odd")]
        ld_x = [sem(f"ld_x{b}") for b in range(B)]
        consts, dve_seq, picked_ok, pick_ln, pick_z = (sem(n) for n in ("consts", "dve_seq", "picked_ok", "pick_ln", "pick_z"))
        nz_ok, cnt_ok, mask_ok, k_gate, cwo_ok = (sem(n) for n in ("nz_ok", "cnt_ok", "mask_ok", "k_gate", "cwo_ok"))
        prep_mm, prep_hi, prep_lo, sel_hi = (sem(n) for n in ("prep_mm", "prep_hi", "prep_lo", "sel_hi"))
        phase = sem("phase")
        a_stats, a_mv, a_eps, a_rstd, a_xn, a_T, a_Thi, a_Tlo, a_sc, a_nmax, a_exp, a_eT, a_eThi, a_eTlo, a_rden, a_pv = (
            sem("a_" + n) for n in ("stats", "mv", "eps", "rstd", "xn", "T", "Thi", "Tlo", "sc", "nmax", "exp", "eT",
                                    "eThi", "eTlo", "rden", "pv"))
        f_x1, f_stats, f_mv, f_eps, f_rstd, f_xn, f_bias, f_T, f_Thi, f_Tlo, f_mm, f_x2 = (
            sem("f_" + n) for n in ("x1", "stats", "mv", "eps", "rstd", "xn", "bias", "T", "Thi", "Tlo", "mm", "x2"))
        b_stats, b_mv, b_eps, b_rstd, b_xn, b_T, b_Thi, b_Tlo, b_rden, b_norm, b_pv, b_x3 = (
            sem("b_" + n) for n in ("stats", "mv", "eps", "rstd", "xn", "T", "Thi", "Tlo", "rden", "norm", "pv", "x3"))
        b_sc, b_nmax, b_exp = sem("b_sc"), sem("b_nmax"), sem("b_exp")
        b_pT, b_pThi, b_pTlo = sem("b_pT"), sem("b_pThi"), sem("b_pTlo")
        e_pad, v_zero, v_pair, vw_mm, vw_hi, vw_lo = (sem(n) for n in ("e_pad", "v_zero", "v_pair", "vw_mm", "vw_hi", "vw_lo"))
        w_abs, w_sum, w_seq, w_ready = (sem(n) for n in ("w_abs", "w_sum", "w_seq", "w_ready"))
        c_stats, c_mv, c_eps, c_rstd, c_xn, c_amax, c_c1, c_r1, c_scales, c_qf, c_qb, c_T, c_qT, c_gu, c_silu, c_h = (
            sem("c_" + n) for n in ("stats", "mv", "eps", "rstd", "xn", "amax", "c1", "r1", "scales", "qf", "qb", "T", "qT",
                                    "gu", "silu", "h"))
        c_hmax, c_c2, c_r2, c_sh, c_hqf, c_hqb, c_hT, c_hqT, c_dn, c_y = (
            sem("c_" + n) for n in ("hmax", "c2", "r2", "sh", "hqf", "hqb", "hT", "hqT", "dn", "y"))

        def pipeline(eng, step, depth, first=0, last=NB):
            start = first + depth + 2
            count = (last - start) // 2 * 2
            for t in range(first, start):
                step(t, t % 2, lambda k, t=t: first <= t - k < last)
            with eng.Fori(0, count // 2) as i:
                t = i * 2 + start
                step(t, start % 2, lambda k: True)
                step(t + 1, (start + 1) % 2, lambda k: True)
            for t in range(start + count, last + depth):
                step(t, t % 2, lambda k, t=t: first <= t - k < last)

        def stage_b(eng, step, at_batch, last_batch=True):
            def two_steps(t):
                step(t, 1, lambda k: True)
                step(t + 1, 0, lambda k: True)

            for t in range(3):
                step(t, t % 2, lambda k, t=t: t >= k)
            at_batch(0)
            two_steps(3)
            with eng.Fori(0, BPB // 2 - 1) as i:
                two_steps(i * 2 + 5)
            with eng.Fori(0, B - 2) as b:
                at_batch(b + 1)
                with eng.Fori(0, BPB // 2) as i:
                    two_steps(b * BPB + i * 2 + BPB + 3)
            if last_batch:
                at_batch(B - 1)
            t0 = (B - 1) * BPB + 3
            with eng.Fori(0, 2) as i:
                two_steps(i * 2 + t0)
            for t in range(t0 + 4, NB + 3):
                step(t, t % 2, lambda k, t=t: t - k < NB)

        def slot4(t, k):
            return slots4[(id4[0] - k) % 4]

        slots4, id4 = [0, 1, 2, 3], [0]

        def pipeline4(eng, step, depth, last=NB):
            start = -(-depth // 4) * 4
            for t in range(start):
                id4[0] = t % 4
                step(t, t % 2, lambda k, t=t: 0 <= t - k < last)
            with eng.Fori(0, (last - start) // 4) as n:
                t = n * 4 + start
                for i in range(4):
                    id4[0] = i
                    step(t + i, i % 2, lambda k: True)
            for t in range(last, last + depth):
                id4[0] = t % 4
                step(t, t % 2, lambda k, t=t: 0 <= t - k < last)

        def wait_apart(eng, *needs):
            counts = [(sem_, n if isinstance(n, int) else eng.compute_val(n)) for sem_, n in needs]
            eng.wait_ge(consts, 4)
            for sem_, n in counts:
                wait(eng, sem_, n)

        def batch_of(g):
            return g // BPB

        def block(tile, g):
            return tile[:, bass.ds(g, 1), :].rearrange("p o d -> p (o d)")

        N_GATE, N_CWO, N_K, N_V, N_M = DC, B, PAIRS, PAIRS, 2 * H
        FIRST_CWO = N_GATE
        FIRST_K = FIRST_CWO + N_CWO
        FIRST_M = FIRST_K + N_K
        FIRST_V = FIRST_M + N_M
        N_PREP = FIRST_V + N_V

        def low_parts(n):
            return min(n, FIRST_K) + min(max(n - FIRST_M, 0), N_M)

        PREP_BANKS = 7

        blk = ctx.enter_context(nc.Block())

        @blk.sync
        def _(sp):
            sp.dma_start(cT[:, :, :], cT_in.rearrange("(c p) n -> p c n", p=P)).then_inc(ld_c, 16)
            sp.dma_start(wg0[:, :, :], a_wg.rearrange("(c p) n -> p c n", p=P)).then_inc(ld_a, 16)
            with nc.allow_non_contiguous_dma(reason="256 biases, once"):
                sp.dma_start(bg[:, :], a_bg.rearrange("(c p) -> p c", p=P)).then_inc(ld_a, 16)
            sp.dma_start(wo0[:, :, :], a_wo.rearrange("(c p) n -> p c n", p=P)).then_inc(ld_a, 16)
            sp.dma_start(bo[:, :], a_bo.rearrange("(o n) -> o n", o=1).broadcast_to([KEYS, D])).then_inc(ld_a, 16)
            sp.dma_start(logit[:, :], f_logits.rearrange("(o n) -> o n", o=1)).then_inc(ld_pick, 16)
            sp.dma_start(uni[:, :], f_u.rearrange("(o n) -> o n", o=1)).then_inc(ld_pick, 16)
            sp.dma_start(wk[:, :, :], b_wk.rearrange("(c p) n -> p c n", p=P)).then_inc(ld_k, 16)
            sp.dma_start(wqT[:, :, :], b_wqT.rearrange("(c p) n -> p c n", p=P)).then_inc(ld_q, 16)
            xb = x.rearrange("b (g p) d -> b p g d", p=P)
            sp.dma_start(xs[:, 0:BPB, :], xb[0]).then_inc(ld_x[0], 16)
            sp.dma_start(wv[:, :, :], b_wv.rearrange("(c p) n -> p c n", p=P)).then_inc(ld_v, 16)
            sp.dma_start(wo1[:, :, :], b_wo.rearrange("(c p) n -> p c n", p=P)).then_inc(ld_wo, 16)
            for b in range(1, B):
                sp.dma_start(xs[:, b * BPB:(b + 1) * BPB, :], xb[b]).then_inc(ld_x[b], 16)
            sp.wait_ge(picked_ok, 1)
            op = sp.value_load(picked[0:1, 0:1], min_val=0, max_val=OPS - 1)
            sp.dma_start(wsel[:, :, :], f_w[bass.ds(op, 1), :, :].rearrange("o (c p) n -> p (o c) n", p=P)).then_inc(ld_sel, 16)
            sp.dma_start(bsel[:, :], f_b[bass.ds(op, 1), :].broadcast_to([P, D])).then_inc(ld_sel, 16)
            sp.wait_ge(phase, 8)
            for n, src in (("g", w_gateT), ("u", w_upT), ("d", w_downT)):
                sp.dma_start(raw[n][:, :].rearrange("p (c n) -> p c n", n=src.shape[1]),
                             src.rearrange("(c p) n -> p c n", p=P)).then_inc(ld_ffn, 16)
            outb = out.rearrange("b (g p) d -> (b g) p d", p=P)
            with sp.Fori(0, NB // 2) as i:
                for q in range(2):
                    sp.wait_ge(c_y, i * 2 + q + 1)
                    sp.dma_start(outb[bass.ds(i * 2 + q, 1), :, :].rearrange("o p d -> (o p) d"), y[:, q, :]).then_inc(st_out[q], 16)
            for q in range(2):
                sp.wait_ge(st_out[q], 16 * (NB // 2))

        @blk.gpsimd
        def _(pool):
            gp = nc.gpsimd
            gp.memset(ident[:, :], 0.0).then_inc(consts, 1)
            gp.memset(mhalf[:, :], -0.5).then_inc(consts, 1)
            gp.memset(ones[:, :], 1.0).then_inc(consts, 1)
            gp.memset(ones_b[:, :], 1.0).then_inc(consts, 1)
            pool.wait_ge(consts, 4)
            gp.affine_select(out=ident[:, :], in_=ident[:, :], compare_op=ALU.not_equal, fill=1.0, base=0,
                             pattern=[[-1, P]], channel_multiplier=1).then_inc(consts, 1)
            pool.wait_ge(consts, 5)
            gp.tensor_copy(ident_b[:, :], ident[:, :]).then_inc(consts, 1)

            def inverse_root(ready, mv, ve, rs, eps_done, done, g, par):
                wait_apart(pool, (ready, g + 1))
                gp.tensor_scalar(ve[:, par, :], mv[:, par, 1:2], EPS, 1.0, ALU.add, ALU.mult).then_inc(eps_done, 1)
                pool.wait_ge(eps_done, g + 1)
                gp.tensor_tensor(rs[:, par, :], ve[:, par, :], mhalf[:, :], ALU.pow).then_inc(done, 1)

            def step_a(t, par, live):
                if live(6):
                    g = t - 6
                    pool.wait_ge(f_xn, g + 1)
                    if isinstance(g, int) and g == 0:
                        pool.wait_ge(ld_sel, 32)
                    gp.tensor_tensor(block(xs, g), block(xs, g), bsel[:, :], ALU.add).then_inc(f_bias, 1)
                if live(5):
                    inverse_root(f_mv, meanvar2, var_eps2, rstd2, f_eps, f_rstd, t - 5, (par + 1) % 2)
                if live(0):
                    inverse_root(a_mv, meanvar, var_eps, rstd, a_eps, a_rstd, t, par)

            pipeline(pool, step_a, 8)
            pool.drain().then_inc(phase, 1)

            pool.wait_ge(phase, 4)
            gp.memset(pair_vT[:, :, :], 0.0).then_inc(v_zero, 1)
            gp.memset(e[:, :, HK:NCH * P], 0.0).then_inc(e_pad, 1)
            pool.wait_ge(v_zero, 1)
            pool.wait_ge(e_pad, 1)

            def pair_values(b):
                for half in range(2):
                    rows = slice(half * HD, (half + 1) * HD)
                    at = PADV + half * KEYS
                    gp.tensor_copy(pair_vT[rows, :, at:at + KEYS],
                                   vT[rows, :, bass.ds(b, 1), :].rearrange("p c o k -> p c (o k)")).then_inc(v_pair, 1)
                    wait_apart(pool, (v_pair, 2 * b + half + 1))

            def step_b(t, par, live):
                if live(3):
                    g, gp_ = t - 3, (par + 1) % 2
                    pool.wait_ge(b_rden, g + 1)
                    eh = e[:, gp_, 0:HK].rearrange("p (h k) -> p h k", k=KEYS)
                    gp.tensor_tensor(eh, eh, rden[:, gp_, :].rearrange("p (h o) -> p h o", o=1).broadcast_to([P, H, KEYS]),
                                     ALU.mult).then_inc(b_norm, 1)
                if live(0):
                    inverse_root(b_mv, meanvar, var_eps, rstd, b_eps, b_rstd, t, par)

            pair_values(0)
            stage_b(pool, step_b, lambda b: (pool.wait_ge(vw_mm, NCH * (b + 1)), pair_values(b + 1)), last_batch=False)
            pool.drain().then_inc(phase, 1)

            def step_c(t, par, live):
                if live(3):
                    g, gp_ = t - 3, (par + 1) % 2
                    wait_apart(pool, (c_r2, g + 1))
                    q = slot4(t, 3)
                    gp.tensor_scalar(s_h[:, gp_, :], r2[:, gp_, :], s_up[:, q, :], 1.0, ALU.mult, ALU.mult).then_inc(c_sh, 1)
                    wait_apart(pool, (c_sh, g + 1), (c_hqb, g - 1))
                    gp.tensor_scalar(hq_f[:, gp_, :], h[:, gp_, :], s_h[:, gp_, :], MAGIC, ALU.mult, ALU.add).then_inc(c_hqf, 1)
                if live(0):
                    inverse_root(c_mv, meanvar, var_eps, rstd, c_eps, c_rstd, t, par)

            pipeline4(pool, step_c, 5)

        @blk.tensor
        def _(pe):
            mm = nc.tensor.matmul

            def split_mm(o, a_hi, a_lo, c_hi, c_lo, start, stop):
                mm(o, a_hi, c_hi, start=start, stop=False)
                mm(o, a_hi, c_lo, start=False, stop=False)
                return mm(o, a_lo, c_hi, start=False, stop=stop)

            pe.wait_ge(nz_ok, 1)
            pe.wait_ge(consts, 4)
            for c in range(DC):
                last = mm(bank[7][0:1, 0:B * KEYS], ones_b[:, 0:1], nonzero[:, c, :], start=c == 0, stop=c == DC - 1)
            last.then_inc(cnt_ok, 1)

            n = 0

            def free_bank():
                if n >= PREP_BANKS:
                    pe.wait_ge(prep_hi, n - PREP_BANKS + 1)
                    pe.wait_ge(prep_lo, low_parts(n - PREP_BANKS + 1))
                return bank[n % PREP_BANKS]

            pe.wait_ge(ld_c, 16)
            pe.wait_ge(ld_a, 64)
            for eo in range(DC):
                o = free_bank()[:, 0:B * KEYS]
                for c in range(DC):
                    last = mm(o, wg0[:, c, eo * P:(eo + 1) * P], cT[:, c, :], start=c == 0, stop=c == DC - 1)
                last.then_inc(prep_mm, 1)
                n += 1
            for b in range(B):
                o = free_bank()[0:KEYS, 0:D]
                for c in range(DC):
                    last = mm(o, cT[:, c, b * KEYS:(b + 1) * KEYS], wo0[:, c, :], start=c == 0, stop=c == DC - 1)
                last.then_inc(prep_mm, 1)
                n += 1

            def project_context(w):
                nonlocal n
                for p in range(PAIRS):
                    o = free_bank()[:, 0:B * KEYS]
                    for c in range(DC):
                        last = mm(o, w[:, c, p * P:(p + 1) * P], cT[:, c, :], start=c == 0, stop=c == DC - 1)
                    last.then_inc(prep_mm, 1)
                    n += 1

            pe.wait_ge(ld_k, 16)
            project_context(wk)
            pe.wait_ge(ld_q, 16)
            for hh in range(H):
                rows = slice(HD * (hh % 2), HD * (hh % 2) + HD)
                pe.wait_ge(prep_hi, FIRST_K + hh // 2 + 1)
                for io in range(DC):
                    mm(free_bank()[:, 0:B * KEYS], wqT[rows, hh // 2, io * P:(io + 1) * P], kT[rows, hh // 2, :],
                       start=True, stop=True).then_inc(prep_mm, 1)
                    n += 1
            pe.wait_ge(ld_v, 16)
            project_context(wv)

            pe.wait_ge(prep_hi, N_PREP)
            pe.wait_ge(prep_lo, low_parts(N_PREP))
            pe.wait_ge(consts, 6)
            T1, SC, ET, PV, T2, FF = bank[0], bank[1], bank[2], bank[3], bank[4], bank[5]

            def step_a(t, par, live):
                if live(7):
                    g, q = t - 7, (par + 1) % 2
                    pe.wait_ge(f_Tlo, g + 1)
                    wait(pe, f_x2, g)
                    if isinstance(g, int) and g == 0:
                        pe.wait_ge(sel_hi, 2)
                    for c in range(DC):
                        last = split_mm(FF[:, 0:D], x2T_hi[:, q, c, :], x2T_lo[:, q, c, :], wsel_hi[:, c, :],
                                        wsel_lo[:, c, :], c == 0, c == DC - 1)
                    last.then_inc(f_mm, 1)
                if live(6):
                    g, q = t - 6, par
                    pe.wait_ge(f_xn, g + 1)
                    wait(pe, f_Tlo, g)
                    for c in range(DC):
                        last = nc.tensor.transpose(T2[:, c * P:(c + 1) * P], xn2[:, q, c * P:(c + 1) * P], ident[:, :])
                    last.then_inc(f_T, 1)
                if live(4):
                    g, q = t - 4, par
                    pe.wait_ge(a_eTlo, g + 1)
                    wait(pe, f_x1, g)
                    b = batch_of(g)
                    split_mm(PV[:, 0:D], e0T_hi[:, q, :], e0T_lo[:, q, :],
                             cwo_hi[:, bass.ds(b, 1), :].rearrange("p o d -> p (o d)"),
                             cwo_lo[:, bass.ds(b, 1), :].rearrange("p o d -> p (o d)"), True, True).then_inc(a_pv, 1)
                if live(3):
                    g, q = t - 3, (par + 1) % 2
                    pe.wait_ge(a_exp, g + 1)
                    wait(pe, a_eTlo, g)
                    nc.tensor.transpose(ET[0:KEYS, 0:P], e0[:, q, :], ident[:, :]).then_inc(a_eT, 1)
                if live(2):
                    g, q = t - 2, par
                    pe.wait_ge(a_Tlo, g + 1)
                    wait(pe, a_exp, g)
                    b = batch_of(g)
                    for c in range(DC):
                        last = split_mm(SC[:, 0:KEYS + 1], xT_hi[:, q, c, :], xT_lo[:, q, c, :],
                                        gate_hi[:, bass.ds(b, 1), c, :].rearrange("p o d -> p (o d)"),
                                        gate_lo[:, bass.ds(b, 1), c, :].rearrange("p o d -> p (o d)"), c == 0, c == DC - 1)
                    last.then_inc(a_sc, 1)
                if live(1):
                    g, q = t - 1, (par + 1) % 2
                    pe.wait_ge(a_xn, g + 1)
                    wait(pe, a_Tlo, g)
                    for c in range(DC):
                        last = nc.tensor.transpose(T1[:, c * P:(c + 1) * P], xn[:, q, c * P:(c + 1) * P], ident[:, :])
                    last.then_inc(a_T, 1)

            pipeline(pe, step_a, 8)
            pe.drain().then_inc(phase, 1)

            pe.wait_ge(phase, 4)
            XT, SCB, PT, OB = bank[0], bank[1:4], bank[4:7], bank[7]

            def value_out(b):
                pe.wait_ge(v_pair, 2 * b + 2)
                for j in range(NCH):
                    if j < 3:
                        wait(pe, b_pTlo, 3 * BPB * b)
                        wait(pe, b_pThi, 3 * BPB * b)
                    else:
                        pe.wait_ge(vw_hi, NCH * b + j - 2)
                        pe.wait_ge(vw_lo, NCH * b + j - 2)
                    ps = overlaps(j)
                    for p in ps:
                        at = P * j - 2 * KEYS * p + PADV
                        last = mm(PT[j % 3][:, 0:D], pair_vT[:, p, at:at + P], wo1[:, p, :],
                                  start=p == ps[0], stop=p == ps[-1])
                    last.then_inc(vw_mm, 1)
                wait_apart(pe, (vw_hi, NCH * (b + 1)), (vw_lo, NCH * (b + 1)))

            def step_b(t, par, live):
                if live(2):
                    g, q = t - 2, par
                    b = batch_of(g)
                    pe.wait_ge(b_Tlo, g + 1)
                    for i, (h0, h1) in enumerate(HEAD_GROUPS):
                        w = (h1 - h0) * KEYS
                        wait_apart(pe, (b_exp, 3 * g - 2 + i))
                        mrow = mask_row[0:1, bass.ds(b, 1), :].broadcast_to([1, h1 - h0, KEYS])
                        mm(SCB[i][:, 0:w], ones_b[0:1, :], mrow, start=True, stop=False)
                        for c in range(DC):
                            ms = [m[:, bass.ds(b, 1), c, h0 * KEYS:h1 * KEYS].rearrange("p o d -> p (o d)") for m in (m_hi, m_lo)]
                            last = split_mm(SCB[i][:, 0:w], xT_hi[:, q, c, :], xT_lo[:, q, c, :], ms[0], ms[1],
                                            False, c == DC - 1)
                        last.then_inc(b_sc, 1)
                if live(1):
                    g, q = t - 1, (par + 1) % 2
                    pe.wait_ge(b_xn, g + 1)
                    wait(pe, b_Tlo, g)
                    for c in range(DC):
                        last = nc.tensor.transpose(XT[:, c * P:(c + 1) * P], xn[:, q, c * P:(c + 1) * P], ident[:, :])
                    last.then_inc(b_T, 1)
                if live(3):
                    g, q = t - 3, (par + 1) % 2
                    pe.wait_ge(b_norm, g + 1)
                    if isinstance(g, int) and g == 0:
                        pe.wait_ge(e_pad, 1)
                    wait(pe, b_pTlo, 3 * g)
                    for i, (j0, j1) in enumerate(T_GROUPS):
                        for j in range(j0, j1):
                            last = nc.tensor.transpose(PT[i][:, (j - j0) * P:(j - j0 + 1) * P],
                                                       e[:, q, j * P:(j + 1) * P], ident[:, :])
                        last.then_inc(b_pT, 1)
                    wait(pe, b_x3, g)
                    for i, (j0, j1) in enumerate(T_GROUPS):
                        pe.wait_ge(b_pTlo, 3 * g + 1 + i)
                        for j in range(j0, j1):
                            last = split_mm(OB[:, 0:D], pT_hi[:, j, :], pT_lo[:, j, :], vwo_hi[:, j, :], vwo_lo[:, j, :],
                                            j == 0, j == NCH - 1)
                    last.then_inc(b_pv, 1)

            stage_b(pe, step_b, value_out)
            pe.drain().then_inc(phase, 1)

            pe.wait_ge(phase, 8)
            pe.wait_ge(w_abs, 1)
            mm(bank[0][:, 0:4], ones[:, :], abs_sum[:, :], start=True, stop=True).then_inc(w_sum, 1)
            XQ, GU, HT, YB = bank[0], bank[1:5], bank[5], bank[6]
            pe.wait_ge(w_ready, 1)
            wg = wq_b["g"][:, :].rearrange("p (c n) -> p c n", c=DC)
            wu = wq_b["u"][:, :].rearrange("p (c n) -> p c n", c=DC)
            wd = wq_b["d"][:, :].rearrange("p (c n) -> p c n", c=IC)

            def step_c(t, par, live):
                if live(4):
                    g, q = t - 4, par
                    pe.wait_ge(c_hqb, g + 1)
                    wait(pe, c_hqT, g)
                    for j in range(IC):
                        last = nc.tensor.transpose(HT[:, :].bitcast(BF16)[:, j * P:(j + 1) * P],
                                                   hq_b[:, q, j * P:(j + 1) * P], ident_b[:, :])
                    last.then_inc(c_hT, 1)
                if live(2):
                    g, q = t - 2, par
                    pe.wait_ge(c_qT, g + 1)
                    for i in range(4):
                        w, half = (wg, wu)[i % 2], i // 2
                        wait(pe, c_h, 2 * (g - 1) + half + 1)
                        for c in range(DC):
                            last = mm(GU[i][:, :], qT[:, q, c, :], w[:, c, half * BANK:(half + 1) * BANK],
                                      start=c == 0, stop=c == DC - 1)
                        last.then_inc(c_gu, 1)
                if live(1):
                    g, q = t - 1, (par + 1) % 2
                    pe.wait_ge(c_qb, g + 1)
                    wait(pe, c_qT, g)
                    for c in range(DC):
                        last = nc.tensor.transpose(XQ[:, :].bitcast(BF16)[:, c * P:(c + 1) * P],
                                                   q_b[:, q, c * P:(c + 1) * P], ident_b[:, :])
                    last.then_inc(c_T, 1)
                if live(4):
                    g = t - 4
                    pe.wait_ge(c_hqT, g + 1)
                    wait(pe, c_y, g)
                    for j in range(IC):
                        last = mm(YB[:, 0:D], hqT[:, j, :], wd[:, j, :], start=j == 0, stop=j == IC - 1)
                    last.then_inc(c_dn, 1)

            pipeline4(pe, step_c, 5)

        @blk.scalar
        def _(act):
            sc = nc.scalar
            act.wait_ge(ld_pick, 32)
            sc.activation(pick[:, 0, :], uni[:, :], ACT.Ln).then_inc(pick_ln, 1)
            act.wait_ge(pick_ln, 1)
            sc.activation(pick[:, 1, :], pick[:, 0, :], ACT.Ln, scale=-1.0).then_inc(pick_ln, 1)
            act.wait_ge(pick_z, 1)
            sc.activation(pick[:, 3, :], pick[:, 2, :], ACT.Exp, accum_out=pick[:, 4, 0:1]).then_inc(pick_ln, 1)
            act.wait_ge(pick_ln, 3)
            sc.activation(pick[:, 4, 1:2], pick[:, 4, 0:1], ACT.Ln).then_inc(pick_ln, 1)

            def hi_part(n, o, src, **kw):
                act.wait_ge(prep_mm, n + 1)
                return sc.activation(o, src, ACT.Copy, **kw)

            n = 0
            act.wait_ge(ld_a, 64)
            for eo in range(DC):
                act.wait_ge(prep_mm, n + 1)
                sc.activation(gate[:, eo, :], bank[n % PREP_BANKS][:, 0:B * KEYS], ACT.Identity,
                              bias=bg[:, eo:eo + 1]).then_inc(prep_hi, 1)
                n += 1
            for eo in range(DC):
                act.wait_ge(prep_hi, eo + 1)
                sc.activation(gate_hi[:, :, eo, 0:KEYS], gate[:, eo, :].rearrange("p (b k) -> p b k", b=B),
                              ACT.Copy).then_inc(k_gate, 1)
            for b in range(B):
                act.wait_ge(cwo_ok, b + 1)
                sc.activation(cwo_hi[:, b, :], cwo[:, :], ACT.Copy).then_inc(prep_hi, 1)
                n += 1
            for p in range(PAIRS):
                hi_part(n, kT[:, p, :], bank[n % PREP_BANKS][:, 0:B * KEYS]).then_inc(prep_hi, 1)
                n += 1
            for hh in range(H):
                for io in range(DC):
                    hi_part(n, m_hi[:, :, io, hh * KEYS:(hh + 1) * KEYS],
                            bank[n % PREP_BANKS][:, 0:B * KEYS].rearrange("p (b k) -> p b k", b=B),
                            scale=HD ** -0.5).then_inc(prep_hi, 1)
                    n += 1
            for p in range(PAIRS):
                hi_part(n, vT[:, p, :, :].rearrange("p b k -> p (b k)"), bank[n % PREP_BANKS][:, 0:B * KEYS]).then_inc(prep_hi, 1)
                n += 1
            act.wait_ge(ld_sel, 32)
            sc.activation(wsel_hi[:, :, :], wsel[:, :, :], ACT.Copy).then_inc(sel_hi, 1)

            def take_hi(T_sem, bank_, dst, done, free, g, q, w):
                act.wait_ge(T_sem, g + 1)
                if free is not None:
                    wait(act, free, g - 1)
                sc.activation(dst[:, q, :, :].rearrange("p c n -> p (c n)"), bank_[:, 0:w], ACT.Copy).then_inc(done, 1)

            def step_a(t, par, live):
                if live(6):
                    take_hi(f_T, bank[4], x2T_hi, f_Thi, f_mm, t - 6, par, D)
                if live(3):
                    g, q = t - 3, (par + 1) % 2
                    act.wait_ge(a_nmax, g + 1)
                    wait(act, a_eT, g - 1)
                    wait(act, a_rden, g - 1)
                    sc.activation(e0[:, q, :], bank[1][:, 0:KEYS], ACT.Exp, bias=nmax0[:, q, :],
                                  accum_out=den0[:, q, :]).then_inc(a_exp, 1)
                    act.wait_ge(a_eT, g + 1)
                    wait(act, a_pv, g - 1)
                    sc.activation(e0T_hi[:, q, :], bank[2][0:KEYS, 0:P], ACT.Copy).then_inc(a_eThi, 1)
                if live(1):
                    take_hi(a_T, bank[0], xT_hi, a_Thi, a_sc, t - 1, (par + 1) % 2, D)

            pipeline(act, step_a, 8)
            act.drain().then_inc(phase, 1)
            act.wait_ge(phase, 4)

            def value_hi(b):
                for j in range(NCH):
                    act.wait_ge(vw_mm, NCH * b + j + 1)
                    if j == 0:
                        wait(act, b_pv, BPB * b)
                    sc.activation(vwo_hi[:, j, :], bank[4 + j % 3][:, 0:D], ACT.Copy).then_inc(vw_hi, 1)

            def exp_group(g, q, i):
                h0, h1 = HEAD_GROUPS[i]
                act.wait_ge(b_nmax, 3 * g + i + 1)
                for hh in range(h0, h1):
                    last = sc.activation(e[:, q, hh * KEYS:(hh + 1) * KEYS], bank[1 + i][:, (hh - h0) * KEYS:(hh - h0 + 1) * KEYS],
                                         ACT.Exp, bias=nmax[:, q, hh:hh + 1], accum_out=den[:, q, hh:hh + 1])
                last.then_inc(b_exp, 1)

            def step_b(t, par, live):
                if live(2):
                    g, q = t - 2, par
                    wait(act, b_pT, 3 * (g - 1))
                    exp_group(g, q, 0)
                if live(1):
                    wait(act, b_sc, 3 * (t - 2))
                    take_hi(b_T, bank[0], xT_hi, b_Thi, None, t - 1, (par + 1) % 2, D)
                if live(3):
                    g = t - 3
                    wait(act, b_pv, g)
                    for i, (j0, j1) in enumerate(T_GROUPS):
                        act.wait_ge(b_pT, 3 * g + i + 1)
                        sc.activation(pT_hi[:, j0:j1, :].rearrange("p c n -> p (c n)"), bank[4 + i][:, 0:(j1 - j0) * P],
                                      ACT.Copy).then_inc(b_pThi, 1)
                if live(2):
                    exp_group(t - 2, par, 1)
                    exp_group(t - 2, par, 2)

            stage_b(act, step_b, value_hi)
            act.drain().then_inc(phase, 1)
            act.wait_ge(phase, 8)

            def step_c(t, par, live):
                if live(4):
                    g = t - 4
                    act.wait_ge(c_hT, g + 1)
                    wait(act, c_dn, g)
                    sc.activation(hqT[:, :, :].rearrange("p c n -> p (c n)"), bank[5][:, :].bitcast(BF16), ACT.Copy).then_inc(c_hqT, 1)
                if live(2):
                    g, q = t - 2, par
                    act.wait_ge(c_scales, g + 1)
                    wait(act, c_h, 2 * (g - 1))
                    for half in range(2):
                        act.wait_ge(c_gu, 4 * g + 2 * half + 1)
                        sc.activation(silu[:, q, half * BANK:(half + 1) * BANK], bank[1 + 2 * half][:, :], ACT.Silu,
                                      scale=s_gate[:, q, :]).then_inc(c_silu, 1)
                if live(3):
                    g, q = t - 3, (par + 1) % 2
                    act.wait_ge(c_hqf, g + 1)
                    wait(act, c_hT, g - 1)
                    sc.activation(hq_b[:, q, :], hq_f[:, q, :], ACT.Copy, bias=-MAGIC).then_inc(c_hqb, 1)
                if live(1):
                    g, q = t - 1, (par + 1) % 2
                    act.wait_ge(c_T, g + 1)
                    wait(act, c_gu, 4 * (g - 1))
                    sc.activation(qT[:, q, :, :].rearrange("p c n -> p (c n)"), bank[0][:, :].bitcast(BF16)[:, 0:D],
                                  ACT.Copy).then_inc(c_qT, 1)

            pipeline4(act, step_c, 5)

        @blk.vector
        def _(dve):
            v = nc.vector
            seq = [0]

            def chain(ins):
                seq[0] += 1
                ins.then_inc(dve_seq, 1)
                dve.wait_ge(dve_seq, seq[0])

            dve.wait_ge(ld_c, 16)
            v.tensor_scalar(nonzero[:, :, :], cT[:, :, :], 0.0, None, ALU.not_equal).then_inc(nz_ok, 1)
            v.memset(gate_hi[:, :, :, KEYS:KEYS + 1].bitcast(F32), 0.0)
            v.memset(gate_lo[:, :, :, KEYS:KEYS + 1].bitcast(F32), 0.0)
            dve.wait_ge(ld_pick, 32)
            chain(v.tensor_reduce(pick[:, 5, 0:1], logit[:, :], axis=AX, op=ALU.max))
            v.tensor_scalar(pick[:, 2, :], logit[:, :], pick[:, 5, 0:1], None, ALU.subtract).then_inc(pick_z, 1)
            dve.wait_ge(pick_ln, 4)
            chain(v.tensor_scalar(pick[:, 6, :], pick[:, 2, :], pick[:, 4, 1:2], None, ALU.subtract))
            chain(v.tensor_tensor(pick[:, 6, :], pick[:, 6, :], pick[:, 1, :], ALU.subtract))
            chain(v.max(pick[:, 7, :], pick[:, 6, :]))
            v.max_index(picked[:, :], pick[:, 7, :], pick[:, 6, :]).then_inc(picked_ok, 1)
            dve.wait_ge(cnt_ok, 1)
            v.tensor_scalar(mask_row[:, :, :].rearrange("p b k -> p (b k)"), bank[7][0:1, 0:B * KEYS], 0.0, MASKED,
                            ALU.is_equal, ALU.mult).then_inc(mask_ok, 1)

            n = 0
            for eo in range(DC):
                dve.wait_ge(k_gate, eo + 1)
                v.tensor_tensor(gate_lo[:, :, eo, 0:KEYS], gate[:, eo, :].rearrange("p (b k) -> p b k", b=B),
                                gate_hi[:, :, eo, 0:KEYS].bitcast(F32), ALU.subtract).then_inc(prep_lo, 1)
                n += 1
            dve.wait_ge(ld_a, 64)
            for b in range(B):
                dve.wait_ge(prep_mm, n + 1)
                v.tensor_tensor(cwo[:, :], bank[n % PREP_BANKS][0:KEYS, 0:D], bo[:, :], ALU.add).then_inc(cwo_ok, 1)
                dve.wait_ge(cwo_ok, b + 1)
                dve.wait_ge(prep_hi, n + 1)
                v.tensor_tensor(cwo_lo[:, b, :], cwo[:, :], cwo_hi[:, b, :].bitcast(F32), ALU.subtract).then_inc(prep_lo, 1)
                dve.wait_ge(prep_lo, n + 1)
                n += 1
            n += PAIRS
            for hh in range(H):
                for io in range(DC):
                    dve.wait_ge(prep_hi, n + 1)
                    v.scalar_tensor_tensor(out=m_lo[:, :, io, hh * KEYS:(hh + 1) * KEYS],
                                           in0=bank[n % PREP_BANKS][:, 0:B * KEYS].rearrange("p (b k) -> p b k", b=B),
                                           scalar=HD ** -0.5, in1=m_hi[:, :, io, hh * KEYS:(hh + 1) * KEYS].bitcast(F32),
                                           op0=ALU.mult, op1=ALU.subtract).then_inc(prep_lo, 1)
                    n += 1
            dve.wait_ge(sel_hi, 1)
            v.tensor_tensor(wsel_lo[:, :, :], wsel[:, :, :], wsel_hi[:, :, :].bitcast(F32), ALU.subtract).then_inc(sel_hi, 1)

            def moments(src, st, mv, st_sem, mv_sem, rstd_sem, g, q):
                v.bn_stats(st[:, q, :], src).then_inc(st_sem, 1)
                wait_apart(dve, (st_sem, g + 1), (rstd_sem, g - 1))
                v.bn_aggr(mv[:, q, :], st[:, q, :]).then_inc(mv_sem, 1)

            def normed(dst, src, mv, rs, rstd_sem, T_sem, done, g, q):
                dve.wait_ge(rstd_sem, g + 1)
                wait(dve, T_sem, g - 1)
                return v.tensor_scalar(dst[:, q, :], src, mv[:, q, 0:1], rs[:, q, :], ALU.subtract, ALU.mult).then_inc(done, 1)

            def take_lo(hi_sem, bank_, hi, lo, done, g, q):
                dve.wait_ge(hi_sem, g + 1)
                v.tensor_tensor(lo[:, q, :, :].rearrange("p c n -> p (c n)"), bank_[:, 0:D],
                                hi[:, q, :, :].rearrange("p c n -> p (c n)").bitcast(F32), ALU.subtract).then_inc(done, 1)

            def step_a(t, par, live):
                if live(8):
                    g = t - 8
                    dve.wait_ge(f_mm, g + 1)
                    dve.wait_ge(f_bias, g + 1)
                    v.tensor_tensor(block(xs, g), bank[5][:, 0:D], block(xs, g), ALU.add).then_inc(f_x2, 1)
                if live(7):
                    g, q = t - 7, (par + 1) % 2
                    wait(dve, f_mm, g - 1)
                    take_lo(f_Thi, bank[4], x2T_hi, x2T_lo, f_Tlo, g, q)
                if live(6):
                    g = t - 6
                    normed(xn2, block(xs, g), meanvar2, rstd2, f_rstd, f_T, f_xn, g, par)
                if live(5):
                    g, q = t - 5, (par + 1) % 2
                    dve.wait_ge(a_pv, g + 1)
                    dve.wait_ge(a_rden, g + 1)
                    v.scalar_tensor_tensor(out=block(xs, g), in0=bank[3][:, 0:D], scalar=rden0[:, q, :], in1=block(xs, g),
                                           op0=ALU.mult, op1=ALU.add).then_inc(f_x1, 1)
                    wait_apart(dve, (f_x1, g + 1))
                    moments(block(xs, g), stats2, meanvar2, f_stats, f_mv, f_rstd, g, q)
                if live(4):
                    g, q = t - 4, par
                    dve.wait_ge(a_eThi, g + 1)
                    wait(dve, a_pv, g - 1)
                    v.tensor_tensor(e0T_lo[:, q, :], bank[2][0:KEYS, 0:P], e0T_hi[:, q, :].bitcast(F32),
                                    ALU.subtract).then_inc(a_eTlo, 1)
                    dve.wait_ge(a_exp, g + 1)
                    wait(dve, f_x1, g - 1)
                    v.reciprocal(rden0[:, q, :], den0[:, q, :]).then_inc(a_rden, 1)
                if live(3):
                    g, q = t - 3, (par + 1) % 2
                    dve.wait_ge(a_sc, g + 1)
                    wait(dve, a_exp, g - 1)
                    v.tensor_reduce(nmax0[:, q, :], bank[1][:, 0:KEYS], axis=AX, op=ALU.max, negate=True).then_inc(a_nmax, 1)
                if live(2):
                    g, q = t - 2, par
                    wait(dve, a_sc, g - 1)
                    take_lo(a_Thi, bank[0], xT_hi, xT_lo, a_Tlo, g, q)
                if live(1):
                    g, q = t - 1, (par + 1) % 2
                    normed(xn, block(xs, g), meanvar, rstd, a_rstd, a_T, a_xn, g, q)
                if live(0):
                    if isinstance(t, int):
                        if t == 0:
                            for b in range(B):
                                dve.wait_ge(ld_x[b], 16)
                    moments(block(xs, t), stats, meanvar, a_stats, a_mv, a_rstd, t, par)

            pipeline(dve, step_a, 8)
            dve.drain().then_inc(phase, 1)
            dve.wait_ge(phase, 4)

            def value_lo(b):
                for j in range(NCH):
                    if j == 0:
                        wait(dve, b_pv, BPB * b)
                    dve.wait_ge(vw_hi, NCH * b + j + 1)
                    v.tensor_tensor(vwo_lo[:, j, :], bank[4 + j % 3][:, 0:D], vwo_hi[:, j, :].bitcast(F32),
                                    ALU.subtract).then_inc(vw_lo, 1)

            def step_b(t, par, live):
                if live(2):
                    g, q = t - 2, par
                    wait(dve, b_exp, 3 * (g - 1))
                    for i, (h0, h1) in enumerate(HEAD_GROUPS):
                        dve.wait_ge(b_sc, 3 * g + i + 1)
                        v.tensor_reduce(nmax[:, q, h0:h1], bank[1 + i][:, 0:(h1 - h0) * KEYS].rearrange("p (h k) -> p h k", k=KEYS),
                                        axis=AX, op=ALU.max, negate=True).then_inc(b_nmax, 1)
                if live(1):
                    g, q = t - 1, (par + 1) % 2
                    wait(dve, b_sc, 3 * (g - 1))
                    take_lo(b_Thi, bank[0], xT_hi, xT_lo, b_Tlo, g, q)
                if live(3):
                    g = t - 3
                    wait(dve, b_pv, g)
                    for i, (j0, j1) in enumerate(T_GROUPS):
                        dve.wait_ge(b_pThi, 3 * g + i + 1)
                        v.tensor_tensor(pT_lo[:, j0:j1, :].rearrange("p c n -> p (c n)"), bank[4 + i][:, 0:(j1 - j0) * P],
                                        pT_hi[:, j0:j1, :].rearrange("p c n -> p (c n)").bitcast(F32),
                                        ALU.subtract).then_inc(b_pTlo, 1)
                if live(0):
                    moments(block(xs, t), stats, meanvar, b_stats, b_mv, b_rstd, t, par)
                    normed(xn, block(xs, t), meanvar, rstd, b_rstd, b_T, b_xn, t, par)
                if live(2):
                    g, q = t - 2, par
                    dve.wait_ge(b_exp, 3 * (g + 1))
                    wait(dve, b_norm, g - 1)
                    v.reciprocal(rden[:, q, :], den[:, q, :]).then_inc(b_rden, 1)
                if live(3):
                    g = t - 3
                    dve.wait_ge(b_pv, g + 1)
                    v.tensor_tensor(block(xs, g), bank[7][:, 0:D], block(xs, g), ALU.add).then_inc(b_x3, 1)

            stage_b(dve, step_b, value_lo)
            dve.drain().then_inc(phase, 1)
            dve.wait_ge(phase, 8)

            dve.wait_ge(ld_ffn, 48)
            names = ("g", "u", "d")
            for i, nme in enumerate(names):
                ins = v.tensor_reduce(abs_sum[:, i:i + 1], raw[nme][:, :], axis=AX, op=ALU.add, apply_absolute_value=True)
            v.memset(abs_sum[:, 3:4], 1.0).then_inc(w_abs, 1)
            dve.wait_ge(w_sum, 1)
            chain(v.tensor_scalar(w_mean[:, :], bank[0][:, 0:4], 1.0 / (D * INNER), CLIP, ALU.mult, ALU.max))
            chain(v.reciprocal(w_inv[:, :], w_mean[:, :]))
            chain(v.tensor_scalar(up_127[:, :], w_mean[:, 1:2], 1.0 / QMAX, None, ALU.mult))
            for i, nme in enumerate(names):
                chain(v.tensor_scalar(wtmp[:, :], raw[nme][:, :], w_inv[:, i:i + 1], MAGIC, ALU.mult, ALU.add))
                chain(v.tensor_scalar(wtmp_b[:, :], wtmp[:, :], MAGIC, 1.0, ALU.subtract, ALU.min))
                chain(v.tensor_scalar(wq_b[nme][:, :], wtmp_b[:, :], -1.0, None, ALU.max))
            v.memset(abs_sum[:, 3:4], 1.0).then_inc(w_ready, 1)

            def step_c(t, par, live):
                if live(5):
                    g, q = t - 5, (par + 1) % 2
                    dve.wait_ge(c_dn, g + 1)
                    if not isinstance(g, int) or g >= 2:
                        dve.wait_ge(st_out[q], 8 * (g - q))
                    v.scalar_tensor_tensor(out=y[:, q, :], in0=bank[6][:, 0:D], scalar=s_y[:, slot4(t, 5), :], in1=block(xs, g),
                                           op0=ALU.mult, op1=ALU.add).then_inc(c_y, 1)
                if live(3):
                    g, q = t - 3, (par + 1) % 2
                    dve.wait_ge(c_hmax, g + 1)
                    v.tensor_scalar(c2[:, q, :], hmax[:, q, :], s_up127[:, slot4(t, 3), :], CLIP / QMAX, ALU.mult,
                                    ALU.max).then_inc(c_c2, 1)
                    dve.wait_ge(c_c2, g + 1)
                    v.tensor_scalar(s_y[:, slot4(t, 3), :], c2[:, q, :], w_mean[:, 2:3], None, ALU.mult)
                    wait(dve, c_sh, g - 1)
                    v.reciprocal(r2[:, q, :], c2[:, q, :]).then_inc(c_r2, 1)
                if live(1):
                    g, q = t - 1, (par + 1) % 2
                    normed(xn, block(xs, g), meanvar, rstd, c_rstd, c_qf, c_xn, g, q)
                    dve.wait_ge(c_xn, g + 1)
                    v.tensor_reduce(amax[:, q, :], xn[:, q, :], axis=AX, op=ALU.max, apply_absolute_value=True).then_inc(c_amax, 1)
                    dve.wait_ge(c_amax, g + 1)
                    v.tensor_scalar(c1[:, q, :], amax[:, q, :], 1.0 / QMAX, CLIP / QMAX, ALU.mult, ALU.max).then_inc(c_c1, 1)
                    dve.wait_ge(c_c1, g + 1)
                    v.reciprocal(r1[:, q, :], c1[:, q, :]).then_inc(c_r1, 1)
                    wait(dve, c_silu, 2 * (g - 1))
                    v.tensor_scalar(s_gate[:, q, :], c1[:, q, :], w_mean[:, 0:1], None, ALU.mult)
                    v.tensor_scalar(s_up[:, slot4(t, 1), :], c1[:, q, :], w_mean[:, 1:2], None, ALU.mult)
                    v.tensor_scalar(s_up127[:, slot4(t, 1), :], c1[:, q, :], up_127[:, :], None, ALU.mult).then_inc(c_scales, 1)
                    dve.wait_ge(c_r1, g + 1)
                    v.tensor_scalar(q_f[:, q, :], xn[:, q, :], r1[:, q, :], MAGIC, ALU.mult, ALU.add).then_inc(c_qf, 1)
                    dve.wait_ge(c_qf, g + 1)
                    wait(dve, c_T, g - 1)
                    v.tensor_scalar(q_b[:, q, :], q_f[:, q, :], MAGIC, None, ALU.subtract).then_inc(c_qb, 1)
                if live(2):
                    g, q = t - 2, par
                    wait(dve, c_hqf, g - 1)
                    for half in range(2):
                        cols = slice(half * BANK, (half + 1) * BANK)
                        dve.wait_ge(c_gu, 4 * g + 2 * half + 2)
                        dve.wait_ge(c_silu, 2 * g + half + 1)
                        v.tensor_tensor(h[:, q, cols], bank[2 + 2 * half][:, :], silu[:, q, cols], ALU.mult).then_inc(c_h, 1)
                    dve.wait_ge(c_h, 2 * g + 2)
                    v.tensor_reduce(hmax[:, q, :], h[:, q, :], axis=AX, op=ALU.max, apply_absolute_value=True).then_inc(c_hmax, 1)
                if live(0):
                    moments(block(xs, t), stats, meanvar, c_stats, c_mv, c_rstd, t, par)

            pipeline4(dve, step_c, 5)


def kernel(**inputs):
    import numpy as np
    import concourse.bacc as bacc
    from concourse.bass_utils import run_bass_kernel_spmd

    def arr(name):
        return np.asarray(inputs[name])

    def head_major(w):
        return w.reshape(D, HD, H).transpose(0, 2, 1).reshape(D, H * HD)

    layout = {
        "x": arr("x"),
        "cT": arr("ctx_1024").reshape(B * KEYS, D).T,
        "a_wg": arr("L0_xattn_Wg"), "a_bg": arr("L0_xattn_bg"), "a_wo": arr("L0_xattn_Wo"), "a_bo": arr("L0_xattn_bo"),
        "f_w": arr("L0_ffn_W"), "f_b": arr("L0_ffn_b"), "f_logits": arr("L0_ffn_logits"), "f_u": arr("L0_ffn_u"),
        "b_wqT": arr("L1_xattn_Wq").T, "b_wk": head_major(arr("L1_xattn_Wk")), "b_wv": head_major(arr("L1_xattn_Wv")),
        "b_wo": arr("L1_xattn_Wo"),
        "w_gateT": arr("L1_ffn_w_gate").T, "w_upT": arr("L1_ffn_w_up").T, "w_downT": arr("L1_ffn_w_down").T,
    }
    arrays = {"in_" + n: np.ascontiguousarray(a) for n, a in layout.items()}
    nc = bacc.Bacc("TRN2", target_bir_lowering=False, num_devices=1)
    aps = [nc.dram_tensor(n, a.shape, F32, kind="ExternalInput").ap() for n, a in arrays.items()]
    out = nc.dram_tensor("out_0", (B, S, D), F32, kind="ExternalOutput").ap()
    build(nc, *aps, out)
    return run_bass_kernel_spmd(nc, [arrays], core_ids=[0]).results[0]["out_0"]
```

```python
from contextlib import ExitStack

import concourse.bass as bass
from concourse import mybir

F32 = mybir.dt.float32
F32R = mybir.dt.float32r
BF16 = mybir.dt.bfloat16
F16 = mybir.dt.float16
U32 = mybir.dt.uint32
ALU = mybir.AluOpType
ACT = mybir.ActivationFunctionType
AX = mybir.AxisListType.X

P = 128
B, S, D = 4, 1024, 256
DC = D // P
NB = B * S // P
BPB = S // P
KEYS = 77
H, HD = 16, 64
HK = H * KEYS
NCH = -(-HK // P)
PAIRS = H // 2
BANK = 512
HEAD_GROUPS = ((0, 6), (6, 12), (12, 16))
T_GROUPS = ((0, 4), (4, 8), (8, 10))
OPS = 8
INNER = 1024
IC = INNER // P
EPS = 1e-5
MASKED = -3.0e38
MAGIC = 1.5 * 2.0 ** 23
OFFSET_16 = 1536.0
MAGIC_16 = 2.0 ** 23 + (0x6400 + OFFSET_16 - 1024)
QMAX = 127.0
CLIP = 1e-5
PADV = P - 1


def wait(eng, sem, count):
    if not (isinstance(count, int) and count <= 0):
        eng.wait_ge(sem, count)


def overlaps(j):
    return [p for p in range(PAIRS) if 2 * KEYS * p < P * (j + 1) and 2 * KEYS * (p + 1) > P * j]


def build(nc, x, cT_in, a_wg, a_bg, a_wo, a_bo, f_w, f_b, f_logits, f_u,
          b_wqT, b_wk, b_wv, b_wo, w_gateT, w_upT, w_downT, out):
    ctx = ExitStack()
    with ctx:
        def sem(name):
            return ctx.enter_context(nc.semaphore(name))

        def alloc(stack, name, shape, dt=F32):
            return stack.enter_context(nc.sbuf_tensor(name, shape, dt))

        xs = alloc(ctx, "xs", [P, NB, D])
        ident = alloc(ctx, "ident", [P, P])
        ident_h = alloc(ctx, "ident_h", [P, P], F16)
        mhalf = alloc(ctx, "mhalf", [P, 1])
        ones_b = alloc(ctx, "ones_b", [P, P], BF16)
        ones = alloc(ctx, "ones", [P, P])
        stats = alloc(ctx, "stats", [P, 2, 6])
        meanvar = alloc(ctx, "meanvar", [P, 2, 2])
        var_eps = alloc(ctx, "var_eps", [P, 2, 1])
        rstd = alloc(ctx, "rstd", [P, 2, 1])
        shift = alloc(ctx, "shift", [P, 2, 1])
        xn = alloc(ctx, "xn", [P, 2, D])
        xT_hi = alloc(ctx, "xT_hi", [P, 2, DC, P], F32R)
        xT_lo = alloc(ctx, "xT_lo", [P, 2, DC, P], F32R)

        c1_all = alloc(ctx, "c1_all", [P, NB])
        a_all = alloc(ctx, "a_all", [P, NB])
        b_all = alloc(ctx, "b_all", [P, NB])
        abs_sum = alloc(ctx, "abs_sum", [P, 4])
        w_sum = alloc(ctx, "w_sum", [P, 4])
        w_mean = alloc(ctx, "w_mean", [P, 4])
        w_inv = alloc(ctx, "w_inv", [P, 4])

        with ExitStack() as ffn:
            wq_b = {n: alloc(ffn, f"wq_{n}", [P, 2 * INNER], BF16) for n in ("g", "u", "d")}
            raw = {n: alloc(ffn, f"raw_{n}", [P, 2 * INNER]) for n in ("g", "u", "d")}
            wtmp = alloc(ffn, "wtmp", [P, 2 * INNER])
            wtmp_b = alloc(ffn, "wtmp_b", [P, 2 * INNER], BF16)
        FFN_BYTES = 3 * 2 * INNER * 2 + 3 * 2 * INNER * 4 + 2 * INNER * 6
        assert FFN_BYTES <= (B - 1) * 2 * DC * HK * 4

        ab = ExitStack()
        m_all = alloc(ab, "m_all", [P, B, 2, DC, HK], F32R)
        m_hi, m_lo = m_all[:, :, 0], m_all[:, :, 1]
        vT = alloc(ab, "vT", [P, PAIRS, B, KEYS])
        wo1 = alloc(ab, "wo1", [P, PAIRS, D])
        mask_row = alloc(ab, "mask_row", [1, B, KEYS], BF16)

        pa = ExitStack()
        cT = alloc(pa, "cT", [P, DC, B * KEYS])
        nonzero = alloc(pa, "nonzero", [P, DC, B * KEYS], BF16)
        wg0 = alloc(pa, "wg0", [P, DC, D])
        wo0 = alloc(pa, "wo0", [P, DC, D])
        bg = alloc(pa, "bg", [P, DC])
        bo = alloc(pa, "bo", [KEYS, D])
        wv = alloc(pa, "wv", [P, DC, H * HD])
        wqT = alloc(pa, "wqT", [P, PAIRS, D])
        kT = alloc(pa, "kT", [P, PAIRS, B * KEYS])
        gate = alloc(pa, "gate", [P, DC, B * KEYS])
        gate_hi = alloc(pa, "gate_hi", [P, B, DC, KEYS + 1], F32R)
        gate_lo = alloc(pa, "gate_lo", [P, B, DC, KEYS + 1], F32R)
        cwo = alloc(pa, "cwo", [KEYS, D])
        cwo_hi = alloc(pa, "cwo_hi", [KEYS, B, D], F32R)
        cwo_lo = alloc(pa, "cwo_lo", [KEYS, B, D], F32R)
        logit = alloc(pa, "logit", [1, OPS])
        uni = alloc(pa, "uni", [1, OPS])
        pick = alloc(pa, "pick", [1, 8, OPS])
        picked = alloc(pa, "picked", [1, OPS], U32)
        wsel = alloc(pa, "wsel", [P, DC, D])
        wsel_hi = alloc(pa, "wsel_hi", [P, DC, D], F32R)
        wsel_lo = alloc(pa, "wsel_lo", [P, DC, D], F32R)
        bsel = alloc(pa, "bsel", [P, D])
        with ExitStack() as key_weights:
            wk = alloc(key_weights, "wk", [P, DC, H * HD])
        stats2 = alloc(pa, "stats2", [P, 2, 6])
        meanvar2 = alloc(pa, "meanvar2", [P, 2, 2])
        var_eps2 = alloc(pa, "var_eps2", [P, 2, 1])
        rstd2 = alloc(pa, "rstd2", [P, 2, 1])
        shift2 = alloc(pa, "shift2", [P, 2, 1])
        xn2 = alloc(pa, "xn2", [P, 2, D])
        x2T_hi = alloc(pa, "x2T_hi", [P, 2, DC, P], F32R)
        x2T_lo = alloc(pa, "x2T_lo", [P, 2, DC, P], F32R)
        nmax0 = alloc(pa, "nmax0", [P, 2, 1])
        den0 = alloc(pa, "den0", [P, 2, 1])
        rden0 = alloc(pa, "rden0", [P, 2, 1])
        e0 = alloc(pa, "e0", [P, 2, KEYS])
        e0T_hi = alloc(pa, "e0T_hi", [KEYS, 2, P], F32R)
        e0T_lo = alloc(pa, "e0T_lo", [KEYS, 2, P], F32R)
        pa.close()

        pb = ExitStack()
        pair_vT = alloc(pb, "pair_vT", [P, PAIRS, 2 * KEYS + 2 * PADV])
        vwo_hi = alloc(pb, "vwo_hi", [P, NCH, D], F32R)
        vwo_lo = alloc(pb, "vwo_lo", [P, NCH, D], F32R)
        e = alloc(pb, "e", [P, 2, NCH * P])
        nmax = alloc(pb, "nmax", [P, 2, H])
        den = alloc(pb, "den", [P, 2, H])
        rden = alloc(pb, "rden", [P, 2, H])
        pT_hi = alloc(pb, "pT_hi", [P, NCH, P], F32R)
        pT_lo = alloc(pb, "pT_lo", [P, NCH, P], F32R)
        stats3 = alloc(pb, "stats3", [P, 2, 6])
        meanvar3 = alloc(pb, "meanvar3", [P, 2, 2])
        var_eps3 = alloc(pb, "var_eps3", [P, 2, 1])
        rstd3 = alloc(pb, "rstd3", [P, 2, 1])
        shift3 = alloc(pb, "shift3", [P, 2, 1])
        xn3 = alloc(pb, "xn3", [P, 2, D])
        amax = alloc(pb, "amax", [P, 2, 1])
        r1 = alloc(pb, "r1", [P, 2, 1])
        pb.close()
        ab.close()

        alloc(ctx, "below", [P, FFN_BYTES // 4])
        q_t = alloc(ctx, "q_t", [P, 2, D])
        qT = alloc(ctx, "qT", [P, 2, DC, P], BF16)
        s_gate = alloc(ctx, "s_gate", [P, 4, 1])
        s_up = alloc(ctx, "s_up", [P, 4, 1])
        silu = alloc(ctx, "silu", [P, 2, INNER])
        h = alloc(ctx, "h", [P, 2, INNER])
        hmax = alloc(ctx, "hmax", [P, 2, 1])
        c2 = alloc(ctx, "c2", [P, 2, 1])
        r2 = alloc(ctx, "r2", [P, 2, 1])
        s_h = alloc(ctx, "s_h", [P, 2, 2])
        s_y = alloc(ctx, "s_y", [P, 4, 1])
        hq_f = alloc(ctx, "hq_f", [P, 2, INNER])
        hqT = alloc(ctx, "hqT", [P, 2, IC, P], BF16)
        y = alloc(ctx, "y", [P, 2, D])

        bank = [ctx.enter_context(nc.psum_tensor(f"bank{i}", [P, BANK], F32)) for i in range(8)]

        ld_c, ld_a, ld_pick, ld_k, ld_q, ld_v, ld_wo, ld_sel, ld_ffn = (
            sem(n) for n in ("ld_c", "ld_a", "ld_pick", "ld_k", "ld_q", "ld_v", "ld_wo", "ld_sel", "ld_ffn"))
        st_out = [sem("st_even"), sem("st_odd")]
        ld_x = [sem(f"ld_x{b}") for b in range(B)]
        consts, dve_seq, picked_ok, pick_ln, pick_z = (sem(n) for n in ("consts", "dve_seq", "picked_ok", "pick_ln", "pick_z"))
        nz_ok, cnt_ok, mask_ok, k_gate, cwo_ok = (sem(n) for n in ("nz_ok", "cnt_ok", "mask_ok", "k_gate", "cwo_ok"))
        prep_mm, prep_hi, prep_lo, sel_hi = (sem(n) for n in ("prep_mm", "prep_hi", "prep_lo", "sel_hi"))
        phase = sem("phase")
        a_stats, a_mv, a_eps, a_rstd, a_xn, a_T, a_Thi, a_Tlo, a_sc, a_nmax, a_exp, a_eT, a_eThi, a_eTlo, a_rden, a_pv = (
            sem("a_" + n) for n in ("stats", "mv", "eps", "rstd", "xn", "T", "Thi", "Tlo", "sc", "nmax", "exp", "eT",
                                    "eThi", "eTlo", "rden", "pv"))
        a_shift, f_shift = sem("a_shift"), sem("f_shift")
        f_x1, f_stats, f_mv, f_eps, f_rstd, f_xn, f_bias, f_T, f_Thi, f_Tlo, f_mm, f_x2 = (
            sem("f_" + n) for n in ("x1", "stats", "mv", "eps", "rstd", "xn", "bias", "T", "Thi", "Tlo", "mm", "x2"))
        b_stats, b_mv, b_eps, b_rstd, b_xn, b_T, b_Thi, b_Tlo, b_pv, b_x3 = (
            sem("b_" + n) for n in ("stats", "mv", "eps", "rstd", "xn", "T", "Thi", "Tlo", "pv", "x3"))
        n_stats, n_mv, n_eps, n_rstd, n_shift, n_xn, n_amax, n_c1, n_r1, n_ab = (
            sem("n_" + n) for n in ("stats", "mv", "eps", "rstd", "shift", "xn", "amax", "c1", "r1", "ab"))
        b_rden, b_norm = sem("b_rden"), sem("b_norm")
        b_sc, b_nmax, b_exp = sem("b_sc"), sem("b_nmax"), sem("b_exp")
        b_pT, b_pThi, b_pTlo = sem("b_pT"), sem("b_pThi"), sem("b_pTlo")
        e_pad, v_zero, v_pair, vw_mm, vw_hi, vw_lo = (sem(n) for n in ("e_pad", "v_zero", "v_pair", "vw_mm", "vw_hi", "vw_lo"))
        w_abs, w_summed, w_ready = sem("w_abs"), sem("w_summed"), sem("w_ready")
        c_scales, c_qt, c_T, c_qT, c_hmax, c_c2, c_r2, c_sy, c_sh, c_hqf, c_hT, c_hqT, c_dn, c_y = (
            sem("c_" + n) for n in ("scales", "qt", "T", "qT", "hmax", "c2", "r2", "sy", "sh", "hqf",
                                    "hT", "hqT", "dn", "y"))
        c_silu, c_h = sem("c_silu"), sem("c_h")
        c_gu = sem("c_gu")

        def pipeline(eng, step, depth, lead=0, first=0, last=NB):
            start = first + depth + 2
            count = (last - lead - start) // 2 * 2
            for t in range(first - lead, start):
                step(t, t % 2, lambda k, t=t: first <= t - k < last)
            with eng.Fori(0, count // 2) as i:
                t = i * 2 + start
                step(t, start % 2, lambda k: True)
                step(t + 1, (start + 1) % 2, lambda k: True)
            for t in range(start + count, last + depth):
                step(t, t % 2, lambda k, t=t: first <= t - k < last)

        def stage_b(eng, step, at_batch, last_batch=True):
            def two_steps(t):
                step(t, 1, lambda k: True)
                step(t + 1, 0, lambda k: True)

            for t in range(7):
                if t == 3:
                    at_batch(0)
                step(t, t % 2, lambda k, t=t: t >= k)
            with eng.Fori(0, 2) as i:
                two_steps(i * 2 + 7)
            with eng.Fori(0, B - 2) as b:
                at_batch(b + 1)
                with eng.Fori(0, BPB // 2) as i:
                    two_steps(b * BPB + i * 2 + BPB + 3)
            if last_batch:
                at_batch(B - 1)
            for t in range((B - 1) * BPB + 3, NB + 5):
                step(t, t % 2, lambda k, t=t: t - k < NB)

        def slot4(t, k):
            return slots4[(id4[0] - k) % 4]

        slots4, id4 = [0, 1, 2, 3], [0]

        def pipeline4(eng, step, depth, last=NB):
            start = -(-depth // 4) * 4
            for t in range(start):
                id4[0] = t % 4
                step(t, t % 2, lambda k, t=t: 0 <= t - k < last)
            with eng.Fori(0, (last - start) // 4) as n:
                t = n * 4 + start
                for i in range(4):
                    id4[0] = i
                    step(t + i, i % 2, lambda k: True)
            for t in range(last, last + depth):
                id4[0] = t % 4
                step(t, t % 2, lambda k, t=t: 0 <= t - k < last)

        def wait_apart(eng, *needs):
            counts = [(sem_, n if isinstance(n, int) else eng.compute_val(n)) for sem_, n in needs]
            eng.wait_ge(consts, 4)
            for sem_, n in counts:
                wait(eng, sem_, n)

        T_SUM = (B - 1) * BPB + 8

        def batch_of(g):
            return g // BPB

        def block(tile, g):
            return tile[:, bass.ds(g, 1), :].rearrange("p o d -> p (o d)")

        N_GATE, N_CWO, N_K, N_V, N_M = DC, B, PAIRS, PAIRS, 2 * H
        FIRST_CWO = N_GATE
        FIRST_K = FIRST_CWO + N_CWO
        FIRST_M = FIRST_K + N_K
        FIRST_V = FIRST_M + N_M
        N_PREP = FIRST_V + N_V

        def low_parts(n):
            return min(n, FIRST_K) + min(max(n - FIRST_M, 0), N_M)

        PREP_BANKS = 7

        blk = ctx.enter_context(nc.Block())

        @blk.sync
        def _(sp):
            sp.dma_start(cT[:, :, :], cT_in.rearrange("(c p) n -> p c n", p=P)).then_inc(ld_c, 16)
            sp.dma_start(wg0[:, :, :], a_wg.rearrange("(c p) n -> p c n", p=P)).then_inc(ld_a, 16)
            with nc.allow_non_contiguous_dma(reason="256 biases, once"):
                sp.dma_start(bg[:, :], a_bg.rearrange("(c p) -> p c", p=P)).then_inc(ld_a, 16)
            sp.dma_start(wo0[:, :, :], a_wo.rearrange("(c p) n -> p c n", p=P)).then_inc(ld_a, 16)
            sp.dma_start(bo[:, :], a_bo.rearrange("(o n) -> o n", o=1).broadcast_to([KEYS, D])).then_inc(ld_a, 16)
            sp.dma_start(logit[:, :], f_logits.rearrange("(o n) -> o n", o=1)).then_inc(ld_pick, 16)
            sp.dma_start(uni[:, :], f_u.rearrange("(o n) -> o n", o=1)).then_inc(ld_pick, 16)
            sp.dma_start(wk[:, :, :], b_wk.rearrange("(c p) n -> p c n", p=P)).then_inc(ld_k, 16)
            sp.dma_start(wqT[:, :, :], b_wqT.rearrange("(c p) n -> p c n", p=P)).then_inc(ld_q, 16)
            xb = x.rearrange("b (g p) d -> b p g d", p=P)
            sp.dma_start(xs[:, 0:BPB, :], xb[0]).then_inc(ld_x[0], 16)
            sp.dma_start(wv[:, :, :], b_wv.rearrange("(c p) n -> p c n", p=P)).then_inc(ld_v, 16)
            sp.dma_start(wo1[:, :, :], b_wo.rearrange("(c p) n -> p c n", p=P)).then_inc(ld_wo, 16)
            for b in range(1, B):
                sp.dma_start(xs[:, b * BPB:(b + 1) * BPB, :], xb[b]).then_inc(ld_x[b], 16)
            sp.wait_ge(picked_ok, 1)
            op = sp.value_load(picked[0:1, 0:1], min_val=0, max_val=OPS - 1)
            sp.dma_start(wsel[:, :, :], f_w[bass.ds(op, 1), :, :].rearrange("o (c p) n -> p (o c) n", p=P)).then_inc(ld_sel, 16)
            sp.dma_start(bsel[:, :], f_b[bass.ds(op, 1), :].broadcast_to([P, D])).then_inc(ld_sel, 16)
            sp.wait_ge(b_sc, 3 * (B - 1) * BPB)
            for n, src in (("g", w_gateT), ("u", w_upT), ("d", w_downT)):
                sp.dma_start(raw[n][:, :].rearrange("p (c n) -> p c n", n=src.shape[1]),
                             src.rearrange("(c p) n -> p c n", p=P)).then_inc(ld_ffn, 16)
            outb = out.rearrange("b (g p) d -> (b g) p d", p=P)
            with sp.Fori(0, NB // 2) as i:
                for q in range(2):
                    sp.wait_ge(c_y, i * 2 + q + 1)
                    sp.dma_start(outb[bass.ds(i * 2 + q, 1), :, :].rearrange("o p d -> (o p) d"), y[:, q, :]).then_inc(st_out[q], 16)
            for q in range(2):
                sp.wait_ge(st_out[q], 16 * (NB // 2))

        @blk.gpsimd
        def _(pool):
            gp = nc.gpsimd
            gp.memset(ident[:, :], 0.0).then_inc(consts, 1)
            gp.memset(mhalf[:, :], -0.5).then_inc(consts, 1)
            gp.memset(ones[:, :], 1.0).then_inc(consts, 1)
            gp.memset(ones_b[:, :], 1.0).then_inc(consts, 1)
            pool.wait_ge(consts, 4)
            gp.affine_select(out=ident[:, :], in_=ident[:, :], compare_op=ALU.not_equal, fill=1.0, base=0,
                             pattern=[[-1, P]], channel_multiplier=1).then_inc(consts, 1)
            pool.wait_ge(consts, 5)
            gp.tensor_copy(ident_h[:, :], ident[:, :]).then_inc(consts, 1)

            def inverse_root(ready, mv, ve, rs, eps_done, done, free, g, par):
                wait_apart(pool, (ready, g + 1), *([(free, g - 1)] if free else []))
                gp.tensor_scalar(ve[:, par, :], mv[:, par, 1:2], EPS, 1.0, ALU.add, ALU.mult).then_inc(eps_done, 1)
                pool.wait_ge(eps_done, g + 1)
                gp.tensor_tensor(rs[:, par, :], ve[:, par, :], mhalf[:, :], ALU.pow).then_inc(done, 1)

            def norm_shift(mv, rs, sh, rstd_done, free, done, g, par):
                wait_apart(pool, (rstd_done, g + 1), (free, g - 1))
                gp.tensor_scalar(sh[:, par, :], mv[:, par, 0:1], rs[:, par, :], -1.0, ALU.mult, ALU.mult).then_inc(done, 1)

            def step_a(t, par, live):
                if live(7):
                    g = t - 7
                    pool.wait_ge(f_xn, g + 1)
                    if isinstance(g, int) and g == 0:
                        pool.wait_ge(ld_sel, 32)
                    gp.tensor_tensor(block(xs, g), block(xs, g), bsel[:, :], ALU.add).then_inc(f_bias, 1)
                if live(5):
                    inverse_root(f_mv, meanvar2, var_eps2, rstd2, f_eps, f_rstd, f_xn, t - 5, (par + 1) % 2)
                    norm_shift(meanvar2, rstd2, shift2, f_rstd, f_xn, f_shift, t - 5, (par + 1) % 2)
                if live(-1):
                    inverse_root(a_mv, meanvar, var_eps, rstd, a_eps, a_rstd, a_xn, t + 1, (par + 1) % 2)
                    norm_shift(meanvar, rstd, shift, a_rstd, a_xn, a_shift, t + 1, (par + 1) % 2)

            pipeline(pool, step_a, 9, lead=1)
            pool.drain().then_inc(phase, 1)

            pool.wait_ge(phase, 4)
            gp.memset(pair_vT[:, :, :], 0.0).then_inc(v_zero, 1)
            gp.memset(e[:, :, HK:NCH * P], 0.0).then_inc(e_pad, 1)
            pool.wait_ge(v_zero, 1)
            pool.wait_ge(e_pad, 1)

            def pair_values(b):
                for half in range(2):
                    rows = slice(half * HD, (half + 1) * HD)
                    at = PADV + half * KEYS
                    gp.tensor_copy(pair_vT[rows, :, at:at + KEYS],
                                   vT[rows, :, bass.ds(b, 1), :].rearrange("p c o k -> p c (o k)")).then_inc(v_pair, 1)
                    wait_apart(pool, (v_pair, 2 * b + half + 1))

            def step_b(t, par, live):
                if live(4):
                    inverse_root(n_mv, meanvar3, var_eps3, rstd3, n_eps, n_rstd, None, t - 4, par)
                    norm_shift(meanvar3, rstd3, shift3, n_rstd, n_ab, n_shift, t - 4, par)
                if live(0):
                    inverse_root(b_mv, meanvar, var_eps, rstd, b_eps, b_rstd, None, t, par)
                if live(2):
                    g, q = t - 2, par
                    for i, (h0, h1) in enumerate(HEAD_GROUPS):
                        pool.wait_ge(b_rden, 3 * g + i + 1)
                        eh = e[:, q, h0 * KEYS:h1 * KEYS].rearrange("p (h k) -> p h k", k=KEYS)
                        gp.tensor_tensor(eh, eh, rden[:, q, h0:h1].rearrange("p (h o) -> p h o", o=1).broadcast_to(
                            [P, h1 - h0, KEYS]), ALU.mult).then_inc(b_norm, 1)
                if isinstance(t, int) and t == T_SUM:
                    pool.wait_ge(w_abs, 1)
                    gp.partition_all_reduce(w_sum[:, :], abs_sum[:, :], P, bass.bass_isa.ReduceOp.add).then_inc(w_summed, 1)

            pair_values(0)
            stage_b(pool, step_b, lambda b: (pool.wait_ge(vw_mm, NCH * (b + 1)), pair_values(b + 1)), last_batch=False)
            pool.drain().then_inc(phase, 1)

            def step_c(t, par, live):
                if live(3):
                    g, q = t - 3, (par + 1) % 2
                    up = s_up[:, slot4(t, 3), :]
                    wait_apart(pool, (c_r2, g + 1), (c_hqf, g - 1))
                    gp.tensor_scalar(s_h[:, q, 0:1], r2[:, q, :], up, QMAX, ALU.mult, ALU.mult).then_inc(c_sh, 1)
                    wait_apart(pool, (c_sh, g + 1), (c_hT, g - 1))
                    gp.tensor_scalar(hq_f[:, q, :], h[:, q, :], s_h[:, q, 0:1], MAGIC_16, ALU.mult, ALU.add).then_inc(c_hqf, 1)

            pipeline4(pool, step_c, 6)

        @blk.tensor
        def _(pe):
            mm = nc.tensor.matmul

            def split_mm(o, a_hi, a_lo, c_hi, c_lo, start, stop):
                mm(o, a_hi, c_hi, start=start, stop=False)
                mm(o, a_hi, c_lo, start=False, stop=False)
                return mm(o, a_lo, c_hi, start=False, stop=stop)

            pe.wait_ge(nz_ok, 1)
            pe.wait_ge(consts, 4)
            for c in range(DC):
                last = mm(bank[7][0:1, 0:B * KEYS], ones_b[:, 0:1], nonzero[:, c, :], start=c == 0, stop=c == DC - 1)
            last.then_inc(cnt_ok, 1)

            n = 0

            def free_bank():
                if n >= PREP_BANKS:
                    pe.wait_ge(prep_hi, n - PREP_BANKS + 1)
                    pe.wait_ge(prep_lo, low_parts(n - PREP_BANKS + 1))
                return bank[n % PREP_BANKS]

            pe.wait_ge(ld_c, 16)
            pe.wait_ge(ld_a, 64)
            for eo in range(DC):
                o = free_bank()[:, 0:B * KEYS]
                for c in range(DC):
                    last = mm(o, wg0[:, c, eo * P:(eo + 1) * P], cT[:, c, :], start=c == 0, stop=c == DC - 1)
                last.then_inc(prep_mm, 1)
                n += 1
            for b in range(B):
                o = free_bank()[0:KEYS, 0:D]
                for c in range(DC):
                    last = mm(o, cT[:, c, b * KEYS:(b + 1) * KEYS], wo0[:, c, :], start=c == 0, stop=c == DC - 1)
                last.then_inc(prep_mm, 1)
                n += 1

            def project_context(w):
                nonlocal n
                for p in range(PAIRS):
                    o = free_bank()[:, 0:B * KEYS]
                    for c in range(DC):
                        last = mm(o, w[:, c, p * P:(p + 1) * P], cT[:, c, :], start=c == 0, stop=c == DC - 1)
                    last.then_inc(prep_mm, 1)
                    n += 1

            pe.wait_ge(ld_k, 16)
            project_context(wk)
            pe.wait_ge(ld_q, 16)
            for hh in range(H):
                rows = slice(HD * (hh % 2), HD * (hh % 2) + HD)
                pe.wait_ge(prep_hi, FIRST_K + hh // 2 + 1)
                for io in range(DC):
                    mm(free_bank()[:, 0:B * KEYS], wqT[rows, hh // 2, io * P:(io + 1) * P], kT[rows, hh // 2, :],
                       start=True, stop=True).then_inc(prep_mm, 1)
                    n += 1
            pe.wait_ge(ld_v, 16)
            project_context(wv)

            pe.wait_ge(prep_hi, N_PREP)
            pe.wait_ge(prep_lo, low_parts(N_PREP))
            pe.wait_ge(consts, 6)
            T1, SC, ET, PV, T2, FF = (bank[0], bank[6]), bank[1], bank[2], bank[3], (bank[4], bank[7]), bank[5]

            COPIES = 3

            def step_a(t, par, live):
                if live(7):
                    g, q = t - 7, (par + 1) % 2
                    pe.wait_ge(f_xn, g + 1)
                    wait(pe, f_Tlo, g - 1)
                    for c in range(DC):
                        last = nc.tensor.transpose(T2[q][:, c * P:(c + 1) * P], xn2[:, q, c * P:(c + 1) * P], ident[:, :])
                    last.then_inc(f_T, 1)
                if live(1):
                    g, q = t - 1, (par + 1) % 2
                    pe.wait_ge(a_xn, g + 1)
                    wait(pe, a_Tlo, g - 1)
                    for c in range(DC):
                        last = nc.tensor.transpose(T1[q][:, c * P:(c + 1) * P], xn[:, q, c * P:(c + 1) * P], ident[:, :])
                    last.then_inc(a_T, 1)
                if live(3):
                    g, q = t - 3, (par + 1) % 2
                    pe.wait_ge(a_exp, g + 1)
                    wait(pe, a_eTlo, g)
                    nc.tensor.transpose(ET[0:KEYS, 0:P], e0[:, q, :], ident[:, :]).then_inc(a_eT, 1)
                if live(8):
                    g, q = t - 8, par
                    pe.wait_ge(f_Tlo, g + 1)
                    wait(pe, f_x2, g)
                    if isinstance(g, int) and g == 0:
                        pe.wait_ge(sel_hi, 2)
                    for c in range(DC):
                        last = split_mm(FF[:, 0:D], x2T_hi[:, q, c, :], x2T_lo[:, q, c, :], wsel_hi[:, c, :],
                                        wsel_lo[:, c, :], c == 0, c == DC - 1)
                    last.then_inc(f_mm, 1)
                if live(2):
                    g, q = t - 2, par
                    pe.wait_ge(a_Tlo, g + 1)
                    wait(pe, a_exp, g)
                    b = batch_of(g)
                    for c in range(DC):
                        gates = [gt[:, bass.ds(b, 1), c, :].broadcast_to([P, COPIES, KEYS + 1]) for gt in (gate_hi, gate_lo)]
                        last = split_mm(SC[:, 0:COPIES * (KEYS + 1)], xT_hi[:, q, c, :], xT_lo[:, q, c, :],
                                        gates[0], gates[1], c == 0, c == DC - 1)
                    last.then_inc(a_sc, 1)
                if live(4):
                    g, q = t - 4, par
                    pe.wait_ge(a_eTlo, g + 1)
                    wait(pe, f_x1, g)
                    b = batch_of(g)
                    split_mm(PV[:, 0:D], e0T_hi[:, q, :], e0T_lo[:, q, :],
                             cwo_hi[:, bass.ds(b, 1), :].rearrange("p o d -> p (o d)"),
                             cwo_lo[:, bass.ds(b, 1), :].rearrange("p o d -> p (o d)"), True, True).then_inc(a_pv, 1)

            pipeline(pe, step_a, 9, lead=1)
            pe.drain().then_inc(phase, 1)

            pe.wait_ge(phase, 4)
            XT, SCB, PT, OB = bank[0], bank[1:4], bank[4:7], bank[7]

            def value_out(b):
                pe.wait_ge(v_pair, 2 * b + 2)
                for j in range(NCH):
                    if j < 3:
                        wait(pe, b_pTlo, 3 * BPB * b)
                        wait(pe, b_pThi, 3 * BPB * b)
                    else:
                        pe.wait_ge(vw_hi, NCH * b + j - 2)
                        pe.wait_ge(vw_lo, NCH * b + j - 2)
                    ps = overlaps(j)
                    for p in ps:
                        at = P * j - 2 * KEYS * p + PADV
                        last = mm(PT[j % 3][:, 0:D], pair_vT[:, p, at:at + P], wo1[:, p, :],
                                  start=p == ps[0], stop=p == ps[-1])
                    last.then_inc(vw_mm, 1)
                wait_apart(pe, (vw_hi, NCH * (b + 1)), (vw_lo, NCH * (b + 1)))

            def scores(g, q, b, i):
                h0, h1 = HEAD_GROUPS[i]
                w = (h1 - h0) * KEYS
                wait_apart(pe, (b_exp, 3 * g - 2 + i))
                mrow = mask_row[0:1, bass.ds(b, 1), :].broadcast_to([1, h1 - h0, KEYS])
                mm(SCB[i][:, 0:w], ones_b[0:1, :], mrow, start=True, stop=False)
                for c in range(DC):
                    ms = [m[:, bass.ds(b, 1), c, h0 * KEYS:h1 * KEYS].rearrange("p o d -> p (o d)") for m in (m_hi, m_lo)]
                    last = split_mm(SCB[i][:, 0:w], xT_hi[:, q, c, :], xT_lo[:, q, c, :], ms[0], ms[1], False, c == DC - 1)
                last.then_inc(b_sc, 1)

            def step_b(t, par, live):
                if live(2):
                    pe.wait_ge(b_Tlo, t - 1)
                    scores(t - 2, par, batch_of(t - 2), 0)
                if live(3):
                    g, q = t - 3, (par + 1) % 2
                    if isinstance(g, int) and g == 0:
                        pe.wait_ge(e_pad, 1)
                    wait(pe, b_pTlo, 3 * g)
                    for i, (j0, j1) in enumerate(T_GROUPS):
                        pe.wait_ge(b_norm, 3 * g + min(i + 2, 3))
                        for j in range(j0, j1):
                            last = nc.tensor.transpose(PT[i][:, (j - j0) * P:(j - j0 + 1) * P],
                                                       e[:, q, j * P:(j + 1) * P], ident[:, :])
                        last.then_inc(b_pT, 1)
                if live(2):
                    scores(t - 2, par, batch_of(t - 2), 1)
                    scores(t - 2, par, batch_of(t - 2), 2)
                if live(1):
                    g, q = t - 1, (par + 1) % 2
                    pe.wait_ge(b_xn, g + 1)
                    wait(pe, b_Tlo, g)
                    for c in range(DC):
                        last = nc.tensor.transpose(XT[:, c * P:(c + 1) * P], xn[:, q, c * P:(c + 1) * P], ident[:, :])
                    last.then_inc(b_T, 1)
                if live(3):
                    g = t - 3
                    wait(pe, b_x3, g)
                    for i, (j0, j1) in enumerate(T_GROUPS):
                        pe.wait_ge(b_pTlo, 3 * g + 1 + i)
                        for j in range(j0, j1):
                            last = split_mm(OB[:, 0:D], pT_hi[:, j, :], pT_lo[:, j, :], vwo_hi[:, j, :], vwo_lo[:, j, :],
                                            j == 0, j == NCH - 1)
                    last.then_inc(b_pv, 1)

            stage_b(pe, step_b, value_out)
            pe.drain().then_inc(phase, 1)

            pe.wait_ge(phase, 8)
            XQ, GU, HT, YB = bank[0], bank[1:5], [bank[i][:, :].bitcast(F16) for i in (5, 6)], bank[7]
            pe.wait_ge(w_ready, 3)
            wg = wq_b["g"][:, :].rearrange("p (c n) -> p c n", c=DC)
            wu = wq_b["u"][:, :].rearrange("p (c n) -> p c n", c=DC)
            wd = wq_b["d"][:, :].rearrange("p (c n) -> p c n", c=IC)

            def step_c(t, par, live):
                if live(1):
                    g, q = t - 1, (par + 1) % 2
                    pe.wait_ge(c_qt, g + 1)
                    wait(pe, c_qT, g)
                    for c in range(DC):
                        last = nc.tensor.transpose(XQ[:, c * P:(c + 1) * P], q_t[:, q, c * P:(c + 1) * P], ident[:, :])
                    last.then_inc(c_T, 1)
                if live(2):
                    g, q = t - 2, par
                    pe.wait_ge(c_qT, g + 1)
                    for i in range(4):
                        w, half = (wg, wu)[i % 2], i // 2
                        wait(pe, c_h, 2 * (g - 1) + half + 1)
                        for c in range(DC):
                            last = mm(GU[i][:, :], qT[:, q, c, :], w[:, c, half * BANK:(half + 1) * BANK],
                                      start=c == 0, stop=c == DC - 1)
                        last.then_inc(c_gu, 1)
                if live(4):
                    g, q = t - 4, par
                    pe.wait_ge(c_hqf, g + 1)
                    low = hq_f[:, q, :].bitcast(F16).rearrange("p (n two) -> p n two", two=2)[:, :, 0]
                    wait(pe, c_hqT, g - 1)
                    for j in range(IC):
                        last = nc.tensor.transpose(HT[q][:, j * P:(j + 1) * P], low[:, j * P:(j + 1) * P], ident_h[:, :])
                    last.then_inc(c_hT, 1)
                if live(5):
                    g, q = t - 5, (par + 1) % 2
                    pe.wait_ge(c_hqT, g + 1)
                    wait(pe, c_y, g)
                    for j in range(IC):
                        last = mm(YB[:, 0:D], hqT[:, q, j, :], wd[:, j, :], start=j == 0, stop=j == IC - 1)
                    last.then_inc(c_dn, 1)

            pipeline4(pe, step_c, 6)

        @blk.scalar
        def _(act):
            sc = nc.scalar
            act.wait_ge(ld_pick, 32)
            sc.activation(pick[:, 0, :], uni[:, :], ACT.Ln).then_inc(pick_ln, 1)
            act.wait_ge(pick_ln, 1)
            sc.activation(pick[:, 1, :], pick[:, 0, :], ACT.Ln, scale=-1.0).then_inc(pick_ln, 1)
            act.wait_ge(pick_z, 1)
            sc.activation(pick[:, 3, :], pick[:, 2, :], ACT.Exp, accum_out=pick[:, 4, 0:1]).then_inc(pick_ln, 1)
            act.wait_ge(pick_ln, 3)
            sc.activation(pick[:, 4, 1:2], pick[:, 4, 0:1], ACT.Ln).then_inc(pick_ln, 1)

            def hi_part(n, o, src, **kw):
                act.wait_ge(prep_mm, n + 1)
                return sc.activation(o, src, ACT.Copy, **kw)

            n = 0
            act.wait_ge(ld_a, 64)
            for eo in range(DC):
                act.wait_ge(prep_mm, n + 1)
                sc.activation(gate[:, eo, :], bank[n % PREP_BANKS][:, 0:B * KEYS], ACT.Identity,
                              bias=bg[:, eo:eo + 1]).then_inc(prep_hi, 1)
                n += 1
            for eo in range(DC):
                act.wait_ge(prep_hi, eo + 1)
                sc.activation(gate_hi[:, :, eo, 0:KEYS], gate[:, eo, :].rearrange("p (b k) -> p b k", b=B),
                              ACT.Copy).then_inc(k_gate, 1)
            for b in range(B):
                act.wait_ge(cwo_ok, b + 1)
                sc.activation(cwo_hi[:, b, :], cwo[:, :], ACT.Copy).then_inc(prep_hi, 1)
                n += 1
            for p in range(PAIRS):
                hi_part(n, kT[:, p, :], bank[n % PREP_BANKS][:, 0:B * KEYS]).then_inc(prep_hi, 1)
                n += 1
            for hh in range(H):
                for io in range(DC):
                    hi_part(n, m_hi[:, :, io, hh * KEYS:(hh + 1) * KEYS],
                            bank[n % PREP_BANKS][:, 0:B * KEYS].rearrange("p (b k) -> p b k", b=B),
                            scale=HD ** -0.5).then_inc(prep_hi, 1)
                    n += 1
            for p in range(PAIRS):
                hi_part(n, vT[:, p, :, :].rearrange("p b k -> p (b k)"), bank[n % PREP_BANKS][:, 0:B * KEYS]).then_inc(prep_hi, 1)
                n += 1
            act.wait_ge(ld_sel, 32)
            sc.activation(wsel_hi[:, :, :], wsel[:, :, :], ACT.Copy).then_inc(sel_hi, 1)

            def take_hi(T_sem, bank_, dst, done, free, g, q, w):
                act.wait_ge(T_sem, g + 1)
                if free is not None:
                    wait(act, free, g - 1)
                sc.activation(dst[:, q, :, :].rearrange("p c n -> p (c n)"), bank_[:, 0:w], ACT.Copy).then_inc(done, 1)

            def normed(src, rs, sh, dst, ready, free, done, g, q):
                act.wait_ge(ready, g + 1)
                wait(act, free, g - 1)
                sc.activation(dst[:, q, :], src, ACT.Identity, scale=rs[:, q, :], bias=sh[:, q, :]).then_inc(done, 1)

            def step_a(t, par, live):
                if live(7):
                    normed(block(xs, t - 7), rstd2, shift2, xn2, f_shift, f_T, f_xn, t - 7, (par + 1) % 2)
                if live(1):
                    normed(block(xs, t - 1), rstd, shift, xn, a_shift, a_T, a_xn, t - 1, (par + 1) % 2)
                if live(3):
                    g, q = t - 3, (par + 1) % 2
                    act.wait_ge(a_nmax, g + 1)
                    wait(act, a_eT, g - 1)
                    wait(act, a_rden, g - 1)
                    sc.activation(e0[:, q, :], bank[1][:, 0:KEYS], ACT.Exp, bias=nmax0[:, q, :],
                                  accum_out=den0[:, q, :]).then_inc(a_exp, 1)
                if live(7):
                    take_hi(f_T, bank[(4, 7)[(par + 1) % 2]], x2T_hi, f_Thi, f_mm, t - 7, (par + 1) % 2, D)
                if live(1):
                    take_hi(a_T, bank[(0, 6)[(par + 1) % 2]], xT_hi, a_Thi, a_sc, t - 1, (par + 1) % 2, D)
                if live(3):
                    g, q = t - 3, (par + 1) % 2
                    act.wait_ge(a_eT, g + 1)
                    wait(act, a_pv, g - 1)
                    sc.activation(e0T_hi[:, q, :], bank[2][0:KEYS, 0:P], ACT.Copy).then_inc(a_eThi, 1)

            pipeline(act, step_a, 9, lead=1)
            act.drain().then_inc(phase, 1)
            act.wait_ge(phase, 4)

            def value_hi(b):
                for j in range(NCH):
                    act.wait_ge(vw_mm, NCH * b + j + 1)
                    if j == 0:
                        wait(act, b_pv, BPB * b)
                    sc.activation(vwo_hi[:, j, :], bank[4 + j % 3][:, 0:D], ACT.Copy).then_inc(vw_hi, 1)

            def exp_group(g, q, i):
                h0, h1 = HEAD_GROUPS[i]
                act.wait_ge(b_nmax, 3 * g + i + 1)
                for hh in range(h0, h1):
                    last = sc.activation(e[:, q, hh * KEYS:(hh + 1) * KEYS], bank[1 + i][:, (hh - h0) * KEYS:(hh - h0 + 1) * KEYS],
                                         ACT.Exp, bias=nmax[:, q, hh:hh + 1], accum_out=den[:, q, hh:hh + 1])
                last.then_inc(b_exp, 1)

            def step_b(t, par, live):
                if live(5):
                    normed(block(xs, t - 5), rstd3, shift3, xn3, n_shift, n_amax, n_xn, t - 5, (par + 1) % 2)
                if live(3):
                    g = t - 3
                    wait(act, b_pv, g)
                    for i, (j0, j1) in enumerate(T_GROUPS):
                        act.wait_ge(b_pT, 3 * g + i + 1)
                        sc.activation(pT_hi[:, j0:j1, :].rearrange("p c n -> p (c n)"), bank[4 + i][:, 0:(j1 - j0) * P],
                                      ACT.Copy).then_inc(b_pThi, 1)
                if live(2):
                    wait(act, b_pT, 3 * (t - 3))
                    exp_group(t - 2, par, 0)
                    exp_group(t - 2, par, 1)
                if live(1):
                    wait(act, b_sc, 3 * (t - 2))
                    take_hi(b_T, bank[0], xT_hi, b_Thi, None, t - 1, (par + 1) % 2, D)
                if live(2):
                    exp_group(t - 2, par, 2)

            stage_b(act, step_b, value_hi)
            act.drain().then_inc(phase, 1)
            act.wait_ge(phase, 8)

            def step_c(t, par, live):
                if live(0):
                    g, q = t, par
                    wait(act, c_T, g - 1)
                    sc.activation(q_t[:, q, :], block(xs, g), ACT.Identity, scale=a_all[:, bass.ds(g, 1)],
                                  bias=b_all[:, bass.ds(g, 1)]).then_inc(c_qt, 1)
                if live(2):
                    g, q = t - 2, par
                    act.wait_ge(c_scales, 2 * g + 2)
                    wait(act, c_h, 2 * (g - 1))
                    for half in range(2):
                        act.wait_ge(c_gu, 4 * g + 2 * half + 1)
                        sc.activation(silu[:, q, half * BANK:(half + 1) * BANK], bank[1 + 2 * half][:, :], ACT.Silu,
                                      scale=s_gate[:, slot4(t, 2), :]).then_inc(c_silu, 1)
                if live(4):
                    g, q = t - 4, par
                    wait(act, c_dn, g - 1)
                    act.wait_ge(c_hT, g + 1)
                    sc.activation(hqT[:, q, :, :].rearrange("p c n -> p (c n)"), bank[5 + q][:, :].bitcast(F16),
                                  ACT.Copy, bias=-OFFSET_16).then_inc(c_hqT, 1)
                if live(0):
                    g, q = t, par
                    if isinstance(g, int) and g == 0:
                        act.wait_ge(w_ready, 1)
                    wait(act, c_sh, g - 3)
                    for s_, w in ((s_gate, 0), (s_up, 1)):
                        sc.activation(s_[:, slot4(t, 0), :], c1_all[:, bass.ds(g, 1)], ACT.Copy,
                                      scale=w_mean[:, w:w + 1]).then_inc(c_scales, 1)
                if live(3):
                    g, q = t - 3, (par + 1) % 2
                    act.wait_ge(c_c2, g + 1)
                    wait(act, c_y, g - 3)
                    sc.activation(s_y[:, slot4(t, 3), :], c2[:, q, :], ACT.Copy, scale=w_mean[:, 3:4]).then_inc(c_sy, 1)

            pipeline4(act, step_c, 6)

        @blk.vector
        def _(dve):
            v = nc.vector
            seq = [0]

            def chain(ins):
                seq[0] += 1
                ins.then_inc(dve_seq, 1)
                dve.wait_ge(dve_seq, seq[0])

            dve.wait_ge(ld_c, 16)
            v.tensor_scalar(nonzero[:, :, :], cT[:, :, :], 0.0, None, ALU.not_equal).then_inc(nz_ok, 1)
            v.memset(gate_hi[:, :, :, KEYS:KEYS + 1].bitcast(F32), 0.0)
            v.memset(gate_lo[:, :, :, KEYS:KEYS + 1].bitcast(F32), 0.0)
            dve.wait_ge(ld_pick, 32)
            chain(v.tensor_reduce(pick[:, 5, 0:1], logit[:, :], axis=AX, op=ALU.max))
            v.tensor_scalar(pick[:, 2, :], logit[:, :], pick[:, 5, 0:1], None, ALU.subtract).then_inc(pick_z, 1)
            dve.wait_ge(pick_ln, 4)
            chain(v.tensor_scalar(pick[:, 6, :], pick[:, 2, :], pick[:, 4, 1:2], None, ALU.subtract))
            chain(v.tensor_tensor(pick[:, 6, :], pick[:, 6, :], pick[:, 1, :], ALU.subtract))
            chain(v.max(pick[:, 7, :], pick[:, 6, :]))
            v.max_index(picked[:, :], pick[:, 7, :], pick[:, 6, :]).then_inc(picked_ok, 1)
            dve.wait_ge(cnt_ok, 1)
            v.tensor_scalar(mask_row[:, :, :].rearrange("p b k -> p (b k)"), bank[7][0:1, 0:B * KEYS], 0.0, MASKED,
                            ALU.is_equal, ALU.mult).then_inc(mask_ok, 1)

            n = 0
            for eo in range(DC):
                dve.wait_ge(k_gate, eo + 1)
                v.tensor_tensor(gate_lo[:, :, eo, 0:KEYS], gate[:, eo, :].rearrange("p (b k) -> p b k", b=B),
                                gate_hi[:, :, eo, 0:KEYS].bitcast(F32), ALU.subtract).then_inc(prep_lo, 1)
                n += 1
            dve.wait_ge(ld_a, 64)
            for b in range(B):
                dve.wait_ge(prep_mm, n + 1)
                v.tensor_tensor(cwo[:, :], bank[n % PREP_BANKS][0:KEYS, 0:D], bo[:, :], ALU.add).then_inc(cwo_ok, 1)
                dve.wait_ge(cwo_ok, b + 1)
                dve.wait_ge(prep_hi, n + 1)
                v.tensor_tensor(cwo_lo[:, b, :], cwo[:, :], cwo_hi[:, b, :].bitcast(F32), ALU.subtract).then_inc(prep_lo, 1)
                dve.wait_ge(prep_lo, n + 1)
                n += 1
            n += PAIRS
            for hh in range(H):
                for io in range(DC):
                    dve.wait_ge(prep_hi, n + 1)
                    v.scalar_tensor_tensor(out=m_lo[:, :, io, hh * KEYS:(hh + 1) * KEYS],
                                           in0=bank[n % PREP_BANKS][:, 0:B * KEYS].rearrange("p (b k) -> p b k", b=B),
                                           scalar=HD ** -0.5, in1=m_hi[:, :, io, hh * KEYS:(hh + 1) * KEYS].bitcast(F32),
                                           op0=ALU.mult, op1=ALU.subtract).then_inc(prep_lo, 1)
                    n += 1
            dve.wait_ge(sel_hi, 1)
            v.tensor_tensor(wsel_lo[:, :, :], wsel[:, :, :], wsel_hi[:, :, :].bitcast(F32), ALU.subtract).then_inc(sel_hi, 1)

            def normed(dst, src, mv, rs, rstd_sem, T_sem, done, g, q):
                dve.wait_ge(rstd_sem, g + 1)
                wait(dve, T_sem, g - 1)
                return v.tensor_scalar(dst[:, q, :], src, mv[:, q, 0:1], rs[:, q, :], ALU.subtract, ALU.mult).then_inc(done, 1)

            def take_lo(hi_sem, bank_, hi, lo, done, g, q):
                dve.wait_ge(hi_sem, g + 1)
                v.tensor_tensor(lo[:, q, :, :].rearrange("p c n -> p (c n)"), bank_[:, 0:D],
                                hi[:, q, :, :].rearrange("p c n -> p (c n)").bitcast(F32), ALU.subtract).then_inc(done, 1)

            def step_a(t, par, live):
                if live(3):
                    g, q = t - 3, (par + 1) % 2
                    dve.wait_ge(a_sc, g + 1)
                    wait(dve, a_exp, g - 1)
                    v.tensor_reduce(nmax0[:, q, :], bank[1][:, 0:KEYS], axis=AX, op=ALU.max, negate=True).then_inc(a_nmax, 1)
                if live(4):
                    g, q = t - 4, par
                    dve.wait_ge(a_eThi, g + 1)
                    wait(dve, a_pv, g - 1)
                    v.tensor_tensor(e0T_lo[:, q, :], bank[2][0:KEYS, 0:P], e0T_hi[:, q, :].bitcast(F32),
                                    ALU.subtract).then_inc(a_eTlo, 1)
                if live(9):
                    g = t - 9
                    dve.wait_ge(f_mm, g + 1)
                    dve.wait_ge(f_bias, g + 1)
                    v.tensor_tensor(block(xs, g), bank[5][:, 0:D], block(xs, g), ALU.add).then_inc(f_x2, 1)
                if live(8):
                    g, q = t - 8, par
                    wait(dve, f_mm, g - 1)
                    take_lo(f_Thi, bank[(4, 7)[q]], x2T_hi, x2T_lo, f_Tlo, g, q)
                if live(5):
                    g, q = t - 5, (par + 1) % 2
                    dve.wait_ge(a_pv, g + 1)
                    dve.wait_ge(a_rden, g + 1)
                    v.scalar_tensor_tensor(out=block(xs, g), in0=bank[3][:, 0:D], scalar=rden0[:, q, :], in1=block(xs, g),
                                           op0=ALU.mult, op1=ALU.add).then_inc(f_x1, 1)
                if live(2):
                    g, q = t - 2, par
                    wait(dve, a_sc, g - 1)
                    take_lo(a_Thi, bank[(0, 6)[q]], xT_hi, xT_lo, a_Tlo, g, q)
                if live(5):
                    g, q = t - 5, (par + 1) % 2
                    wait_apart(dve, (f_x1, g + 1))
                    v.bn_stats(stats2[:, q, :], block(xs, g)).then_inc(f_stats, 1)
                if live(-1):
                    g, q = t + 1, (par + 1) % 2
                    if isinstance(g, int) and g in (0, BPB):
                        for b in (0,) if g == 0 else range(1, B):
                            dve.wait_ge(ld_x[b], 16)
                    v.bn_stats(stats[:, q, :], block(xs, g)).then_inc(a_stats, 1)
                if live(5):
                    g, q = t - 5, (par + 1) % 2
                    wait_apart(dve, (f_stats, g + 1), (f_shift, g - 1))
                    v.bn_aggr(meanvar2[:, q, :], stats2[:, q, :]).then_inc(f_mv, 1)
                if live(-1):
                    g, q = t + 1, (par + 1) % 2
                    wait_apart(dve, (a_stats, g + 1), (a_shift, g - 1))
                    v.bn_aggr(meanvar[:, q, :], stats[:, q, :]).then_inc(a_mv, 1)
                if live(4):
                    g, q = t - 4, par
                    dve.wait_ge(a_exp, g + 1)
                    wait(dve, f_x1, g - 1)
                    v.reciprocal(rden0[:, q, :], den0[:, q, :]).then_inc(a_rden, 1)

            pipeline(dve, step_a, 9, lead=1)
            dve.drain().then_inc(phase, 1)
            dve.wait_ge(phase, 4)

            def value_lo(b):
                for j in range(NCH):
                    if j == 0:
                        wait(dve, b_pv, BPB * b)
                    dve.wait_ge(vw_hi, NCH * b + j + 1)
                    v.tensor_tensor(vwo_lo[:, j, :], bank[4 + j % 3][:, 0:D], vwo_hi[:, j, :].bitcast(F32),
                                    ALU.subtract).then_inc(vw_lo, 1)

            names = ("g", "u", "d")

            def weights(t):
                i = t - (T_SUM - 3)
                if 0 <= i < 3:
                    if i == 0:
                        dve.wait_ge(ld_ffn, 48)
                    v.tensor_reduce(abs_sum[:, i:i + 1], raw[names[i]][:, :], axis=AX, op=ALU.add, apply_absolute_value=True)
                    if i == 2:
                        v.memset(abs_sum[:, 3:4], 1.0).then_inc(w_abs, 1)
                i = t - (T_SUM + 1)
                if 0 <= i < 3:
                    if i == 0:
                        dve.wait_ge(w_summed, 1)
                        chain(v.tensor_scalar(w_mean[:, :], w_sum[:, :], 1.0 / (D * INNER), CLIP, ALU.mult, ALU.max))
                        chain(v.reciprocal(w_inv[:, :], w_mean[:, :]))
                        chain(v.tensor_scalar(w_mean[:, 3:4], w_mean[:, 2:3], 1.0 / QMAX, None, ALU.mult))
                    chain(v.tensor_scalar(wtmp[:, :], raw[names[i]][:, :], w_inv[:, i:i + 1], MAGIC, ALU.mult, ALU.add))
                    chain(v.tensor_scalar(wtmp_b[:, :], wtmp[:, :], MAGIC, 1.0, ALU.subtract, ALU.min))
                    v.tensor_scalar(wq_b[names[i]][:, :], wtmp_b[:, :], -1.0, None, ALU.max).then_inc(w_ready, 1)

            def head_max(g, q, i):
                h0, h1 = HEAD_GROUPS[i]
                dve.wait_ge(b_sc, 3 * g + i + 1)
                v.tensor_reduce(nmax[:, q, h0:h1], bank[1 + i][:, 0:(h1 - h0) * KEYS].rearrange("p (h k) -> p h k", k=KEYS),
                                axis=AX, op=ALU.max, negate=True).then_inc(b_nmax, 1)

            def head_reciprocal(g, q, i):
                h0, h1 = HEAD_GROUPS[i]
                dve.wait_ge(b_exp, 3 * g + i + 1)
                v.reciprocal(rden[:, q, h0:h1], den[:, q, h0:h1]).then_inc(b_rden, 1)

            def step_b(t, par, live):
                g2, q2 = t - 2, par
                if live(5):
                    g, q = t - 5, (par + 1) % 2
                    dve.wait_ge(n_xn, g + 1)
                    v.tensor_reduce(amax[:, q, :], xn3[:, q, :], axis=AX, op=ALU.max, apply_absolute_value=True).then_inc(n_amax, 1)
                if live(2):
                    wait(dve, b_exp, 3 * (g2 - 1))
                    head_max(g2, q2, 0)
                if live(5):
                    g, q = t - 5, (par + 1) % 2
                    dve.wait_ge(n_amax, g + 1)
                    v.tensor_scalar(c1_all[:, bass.ds(g, 1)], amax[:, q, :], 1.0 / QMAX, CLIP / QMAX, ALU.mult, ALU.max).then_inc(n_c1, 1)
                if live(3):
                    g = t - 3
                    wait(dve, b_pv, g)
                    for i, (j0, j1) in enumerate(T_GROUPS):
                        dve.wait_ge(b_pThi, 3 * g + i + 1)
                        v.tensor_tensor(pT_lo[:, j0:j1, :].rearrange("p c n -> p (c n)"), bank[4 + i][:, 0:(j1 - j0) * P],
                                        pT_hi[:, j0:j1, :].rearrange("p c n -> p (c n)").bitcast(F32),
                                        ALU.subtract).then_inc(b_pTlo, 1)
                if live(5):
                    g, q = t - 5, (par + 1) % 2
                    wait_apart(dve, (n_c1, g + 1))
                    v.reciprocal(r1[:, q, :], c1_all[:, bass.ds(g, 1)]).then_inc(n_r1, 1)
                if live(0):
                    v.bn_stats(stats[:, par, :], block(xs, t)).then_inc(b_stats, 1)
                if live(4):
                    wait_apart(dve, (b_x3, t - 3))
                    v.bn_stats(stats3[:, par, :], block(xs, t - 4)).then_inc(n_stats, 1)
                if live(2):
                    head_max(g2, q2, 1)
                if live(0):
                    wait_apart(dve, (b_stats, t + 1), (b_rstd, t - 1))
                    v.bn_aggr(meanvar[:, par, :], stats[:, par, :]).then_inc(b_mv, 1)
                if live(2):
                    head_max(g2, q2, 2)
                if live(4):
                    wait_apart(dve, (n_stats, t - 3), (n_shift, t - 5))
                    v.bn_aggr(meanvar3[:, par, :], stats3[:, par, :]).then_inc(n_mv, 1)
                if live(2):
                    wait(dve, b_norm, 3 * (g2 - 1))
                    head_reciprocal(g2, q2, 0)
                if live(5):
                    g, q = t - 5, (par + 1) % 2
                    dve.wait_ge(n_r1, g + 1)
                    v.tensor_tensor(a_all[:, bass.ds(g, 1)], rstd3[:, q, :], r1[:, q, :], ALU.mult)
                    v.tensor_tensor(b_all[:, bass.ds(g, 1)], shift3[:, q, :], r1[:, q, :], ALU.mult).then_inc(n_ab, 1)
                if live(2):
                    head_reciprocal(g2, q2, 1)
                if live(1):
                    g, q = t - 1, (par + 1) % 2
                    wait(dve, b_sc, 3 * (g - 1))
                    take_lo(b_Thi, bank[0], xT_hi, xT_lo, b_Tlo, g, q)
                if live(0):
                    normed(xn, block(xs, t), meanvar, rstd, b_rstd, b_T, b_xn, t, par)
                if live(2):
                    head_reciprocal(g2, q2, 2)
                if live(3):
                    g = t - 3
                    dve.wait_ge(b_pv, g + 1)
                    v.tensor_tensor(block(xs, g), bank[7][:, 0:D], block(xs, g), ALU.add).then_inc(b_x3, 1)
                if isinstance(t, int):
                    weights(t)

            stage_b(dve, step_b, value_lo)
            dve.drain().then_inc(phase, 1)
            dve.wait_ge(phase, 8)

            def step_c(t, par, live):
                if live(3):
                    g, q = t - 3, (par + 1) % 2
                    dve.wait_ge(c_hmax, g + 1)
                    dve.wait_ge(c_scales, 2 * g + 2)
                    wait(dve, c_sh, g - 1)
                    wait(dve, c_sy, g - 1)
                    v.tensor_scalar(c2[:, q, :], hmax[:, q, :], s_up[:, slot4(t, 3), :], CLIP, ALU.mult, ALU.max).then_inc(c_c2, 1)
                if live(1):
                    g, q = t - 1, (par + 1) % 2
                    dve.wait_ge(c_T, g + 1)
                    wait(dve, c_gu, 4 * (g - 1))
                    v.tensor_scalar(qT[:, q, :, :].rearrange("p c n -> p (c n)"), bank[0][:, 0:D], MAGIC, MAGIC,
                                    ALU.add, ALU.subtract).then_inc(c_qT, 1)
                if live(3):
                    g, q = t - 3, (par + 1) % 2
                    dve.wait_ge(c_c2, g + 1)
                    v.reciprocal(r2[:, q, :], c2[:, q, :]).then_inc(c_r2, 1)
                if live(6):
                    g, q = t - 6, par
                    dve.wait_ge(c_dn, g + 1)
                    dve.wait_ge(c_sy, g + 1)
                    if not isinstance(g, int) or g >= 2:
                        dve.wait_ge(st_out[q], 8 * (g - q))
                    v.scalar_tensor_tensor(out=y[:, q, :], in0=bank[7][:, 0:D], scalar=s_y[:, slot4(t, 6), :], in1=block(xs, g),
                                           op0=ALU.mult, op1=ALU.add).then_inc(c_y, 1)
                if live(2):
                    g, q = t - 2, par
                    wait(dve, c_hqf, g - 1)
                    for half in range(2):
                        cols = slice(half * BANK, (half + 1) * BANK)
                        dve.wait_ge(c_gu, 4 * g + 2 * half + 2)
                        dve.wait_ge(c_silu, 2 * g + half + 1)
                        v.tensor_tensor(h[:, q, cols], bank[2 + 2 * half][:, :], silu[:, q, cols], ALU.mult).then_inc(c_h, 1)
                    dve.wait_ge(c_h, 2 * g + 2)
                    v.tensor_reduce(hmax[:, q, :], h[:, q, :], axis=AX, op=ALU.max, apply_absolute_value=True).then_inc(c_hmax, 1)

            pipeline4(dve, step_c, 6)


def kernel(**inputs):
    import numpy as np
    import concourse.bacc as bacc
    from concourse.bass_utils import run_bass_kernel_spmd

    def arr(name):
        return np.asarray(inputs[name])

    def head_major(w):
        return w.reshape(D, HD, H).transpose(0, 2, 1).reshape(D, H * HD)

    layout = {
        "x": arr("x"),
        "cT": arr("ctx_1024").reshape(B * KEYS, D).T,
        "a_wg": arr("L0_xattn_Wg"), "a_bg": arr("L0_xattn_bg"), "a_wo": arr("L0_xattn_Wo"), "a_bo": arr("L0_xattn_bo"),
        "f_w": arr("L0_ffn_W"), "f_b": arr("L0_ffn_b"), "f_logits": arr("L0_ffn_logits"), "f_u": arr("L0_ffn_u"),
        "b_wqT": arr("L1_xattn_Wq").T, "b_wk": head_major(arr("L1_xattn_Wk")), "b_wv": head_major(arr("L1_xattn_Wv")),
        "b_wo": arr("L1_xattn_Wo"),
        "w_gateT": arr("L1_ffn_w_gate").T, "w_upT": arr("L1_ffn_w_up").T, "w_downT": arr("L1_ffn_w_down").T,
    }
    arrays = {"in_" + n: np.ascontiguousarray(a) for n, a in layout.items()}
    nc = bacc.Bacc("TRN2", target_bir_lowering=False, num_devices=1)
    aps = [nc.dram_tensor(n, a.shape, F32, kind="ExternalInput").ap() for n, a in arrays.items()]
    out = nc.dram_tensor("out_0", (B, S, D), F32, kind="ExternalOutput").ap()
    build(nc, *aps, out)
    return run_bass_kernel_spmd(nc, [arrays], core_ids=[0]).results[0]["out_0"]
```

```python
from contextlib import ExitStack

import concourse.bass as bass
from concourse import mybir

F32 = mybir.dt.float32
F32R = mybir.dt.float32r
BF16 = mybir.dt.bfloat16
F16 = mybir.dt.float16
U32 = mybir.dt.uint32
ALU = mybir.AluOpType
ACT = mybir.ActivationFunctionType
AX = mybir.AxisListType.X

P = 128
B, S, D = 4, 1024, 256
DC = D // P
NB = B * S // P
BPB = S // P
KEYS = 77
H, HD = 16, 64
HK = H * KEYS
NCH = -(-HK // P)
PAIRS = H // 2
BANK = 512
HEAD_GROUPS = ((0, 6), (6, 12), (12, 16))
T_GROUPS = ((0, 4), (4, 8), (8, 10))
OPS = 8
INNER = 1024
IC = INNER // P
EPS = 1e-5
MASKED = -3.0e38
MAGIC = 1.5 * 2.0 ** 23
OFFSET_16 = 1536.0
MAGIC_16 = 2.0 ** 23 + (0x6400 + OFFSET_16 - 1024)
QMAX = 127.0
CLIP = 1e-5
PADV = P - 1


def wait(eng, sem, count):
    if not (isinstance(count, int) and count <= 0):
        eng.wait_ge(sem, count)


def overlaps(j):
    return [p for p in range(PAIRS) if 2 * KEYS * p < P * (j + 1) and 2 * KEYS * (p + 1) > P * j]


def build(nc, x, cT_in, a_wg, a_bg, a_wo, a_bo, f_w, f_b, f_logits, f_u,
          b_wqT, b_wk, b_wv, b_wo, w_gateT, w_upT, w_downT, out):
    ctx = ExitStack()
    with ctx:
        def sem(name):
            return ctx.enter_context(nc.semaphore(name))

        def alloc(stack, name, shape, dt=F32):
            return stack.enter_context(nc.sbuf_tensor(name, shape, dt))

        with ExitStack() as early:
            alloc(early, "x_first", [P, BPB, D])
            cT_hi = alloc(early, "cT_hi", [P, DC, B * KEYS], F32R)
            cT_lo = alloc(early, "cT_lo", [P, DC, B * KEYS], F32R)
            wqT_hi = alloc(early, "wqT_hi", [P, PAIRS, D], F32R)
            kT_hi = alloc(early, "kT_hi", [P, PAIRS, B * KEYS], F32R)
        xs = alloc(ctx, "xs", [P, NB, D])
        ident = alloc(ctx, "ident", [P, P])
        ident_h = alloc(ctx, "ident_h", [P, P], F16)
        mhalf = alloc(ctx, "mhalf", [P, 1])
        ones_b = alloc(ctx, "ones_b", [P, P], BF16)
        ones = alloc(ctx, "ones", [P, P])
        stats = alloc(ctx, "stats", [P, 2, 6])
        meanvar = alloc(ctx, "meanvar", [P, 2, 2])
        var_eps = alloc(ctx, "var_eps", [P, 2, 1])
        rstd = alloc(ctx, "rstd", [P, 2, 1])
        shift = alloc(ctx, "shift", [P, 2, 1])
        xn = alloc(ctx, "xn", [P, 2, D])
        xT_hi = alloc(ctx, "xT_hi", [P, 2, DC, P], F32R)
        xT_lo = alloc(ctx, "xT_lo", [P, 2, DC, P], F32R)

        c1_all = alloc(ctx, "c1_all", [P, NB])
        a_all = alloc(ctx, "a_all", [P, NB])
        b_all = alloc(ctx, "b_all", [P, NB])
        abs_sum = alloc(ctx, "abs_sum", [P, 4])
        w_sum = alloc(ctx, "w_sum", [P, 4])
        w_mean = alloc(ctx, "w_mean", [P, 4])
        w_inv = alloc(ctx, "w_inv", [P, 4])

        with ExitStack() as ffn:
            raw = {n: alloc(ffn, f"raw_{n}", [P, 2 * INNER]) for n in ("g", "u", "d")}
            wtmp = alloc(ffn, "wtmp", [P, INNER])
            wtmp_b = alloc(ffn, "wtmp_b", [P, INNER], BF16)
            wq_b = {n: alloc(ffn, f"wq_{n}", [P, 2 * INNER], BF16) for n in ("g", "u", "d")}
        M_BYTES = 2 * DC * HK * 4
        FFN_BYTES = 3 * 2 * INNER * (4 + 2) + INNER * 6
        assert 3 * 2 * INNER * 4 <= (B - 2) * M_BYTES and FFN_BYTES <= (B - 1) * M_BYTES

        ab = ExitStack()
        with ExitStack() as early:
            wk_hi = alloc(early, "wk_hi", [P, DC, H * HD], F32R)
            wv_hi = alloc(early, "wv_hi", [P, DC, H * HD], F32R)
        m_all = alloc(ab, "m_all", [P, B, 2, DC, HK], F32R)
        m_hi, m_lo = m_all[:, :, 0], m_all[:, :, 1]
        vT = alloc(ab, "vT", [P, PAIRS, B, KEYS])
        wo1 = alloc(ab, "wo1", [P, PAIRS, D])
        mask_row = alloc(ab, "mask_row", [1, B, KEYS], BF16)

        before = ExitStack()
        with ExitStack() as whole:
            wv = alloc(whole, "wv", [P, DC, H * HD])
        wv_lo = alloc(before, "wv_lo", [P, DC, H * HD], F32R)
        wg0 = alloc(before, "wg0", [P, DC, D])
        wo0 = alloc(before, "wo0", [P, DC, D])
        nonzero = alloc(before, "nonzero", [P, DC, B * KEYS], BF16)
        with ExitStack() as whole:
            wqT = alloc(whole, "wqT", [P, PAIRS, D])
        wqT_lo = alloc(before, "wqT_lo", [P, PAIRS, D], F32R)
        kT_lo = alloc(before, "kT_lo", [P, PAIRS, B * KEYS], F32R)
        bg = alloc(before, "bg", [P, DC])
        bo = alloc(before, "bo", [KEYS, D])
        gate = alloc(before, "gate", [P, DC, B * KEYS])
        cT = alloc(before, "cT", [P, DC, B * KEYS])
        before.close()

        values = ExitStack()
        pair_vT = alloc(values, "pair_vT", [P, PAIRS, 2 * KEYS + 2 * PADV])
        vwo_hi = alloc(values, "vwo_hi", [P, NCH, D], F32R)
        vwo_lo = alloc(values, "vwo_lo", [P, NCH, D], F32R)
        prep_bytes = sum(-(-n * 4 // 64) * 64 for n in (PAIRS * D, PAIRS * B * KEYS, DC * H * HD, DC * D, DC * D, DC, D,
                                                        DC * B * KEYS // 2, DC * B * KEYS, DC * B * KEYS))
        value_bytes = 4 * (PAIRS * (2 * KEYS + 2 * PADV) + 2 * NCH * D)
        if prep_bytes > value_bytes:
            alloc(values, "after_values", [P, -(-(prep_bytes - value_bytes) // 4)])

        pa = ExitStack()
        cwo = alloc(pa, "cwo", [KEYS, D])
        gate_hi = alloc(pa, "gate_hi", [P, B, DC, KEYS + 1], F32R)
        gate_lo = alloc(pa, "gate_lo", [P, B, DC, KEYS + 1], F32R)
        cwo_hi = alloc(pa, "cwo_hi", [KEYS, B, D], F32R)
        cwo_lo = alloc(pa, "cwo_lo", [KEYS, B, D], F32R)
        logit = alloc(pa, "logit", [1, OPS])
        uni = alloc(pa, "uni", [1, OPS])
        pick = alloc(pa, "pick", [1, 8, OPS])
        picked = alloc(pa, "picked", [1, OPS], U32)
        wsel = alloc(pa, "wsel", [P, DC, D])
        wsel_hi = alloc(pa, "wsel_hi", [P, DC, D], F32R)
        wsel_lo = alloc(pa, "wsel_lo", [P, DC, D], F32R)
        bsel = alloc(pa, "bsel", [P, D])
        with ExitStack() as key_weights:
            wk = alloc(key_weights, "wk", [P, DC, H * HD])
        with ExitStack() as key_weights:
            wk_lo = alloc(key_weights, "wk_lo", [P, DC, H * HD], F32R)
        stats2 = alloc(pa, "stats2", [P, 2, 6])
        meanvar2 = alloc(pa, "meanvar2", [P, 2, 2])
        var_eps2 = alloc(pa, "var_eps2", [P, 2, 1])
        rstd2 = alloc(pa, "rstd2", [P, 2, 1])
        shift2 = alloc(pa, "shift2", [P, 2, 1])
        xn2 = alloc(pa, "xn2", [P, 2, D])
        x2T_hi = alloc(pa, "x2T_hi", [P, 2, DC, P], F32R)
        x2T_lo = alloc(pa, "x2T_lo", [P, 2, DC, P], F32R)
        nmax0 = alloc(pa, "nmax0", [P, 2, 1])
        den0 = alloc(pa, "den0", [P, 2, 1])
        rden0 = alloc(pa, "rden0", [P, 2, 1])
        e0 = alloc(pa, "e0", [P, 2, KEYS])
        e0T_hi = alloc(pa, "e0T_hi", [KEYS, 2, P], F32R)
        e0T_lo = alloc(pa, "e0T_lo", [KEYS, 2, P], F32R)
        pa.close()

        pb = ExitStack()
        e = alloc(pb, "e", [P, 2, NCH * P])
        nmax = alloc(pb, "nmax", [P, 2, H])
        den = alloc(pb, "den", [P, 2, H])
        rden = alloc(pb, "rden", [P, 2, H])
        pT_hi = alloc(pb, "pT_hi", [P, NCH, P], F32R)
        pT_lo = alloc(pb, "pT_lo", [P, NCH, P], F32R)
        stats3 = alloc(pb, "stats3", [P, 2, 6])
        meanvar3 = alloc(pb, "meanvar3", [P, 2, 2])
        var_eps3 = alloc(pb, "var_eps3", [P, 2, 1])
        rstd3 = alloc(pb, "rstd3", [P, 2, 1])
        shift3 = alloc(pb, "shift3", [P, 2, 1])
        xn3 = alloc(pb, "xn3", [P, 2, D])
        amax = alloc(pb, "amax", [P, 2, 1])
        r1 = alloc(pb, "r1", [P, 2, 1])
        pb.close()
        values.close()
        ab.close()

        alloc(ctx, "below", [P, FFN_BYTES // 4])
        q_t = alloc(ctx, "q_t", [P, 2, D])
        qT = alloc(ctx, "qT", [P, 2, DC, P], BF16)
        s_gate = alloc(ctx, "s_gate", [P, 4, 1])
        s_up = alloc(ctx, "s_up", [P, 4, 1])
        silu = alloc(ctx, "silu", [P, 2, INNER])
        h = alloc(ctx, "h", [P, 2, INNER])
        hmax = alloc(ctx, "hmax", [P, 2, 1])
        c2 = alloc(ctx, "c2", [P, 2, 1])
        r2 = alloc(ctx, "r2", [P, 2, 1])
        s_h = alloc(ctx, "s_h", [P, 2, 2])
        s_y = alloc(ctx, "s_y", [P, 4, 1])
        hq_f = alloc(ctx, "hq_f", [P, 2, INNER])
        hqT = alloc(ctx, "hqT", [P, 2, IC, P], BF16)
        y = alloc(ctx, "y", [P, 2, D])

        bank = [ctx.enter_context(nc.psum_tensor(f"bank{i}", [P, BANK], F32)) for i in range(8)]

        split_hi, split_lo, ld_c, ld_a, ld_pick, ld_k, ld_q, ld_v, ld_wo, ld_sel, ld_ffn = (
            sem(n) for n in ("split_hi", "split_lo", "ld_c", "ld_a", "ld_pick", "ld_k", "ld_q", "ld_v", "ld_wo", "ld_sel", "ld_ffn"))
        st_out = [sem("st_even"), sem("st_odd")]
        ld_x = [sem(f"ld_x{b}") for b in range(B)]
        consts, dve_seq, picked_ok, pick_ln, pick_z = (sem(n) for n in ("consts", "dve_seq", "picked_ok", "pick_ln", "pick_z"))
        nz_ok, cnt_ok, mask_ok, k_gate, cwo_ok = (sem(n) for n in ("nz_ok", "cnt_ok", "mask_ok", "k_gate", "cwo_ok"))
        prep_mm, prep_hi, prep_lo, sel_hi = (sem(n) for n in ("prep_mm", "prep_hi", "prep_lo", "sel_hi"))
        a_stats, a_mv, a_eps, a_rstd, a_xn, a_T, a_Thi, a_Tlo, a_sc, a_nmax, a_exp, a_eT, a_eThi, a_eTlo, a_rden, a_pv = (
            sem("a_" + n) for n in ("stats", "mv", "eps", "rstd", "xn", "T", "Thi", "Tlo", "sc", "nmax", "exp", "eT",
                                    "eThi", "eTlo", "rden", "pv"))
        a_shift, f_shift = sem("a_shift"), sem("f_shift")
        f_x1, f_stats, f_mv, f_eps, f_rstd, f_xn, f_bias, f_T, f_Thi, f_Tlo, f_mm, f_x2 = (
            sem("f_" + n) for n in ("x1", "stats", "mv", "eps", "rstd", "xn", "bias", "T", "Thi", "Tlo", "mm", "x2"))
        b_stats, b_mv, b_eps, b_rstd, b_xn, b_T, b_Thi, b_Tlo, b_pv, b_x3 = (
            sem("b_" + n) for n in ("stats", "mv", "eps", "rstd", "xn", "T", "Thi", "Tlo", "pv", "x3"))
        n_stats, n_mv, n_eps, n_rstd, n_shift, n_xn, n_amax, n_c1, n_r1, n_ab = (
            sem("n_" + n) for n in ("stats", "mv", "eps", "rstd", "shift", "xn", "amax", "c1", "r1", "ab"))
        b_rden, b_norm = sem("b_rden"), sem("b_norm")
        b_sc, b_nmax, b_exp = sem("b_sc"), sem("b_nmax"), sem("b_exp")
        b_pT, b_pThi, b_pTlo = sem("b_pT"), sem("b_pThi"), sem("b_pTlo")
        e_pad, v_zero, v_pair, vw_mm, vw_hi, vw_lo = (sem(n) for n in ("e_pad", "v_zero", "v_pair", "vw_mm", "vw_hi", "vw_lo"))
        w_abs, w_summed, w_ready = sem("w_abs"), sem("w_summed"), sem("w_ready")
        c_scales, c_qt, c_T, c_qT, c_hmax, c_c2, c_r2, c_sy, c_sh, c_hqf, c_hT, c_hqT, c_dn, c_y = (
            sem("c_" + n) for n in ("scales", "qt", "T", "qT", "hmax", "c2", "r2", "sy", "sh", "hqf",
                                    "hT", "hqT", "dn", "y"))
        c_silu, c_h = sem("c_silu"), sem("c_h")
        c_gu = sem("c_gu")

        UNROLL = 4

        def pipeline(eng, step, depth, until, lead=0, first=0, last=NB):
            start = first + depth + 2
            count = (last - lead - start) // UNROLL * UNROLL
            for t in range(first - lead, start):
                step(t, t % 2, lambda k, t=t: first <= t - k < last)
            with eng.Fori(0, count // UNROLL) as i:
                for j in range(UNROLL):
                    step(i * UNROLL + start + j, (start + j) % 2, lambda k: True)
            for t in range(start + count, until):
                step(t, t % 2, lambda k, t=t: first <= t - k < last)

        def slot4(t, k):
            return slots4[(id4[0] - k) % 4]

        slots4, id4 = [0, 1, 2, 3], [0]

        A_END, B_END = NB + 9, NB + 5
        B_IN = {NB + 8: (0, 1, 2)}
        C_IN = {NB + 1: (0, 1), NB + 2: (2,), NB + 3: (3,), NB + 4: (4,)}
        B_READY, C_READY = 3, 5

        def live_at(t):
            return lambda k: 0 <= t - k < NB

        def wait_all(eng, needs):
            for sem_, count in needs:
                eng.wait_ge(sem_, count)

        def into_b(eng, step_a, step_b, before=None):
            for t in range(NB + 2, A_END):
                step_a(t, t % 2, live_at(t))
                for u in B_IN.get(t, ()):
                    if u == 0:
                        wait_all(eng, ((a_shift, NB), (a_T, NB), (a_Tlo, NB), (a_sc, NB), (a_exp, NB)))
                    if u == 2:
                        wait_all(eng, ((a_eTlo, NB), (a_pv, NB), (f_x1, NB)))
                        if before:
                            before()
                    step_b(u, u % 2, live_at(u))
            wait_all(eng, ((f_Tlo, NB), (f_mm, NB), (f_bias, NB), (f_x2, NB)))

        def into_c(eng, step_b, step_c):
            for t in range(NB + 1, B_END):
                step_b(t, t % 2, live_at(t))
                for u in C_IN[t]:
                    if u == 0:
                        wait_all(eng, ((b_sc, 3 * NB), (b_exp, 3 * NB), (b_Tlo, NB)))
                    if u == 2:
                        wait_all(eng, ((b_pTlo, 3 * NB), (b_x3, NB)))
                    id4[0] = u % 4
                    step_c(u, u % 2, live_at(u))

        first_of = [None]

        def stage_b(eng, step, at_batch, batches=range(1, B)):
            for t in range(B_READY, BPB + 3):
                if t == 3 and 0 in batches:
                    at_batch(0)
                step(t, t % 2, lambda k, t=t: t >= k)
            with eng.Fori(0, B - 2) as b:
                at_batch(b + 1)
                for j in range(BPB):
                    first_of[0] = b + 1 if j == 0 else None
                    step(b * BPB + BPB + 3 + j, (j + 1) % 2, lambda k: True)
            if B - 1 in batches:
                at_batch(B - 1)
            for t in range((B - 1) * BPB + 3, NB + 1):
                first_of[0] = B - 1 if t == (B - 1) * BPB + 3 else None
                step(t, t % 2, lambda k, t=t: t - k < NB)

        def pipeline4(eng, step, depth, last=NB):
            start = -(-depth // 4) * 4
            for t in range(C_READY, start):
                id4[0] = t % 4
                step(t, t % 2, lambda k, t=t: 0 <= t - k < last)
            with eng.Fori(0, (last - start) // 4) as n:
                t = n * 4 + start
                for i in range(4):
                    id4[0] = i
                    step(t + i, i % 2, lambda k: True)
            for t in range(last, last + depth):
                id4[0] = t % 4
                step(t, t % 2, lambda k, t=t: 0 <= t - k < last)

        def wait_apart(eng, *needs):
            counts = [(sem_, n if isinstance(n, int) else eng.compute_val(n)) for sem_, n in needs]
            eng.wait_ge(consts, 4)
            for sem_, n in counts:
                wait(eng, sem_, n)

        FIRST_VALUES = {-1: range(0, 2), 0: range(2, 4), 1: range(4, 6), 2: range(6, 8), 3: range(8, NCH)}

        T_SUM = (B - 1) * BPB + 6

        def batch_of(g):
            return g // BPB

        def block(tile, g):
            return tile[:, bass.ds(g, 1), :].rearrange("p o d -> p (o d)")

        N_GATE, N_CWO, N_K, N_V, N_M = DC, B, PAIRS, PAIRS, DC * H
        FIRST_CWO = N_GATE
        FIRST_K = FIRST_CWO + N_CWO
        FIRST_V = FIRST_K + N_K
        FIRST_M = FIRST_V + N_V
        N_PREP = FIRST_M + N_M

        def low_parts(n):
            return min(n, FIRST_V) + min(max(n - FIRST_M, 0), N_M)

        HALF_W, HALF_P = H * HD // 2, PAIRS // 2
        SPLITS = [(cT_hi[:, :, :], cT_lo[:, :, :], cT[:, :, :], ld_c)]
        SPLITS += [(hi_[:, :, i * HALF_W:(i + 1) * HALF_W], lo_[:, :, i * HALF_W:(i + 1) * HALF_W],
                    w[:, :, i * HALF_W:(i + 1) * HALF_W], ld)
                   for hi_, lo_, w, ld in ((wk_hi, wk_lo, wk, ld_k), (wv_hi, wv_lo, wv, ld_v)) for i in range(2)]
        SPLITS += [(wqT_hi[:, i * HALF_P:(i + 1) * HALF_P, :], wqT_lo[:, i * HALF_P:(i + 1) * HALF_P, :],
                    wqT[:, i * HALF_P:(i + 1) * HALF_P, :], ld_q) for i in range(2)]
        OF_K, OF_V, OF_Q = 1, 3, 5

        PREP_BANKS = 7

        blk = ctx.enter_context(nc.Block())

        @blk.sync
        def _(sp):
            sp.dma_start(cT[:, :, :], cT_in.rearrange("(c p) n -> p c n", p=P)).then_inc(ld_c, 16)
            sp.dma_start(wg0[:, :, :], a_wg.rearrange("(c p) n -> p c n", p=P)).then_inc(ld_a, 16)
            with nc.allow_non_contiguous_dma(reason="256 biases, once"):
                sp.dma_start(bg[:, :], a_bg.rearrange("(c p) -> p c", p=P)).then_inc(ld_a, 16)
            sp.dma_start(wo0[:, :, :], a_wo.rearrange("(c p) n -> p c n", p=P)).then_inc(ld_a, 16)
            sp.dma_start(bo[:, :], a_bo.rearrange("(o n) -> o n", o=1).broadcast_to([KEYS, D])).then_inc(ld_a, 16)
            sp.dma_start(logit[:, :], f_logits.rearrange("(o n) -> o n", o=1)).then_inc(ld_pick, 16)
            sp.dma_start(uni[:, :], f_u.rearrange("(o n) -> o n", o=1)).then_inc(ld_pick, 16)
            sp.dma_start(wk[:, :, :], b_wk.rearrange("(c p) n -> p c n", p=P)).then_inc(ld_k, 16)
            sp.dma_start(wv[:, :, :], b_wv.rearrange("(c p) n -> p c n", p=P)).then_inc(ld_v, 16)
            sp.dma_start(wqT[:, :, :], b_wqT.rearrange("(c p) n -> p c n", p=P)).then_inc(ld_q, 16)
            xb = x.rearrange("b (g p) d -> b p g d", p=P)
            sp.dma_start(xs[:, 0:BPB, :], xb[0]).then_inc(ld_x[0], 16)
            sp.dma_start(wo1[:, :, :], b_wo.rearrange("(c p) n -> p c n", p=P)).then_inc(ld_wo, 16)
            sp.wait_ge(picked_ok, 1)
            op = sp.value_load(picked[0:1, 0:1], min_val=0, max_val=OPS - 1)
            sp.dma_start(wsel[:, :, :], f_w[bass.ds(op, 1), :, :].rearrange("o (c p) n -> p (o c) n", p=P)).then_inc(ld_sel, 16)
            sp.dma_start(bsel[:, :], f_b[bass.ds(op, 1), :].broadcast_to([P, D])).then_inc(ld_sel, 16)
            sp.wait_ge(prep_mm, N_PREP)
            for b in range(1, B):
                sp.dma_start(xs[:, b * BPB:(b + 1) * BPB, :], xb[b]).then_inc(ld_x[b], 16)
            sp.wait_ge(b_sc, 3 * (B - 2) * BPB)
            for n, src in (("g", w_gateT), ("u", w_upT), ("d", w_downT)):
                sp.dma_start(raw[n][:, :].rearrange("p (c n) -> p c n", n=src.shape[1]),
                             src.rearrange("(c p) n -> p c n", p=P)).then_inc(ld_ffn, 16)
            outb = out.rearrange("b (g p) d -> (b g) p d", p=P)
            with sp.Fori(0, NB // 2) as i:
                for q in range(2):
                    sp.wait_ge(c_y, i * 2 + q + 1)
                    sp.dma_start(outb[bass.ds(i * 2 + q, 1), :, :].rearrange("o p d -> (o p) d"), y[:, q, :]).then_inc(st_out[q], 16)
            for q in range(2):
                sp.wait_ge(st_out[q], 16 * (NB // 2))

        @blk.gpsimd
        def _(pool):
            gp = nc.gpsimd
            gp.memset(ident[:, :], 0.0).then_inc(consts, 1)
            gp.memset(mhalf[:, :], -0.5).then_inc(consts, 1)
            gp.memset(ones[:, :], 1.0).then_inc(consts, 1)
            gp.memset(ones_b[:, :], 1.0).then_inc(consts, 1)
            pool.wait_ge(consts, 4)
            gp.affine_select(out=ident[:, :], in_=ident[:, :], compare_op=ALU.not_equal, fill=1.0, base=0,
                             pattern=[[-1, P]], channel_multiplier=1).then_inc(consts, 1)
            pool.wait_ge(consts, 5)
            gp.tensor_copy(ident_h[:, :], ident[:, :]).then_inc(consts, 1)

            def inverse_root(ready, mv, ve, rs, eps_done, done, free, g, par):
                wait_apart(pool, (ready, g + 1), *([(free, g - 1)] if free else []))
                gp.tensor_scalar(ve[:, par, :], mv[:, par, 1:2], EPS, 1.0, ALU.add, ALU.mult).then_inc(eps_done, 1)
                pool.wait_ge(eps_done, g + 1)
                gp.tensor_tensor(rs[:, par, :], ve[:, par, :], mhalf[:, :], ALU.pow).then_inc(done, 1)

            def norm_shift(mv, rs, sh, rstd_done, free, done, g, par):
                wait_apart(pool, (rstd_done, g + 1), (free, g - 1))
                gp.tensor_scalar(sh[:, par, :], mv[:, par, 0:1], rs[:, par, :], -1.0, ALU.mult, ALU.mult).then_inc(done, 1)

            pool.wait_ge(prep_mm, FIRST_M)
            gp.memset(pair_vT[:, :, :], 0.0).then_inc(v_zero, 1)

            def step_a(t, par, live):
                if live(7):
                    g = t - 7
                    pool.wait_ge(f_xn, g + 1)
                    if isinstance(g, int) and g == 0:
                        pool.wait_ge(ld_sel, 32)
                    gp.tensor_tensor(block(xs, g), block(xs, g), bsel[:, :], ALU.add).then_inc(f_bias, 1)
                if live(5):
                    inverse_root(f_mv, meanvar2, var_eps2, rstd2, f_eps, f_rstd, f_xn, t - 5, (par + 1) % 2)
                    norm_shift(meanvar2, rstd2, shift2, f_rstd, f_xn, f_shift, t - 5, (par + 1) % 2)
                if live(-1):
                    inverse_root(a_mv, meanvar, var_eps, rstd, a_eps, a_rstd, a_xn, t + 1, (par + 1) % 2)
                    norm_shift(meanvar, rstd, shift, a_rstd, a_xn, a_shift, t + 1, (par + 1) % 2)

            pipeline(pool, step_a, 9, NB + 2, lead=1)

            def pad_probabilities():
                gp.memset(e[:, :, HK:NCH * P], 0.0).then_inc(e_pad, 1)
                pool.wait_ge(e_pad, 1)

            def pair_values(b):
                for half in range(2):
                    rows = slice(half * HD, (half + 1) * HD)
                    at = PADV + half * KEYS
                    gp.tensor_copy(pair_vT[rows, :, at:at + KEYS],
                                   vT[rows, :, bass.ds(b, 1), :].rearrange("p c o k -> p c (o k)")).then_inc(v_pair, 1)
                    wait_apart(pool, (v_pair, 2 * b + half + 1))

            def step_b(t, par, live):
                if live(4):
                    inverse_root(n_mv, meanvar3, var_eps3, rstd3, n_eps, n_rstd, None, t - 4, par)
                    norm_shift(meanvar3, rstd3, shift3, n_rstd, n_ab, n_shift, t - 4, par)
                if live(0):
                    inverse_root(b_mv, meanvar, var_eps, rstd, b_eps, b_rstd, None, t, par)
                if live(2):
                    g, q = t - 2, par
                    for i, (h0, h1) in enumerate(HEAD_GROUPS):
                        pool.wait_ge(b_rden, 3 * g + i + 1)
                        eh = e[:, q, h0 * KEYS:h1 * KEYS].rearrange("p (h k) -> p h k", k=KEYS)
                        gp.tensor_tensor(eh, eh, rden[:, q, h0:h1].rearrange("p (h o) -> p h o", o=1).broadcast_to(
                            [P, h1 - h0, KEYS]), ALU.mult).then_inc(b_norm, 1)
                if isinstance(t, int) and t == T_SUM:
                    pool.wait_ge(w_abs, 1)
                    gp.partition_all_reduce(w_sum[:, :], abs_sum[:, :], P, bass.bass_isa.ReduceOp.add).then_inc(w_summed, 1)

            into_b(pool, step_a, step_b, pad_probabilities)
            stage_b(pool, step_b, lambda b: (pool.wait_ge(vw_mm, NCH * (b + 1)), pair_values(b + 1)), batches=range(B - 1))

            def step_c(t, par, live):
                if live(3):
                    g, q = t - 3, (par + 1) % 2
                    up = s_up[:, slot4(t, 3), :]
                    wait_apart(pool, (c_r2, g + 1), (c_hqf, g - 1))
                    gp.tensor_scalar(s_h[:, q, 0:1], r2[:, q, :], up, QMAX, ALU.mult, ALU.mult).then_inc(c_sh, 1)
                    wait_apart(pool, (c_sh, g + 1), (c_hT, g - 1))
                    gp.tensor_scalar(hq_f[:, q, :], h[:, q, :], s_h[:, q, 0:1], MAGIC_16, ALU.mult, ALU.add).then_inc(c_hqf, 1)

            into_c(pool, step_b, step_c)
            pipeline4(pool, step_c, 6)

        @blk.tensor
        def _(pe):
            mm = nc.tensor.matmul

            def split_mm(o, a_hi, a_lo, c_hi, c_lo, start, stop):
                mm(o, a_hi, c_hi, start=start, stop=False)
                mm(o, a_hi, c_lo, start=False, stop=False)
                return mm(o, a_lo, c_hi, start=False, stop=stop)

            pe.wait_ge(nz_ok, 1)
            pe.wait_ge(consts, 4)
            for c in range(DC):
                last = mm(bank[7][0:1, 0:B * KEYS], ones_b[:, 0:1], nonzero[:, c, :], start=c == 0, stop=c == DC - 1)
            last.then_inc(cnt_ok, 1)

            n = 0

            def free_bank():
                if n >= PREP_BANKS:
                    pe.wait_ge(prep_hi, n - PREP_BANKS + 1)
                    pe.wait_ge(prep_lo, low_parts(n - PREP_BANKS + 1))
                return bank[n % PREP_BANKS]

            pe.wait_ge(ld_c, 16)
            pe.wait_ge(ld_a, 64)
            for eo in range(DC):
                o = free_bank()[:, 0:B * KEYS]
                for c in range(DC):
                    last = mm(o, wg0[:, c, eo * P:(eo + 1) * P], cT[:, c, :], start=c == 0, stop=c == DC - 1)
                last.then_inc(prep_mm, 1)
                n += 1
            for b in range(B):
                o = free_bank()[0:KEYS, 0:D]
                for c in range(DC):
                    last = mm(o, cT[:, c, b * KEYS:(b + 1) * KEYS], wo0[:, c, :], start=c == 0, stop=c == DC - 1)
                last.then_inc(prep_mm, 1)
                n += 1

            def project_context(hi_, lo_, first):
                nonlocal n
                for p in range(PAIRS):
                    if p % HALF_P == 0:
                        pe.wait_ge(split_lo, first + p // HALF_P + 1)
                    o = free_bank()[:, 0:B * KEYS]
                    for c in range(DC):
                        cols = slice(p * P, (p + 1) * P)
                        last = split_mm(o, hi_[:, c, cols], lo_[:, c, cols], cT_hi[:, c, :], cT_lo[:, c, :], c == 0, c == DC - 1)
                    last.then_inc(prep_mm, 1)
                    n += 1

            project_context(wk_hi, wk_lo, OF_K)
            project_context(wv_hi, wv_lo, OF_V)
            for hh in range(H):
                rows = slice(HD * (hh % 2), HD * (hh % 2) + HD)
                pe.wait_ge(prep_hi, FIRST_K + hh // 2 + 1)
                pe.wait_ge(prep_lo, FIRST_K + hh // 2 + 1)
                pe.wait_ge(split_lo, OF_Q + hh // 2 // HALF_P + 1)
                for io in range(DC):
                    cols = slice(io * P, (io + 1) * P)
                    split_mm(free_bank()[:, 0:B * KEYS], wqT_hi[rows, hh // 2, cols], wqT_lo[rows, hh // 2, cols],
                             kT_hi[rows, hh // 2, :], kT_lo[rows, hh // 2, :], True, True).then_inc(prep_mm, 1)
                    n += 1

            def values_out(b):
                wait_apart(pe, (vw_hi, NCH * (b + 1)), (vw_lo, NCH * (b + 1)))

            def value_out(b, chunks=range(NCH), banks=(4, 5, 6)):
                pe.wait_ge(v_pair, 2 * b + 2)
                for j in chunks:
                    if j < 3:
                        wait(pe, b_pTlo, 3 * BPB * b)
                        wait(pe, b_pThi, 3 * BPB * b)
                    else:
                        pe.wait_ge(vw_hi, NCH * b + j - 2)
                        pe.wait_ge(vw_lo, NCH * b + j - 2)
                    ps = overlaps(j)
                    for p in ps:
                        at = P * j - 2 * KEYS * p + PADV
                        last = mm(bank[banks[j % 3]][:, 0:D], pair_vT[:, p, at:at + P], wo1[:, p, :],
                                  start=p == ps[0], stop=p == ps[-1])
                    last.then_inc(vw_mm, 1)
                if isinstance(b, int) and b == 0 and NCH - 1 in chunks:
                    values_out(b)

            pe.wait_ge(prep_hi, N_PREP)
            pe.wait_ge(prep_lo, low_parts(N_PREP))
            pe.wait_ge(consts, 6)
            T1, SC, ET, PV, T2, FF = (bank[0], bank[6]), bank[1], bank[2], bank[3], (bank[4], bank[7]), bank[5]

            COPIES = 3

            def step_a(t, par, live):
                if live(7):
                    g, q = t - 7, (par + 1) % 2
                    pe.wait_ge(f_xn, g + 1)
                    wait(pe, f_Tlo, g - 1)
                    for c in range(DC):
                        last = nc.tensor.transpose(T2[q][:, c * P:(c + 1) * P], xn2[:, q, c * P:(c + 1) * P], ident[:, :])
                    last.then_inc(f_T, 1)
                if live(1):
                    g, q = t - 1, (par + 1) % 2
                    pe.wait_ge(a_xn, g + 1)
                    wait(pe, a_Tlo, g - 1)
                    for c in range(DC):
                        last = nc.tensor.transpose(T1[q][:, c * P:(c + 1) * P], xn[:, q, c * P:(c + 1) * P], ident[:, :])
                    last.then_inc(a_T, 1)
                if live(3):
                    g, q = t - 3, (par + 1) % 2
                    pe.wait_ge(a_exp, g + 1)
                    wait(pe, a_eTlo, g)
                    nc.tensor.transpose(ET[0:KEYS, 0:P], e0[:, q, :], ident[:, :]).then_inc(a_eT, 1)
                if live(8):
                    g, q = t - 8, par
                    pe.wait_ge(f_Tlo, g + 1)
                    wait(pe, f_x2, g)
                    if isinstance(g, int) and g == 0:
                        pe.wait_ge(sel_hi, 2)
                    for c in range(DC):
                        last = split_mm(FF[:, 0:D], x2T_hi[:, q, c, :], x2T_lo[:, q, c, :], wsel_hi[:, c, :],
                                        wsel_lo[:, c, :], c == 0, c == DC - 1)
                    last.then_inc(f_mm, 1)
                if live(2):
                    g, q = t - 2, par
                    pe.wait_ge(a_Tlo, g + 1)
                    wait(pe, a_exp, g)
                    b = batch_of(g)
                    for c in range(DC):
                        gates = [gt[:, bass.ds(b, 1), c, :].broadcast_to([P, COPIES, KEYS + 1]) for gt in (gate_hi, gate_lo)]
                        last = split_mm(SC[:, 0:COPIES * (KEYS + 1)], xT_hi[:, q, c, :], xT_lo[:, q, c, :],
                                        gates[0], gates[1], c == 0, c == DC - 1)
                    last.then_inc(a_sc, 1)
                if live(4):
                    g, q = t - 4, par
                    pe.wait_ge(a_eTlo, g + 1)
                    wait(pe, f_x1, g)
                    b = batch_of(g)
                    split_mm(PV[:, 0:D], e0T_hi[:, q, :], e0T_lo[:, q, :],
                             cwo_hi[:, bass.ds(b, 1), :].rearrange("p o d -> p (o d)"),
                             cwo_lo[:, bass.ds(b, 1), :].rearrange("p o d -> p (o d)"), True, True).then_inc(a_pv, 1)
                if isinstance(t, int) and t in FIRST_VALUES:
                    value_out(0, FIRST_VALUES[t], (4, 5, 7))

            pipeline(pe, step_a, 9, NB + 2, lead=1)

            XT, SCB, PT, OB = bank[0], bank[1:4], bank[4:7], bank[7]

            def scores(g, q, b, i):
                h0, h1 = HEAD_GROUPS[i]
                w = (h1 - h0) * KEYS
                wait_apart(pe, (b_exp, 3 * g - 2 + i))
                mrow = mask_row[0:1, bass.ds(b, 1), :].broadcast_to([1, h1 - h0, KEYS])
                mm(SCB[i][:, 0:w], ones_b[0:1, :], mrow, start=True, stop=False)
                for c in range(DC):
                    ms = [m[:, bass.ds(b, 1), c, h0 * KEYS:h1 * KEYS].rearrange("p o d -> p (o d)") for m in (m_hi, m_lo)]
                    last = split_mm(SCB[i][:, 0:w], xT_hi[:, q, c, :], xT_lo[:, q, c, :], ms[0], ms[1], False, c == DC - 1)
                last.then_inc(b_sc, 1)

            def step_b(t, par, live):
                if live(2):
                    pe.wait_ge(b_Tlo, t - 1)
                    scores(t - 2, par, batch_of(t - 2), 0)
                if live(3):
                    g, q = t - 3, (par + 1) % 2
                    if isinstance(g, int) and g == 0:
                        pe.wait_ge(e_pad, 1)
                    wait(pe, b_pTlo, 3 * g)
                    if first_of[0] is not None:
                        values_out(first_of[0])
                    for i, (j0, j1) in enumerate(T_GROUPS):
                        pe.wait_ge(b_norm, 3 * g + min(i + 2, 3))
                        for j in range(j0, j1):
                            last = nc.tensor.transpose(PT[i][:, (j - j0) * P:(j - j0 + 1) * P],
                                                       e[:, q, j * P:(j + 1) * P], ident[:, :])
                        last.then_inc(b_pT, 1)
                if live(1):
                    g, q = t - 1, (par + 1) % 2
                    pe.wait_ge(b_xn, g + 1)
                    wait(pe, b_Tlo, g)
                    for c in range(DC):
                        last = nc.tensor.transpose(XT[:, c * P:(c + 1) * P], xn[:, q, c * P:(c + 1) * P], ident[:, :])
                    last.then_inc(b_T, 1)
                if live(2):
                    scores(t - 2, par, batch_of(t - 2), 1)
                    scores(t - 2, par, batch_of(t - 2), 2)
                if live(3):
                    g = t - 3
                    wait(pe, b_x3, g)
                    for i, (j0, j1) in enumerate(T_GROUPS):
                        pe.wait_ge(b_pTlo, 3 * g + 1 + i)
                        for j in range(j0, j1):
                            last = split_mm(OB[:, 0:D], pT_hi[:, j, :], pT_lo[:, j, :], vwo_hi[:, j, :], vwo_lo[:, j, :],
                                            j == 0, j == NCH - 1)
                    last.then_inc(b_pv, 1)

            into_b(pe, step_a, step_b)
            stage_b(pe, step_b, value_out)

            XQ, GU, HT, YB = bank[0], bank[1:5], [bank[i][:, :].bitcast(F16) for i in (5, 6)], bank[7]
            wg = wq_b["g"][:, :].rearrange("p (c n) -> p c n", c=DC)
            wu = wq_b["u"][:, :].rearrange("p (c n) -> p c n", c=DC)
            wd = wq_b["d"][:, :].rearrange("p (c n) -> p c n", c=IC)

            def step_c(t, par, live):
                if live(1):
                    g, q = t - 1, (par + 1) % 2
                    pe.wait_ge(c_qt, g + 1)
                    wait(pe, c_qT, g)
                    for c in range(DC):
                        last = nc.tensor.transpose(XQ[:, c * P:(c + 1) * P], q_t[:, q, c * P:(c + 1) * P], ident[:, :])
                    last.then_inc(c_T, 1)
                if live(2):
                    g, q = t - 2, par
                    pe.wait_ge(c_qT, g + 1)
                    if isinstance(g, int) and g == 0:
                        pe.wait_ge(w_ready, 6)
                    for i in range(4):
                        w, half = (wg, wu)[i % 2], i // 2
                        wait(pe, c_h, 2 * (g - 1) + half + 1)
                        for c in range(DC):
                            last = mm(GU[i][:, :], qT[:, q, c, :], w[:, c, half * BANK:(half + 1) * BANK],
                                      start=c == 0, stop=c == DC - 1)
                        last.then_inc(c_gu, 1)
                if live(4):
                    g, q = t - 4, par
                    pe.wait_ge(c_hqf, g + 1)
                    low = hq_f[:, q, :].bitcast(F16).rearrange("p (n two) -> p n two", two=2)[:, :, 0]
                    wait(pe, c_hqT, g - 1)
                    for j in range(IC):
                        last = nc.tensor.transpose(HT[q][:, j * P:(j + 1) * P], low[:, j * P:(j + 1) * P], ident_h[:, :])
                    last.then_inc(c_hT, 1)
                if live(5):
                    g, q = t - 5, (par + 1) % 2
                    pe.wait_ge(c_hqT, g + 1)
                    wait(pe, c_y, g)
                    for j in range(IC):
                        last = mm(YB[:, 0:D], hqT[:, q, j, :], wd[:, j, :], start=j == 0, stop=j == IC - 1)
                    last.then_inc(c_dn, 1)

            into_c(pe, step_b, step_c)
            pipeline4(pe, step_c, 6)

        @blk.scalar
        def _(act):
            sc = nc.scalar
            def split_high(first, last):
                for i in range(first, last):
                    act.wait_ge(SPLITS[i][3], 16)
                    sc.activation(SPLITS[i][0], SPLITS[i][2], ACT.Copy).then_inc(split_hi, 1)

            split_high(0, OF_K)
            act.wait_ge(ld_pick, 32)
            sc.activation(pick[:, 0, :], uni[:, :], ACT.Ln).then_inc(pick_ln, 1)
            act.wait_ge(pick_ln, 1)
            sc.activation(pick[:, 1, :], pick[:, 0, :], ACT.Ln, scale=-1.0).then_inc(pick_ln, 1)
            act.wait_ge(pick_z, 1)
            sc.activation(pick[:, 3, :], pick[:, 2, :], ACT.Exp, accum_out=pick[:, 4, 0:1]).then_inc(pick_ln, 1)
            act.wait_ge(pick_ln, 3)
            sc.activation(pick[:, 4, 1:2], pick[:, 4, 0:1], ACT.Ln).then_inc(pick_ln, 1)

            def hi_part(n, o, src, **kw):
                act.wait_ge(prep_mm, n + 1)
                return sc.activation(o, src, ACT.Copy, **kw)

            n = 0
            act.wait_ge(ld_a, 64)
            for eo in range(DC):
                act.wait_ge(prep_mm, n + 1)
                sc.activation(gate[:, eo, :], bank[n % PREP_BANKS][:, 0:B * KEYS], ACT.Identity,
                              bias=bg[:, eo:eo + 1]).then_inc(prep_hi, 1)
                n += 1
            for eo in range(DC):
                act.wait_ge(prep_hi, eo + 1)
                sc.activation(gate_hi[:, :, eo, 0:KEYS], gate[:, eo, :].rearrange("p (b k) -> p b k", b=B),
                              ACT.Copy).then_inc(k_gate, 1)
            split_high(OF_K, OF_V)
            for b in range(B):
                act.wait_ge(cwo_ok, b + 1)
                sc.activation(cwo_hi[:, b, :], cwo[:, :], ACT.Copy).then_inc(prep_hi, 1)
                n += 1
            for p in range(PAIRS):
                if p == 1:
                    split_high(OF_V, OF_Q)
                hi_part(n, kT_hi[:, p, :], bank[n % PREP_BANKS][:, 0:B * KEYS]).then_inc(prep_hi, 1)
                n += 1
            for p in range(PAIRS):
                if p == 1:
                    split_high(OF_Q, len(SPLITS))
                hi_part(n, vT[:, p, :, :].rearrange("p b k -> p (b k)"), bank[n % PREP_BANKS][:, 0:B * KEYS]).then_inc(prep_hi, 1)
                n += 1
            for hh in range(H):
                if hh == 4:
                    act.wait_ge(ld_sel, 32)
                    sc.activation(wsel_hi[:, :, :], wsel[:, :, :], ACT.Copy).then_inc(sel_hi, 1)
                    act.wait_ge(v_zero, 1)
                    act.wait_ge(prep_hi, FIRST_M)
                    for half in range(2):
                        rows, at = slice(half * HD, (half + 1) * HD), PADV + half * KEYS
                        sc.activation(pair_vT[rows, :, at:at + KEYS], vT[rows, :, 0, :], ACT.Copy).then_inc(v_pair, 1)
                for io in range(DC):
                    hi_part(n, m_hi[:, :, io, hh * KEYS:(hh + 1) * KEYS],
                            bank[n % PREP_BANKS][:, 0:B * KEYS].rearrange("p (b k) -> p b k", b=B),
                            scale=HD ** -0.5).then_inc(prep_hi, 1)
                    n += 1
            def take_hi(T_sem, bank_, dst, done, free, g, q, w):
                act.wait_ge(T_sem, g + 1)
                if free is not None:
                    wait(act, free, g - 1)
                sc.activation(dst[:, q, :, :].rearrange("p c n -> p (c n)"), bank_[:, 0:w], ACT.Copy).then_inc(done, 1)

            def normed(src, rs, sh, dst, ready, free, done, g, q):
                act.wait_ge(ready, g + 1)
                wait(act, free, g - 1)
                sc.activation(dst[:, q, :], src, ACT.Identity, scale=rs[:, q, :], bias=sh[:, q, :]).then_inc(done, 1)

            def value_hi(b, chunks=range(NCH), banks=(4, 5, 6)):
                for j in chunks:
                    act.wait_ge(vw_mm, NCH * b + j + 1)
                    if j == 0:
                        wait(act, b_pv, BPB * b)
                    sc.activation(vwo_hi[:, j, :], bank[banks[j % 3]][:, 0:D], ACT.Copy).then_inc(vw_hi, 1)

            def step_a(t, par, live):
                if live(7):
                    normed(block(xs, t - 7), rstd2, shift2, xn2, f_shift, f_T, f_xn, t - 7, (par + 1) % 2)
                if live(1):
                    normed(block(xs, t - 1), rstd, shift, xn, a_shift, a_T, a_xn, t - 1, (par + 1) % 2)
                if live(3):
                    g, q = t - 3, (par + 1) % 2
                    act.wait_ge(a_nmax, g + 1)
                    wait(act, a_eT, g - 1)
                    wait(act, a_rden, g - 1)
                    sc.activation(e0[:, q, :], bank[1][:, 0:KEYS], ACT.Exp, bias=nmax0[:, q, :],
                                  accum_out=den0[:, q, :]).then_inc(a_exp, 1)
                if live(7):
                    take_hi(f_T, bank[(4, 7)[(par + 1) % 2]], x2T_hi, f_Thi, f_mm, t - 7, (par + 1) % 2, D)
                if live(1):
                    take_hi(a_T, bank[(0, 6)[(par + 1) % 2]], xT_hi, a_Thi, a_sc, t - 1, (par + 1) % 2, D)
                if live(3):
                    g, q = t - 3, (par + 1) % 2
                    act.wait_ge(a_eT, g + 1)
                    wait(act, a_pv, g - 1)
                    sc.activation(e0T_hi[:, q, :], bank[2][0:KEYS, 0:P], ACT.Copy).then_inc(a_eThi, 1)
                if isinstance(t, int) and t in FIRST_VALUES:
                    value_hi(0, FIRST_VALUES[t], (4, 5, 7))

            pipeline(act, step_a, 9, NB + 2, lead=1)

            def exp_group(g, q, i):
                h0, h1 = HEAD_GROUPS[i]
                act.wait_ge(b_nmax, 3 * g + i + 1)
                for hh in range(h0, h1):
                    last = sc.activation(e[:, q, hh * KEYS:(hh + 1) * KEYS], bank[1 + i][:, (hh - h0) * KEYS:(hh - h0 + 1) * KEYS],
                                         ACT.Exp, bias=nmax[:, q, hh:hh + 1], accum_out=den[:, q, hh:hh + 1])
                last.then_inc(b_exp, 1)

            def step_b(t, par, live):
                if live(5):
                    normed(block(xs, t - 5), rstd3, shift3, xn3, n_shift, n_amax, n_xn, t - 5, (par + 1) % 2)
                if live(3):
                    g = t - 3
                    wait(act, b_pv, g)
                    for i, (j0, j1) in enumerate(T_GROUPS):
                        act.wait_ge(b_pT, 3 * g + i + 1)
                        sc.activation(pT_hi[:, j0:j1, :].rearrange("p c n -> p (c n)"), bank[4 + i][:, 0:(j1 - j0) * P],
                                      ACT.Copy).then_inc(b_pThi, 1)
                if live(2):
                    wait(act, b_pT, 3 * (t - 3))
                    exp_group(t - 2, par, 0)
                if live(1):
                    wait(act, b_sc, 3 * (t - 2))
                    take_hi(b_T, bank[0], xT_hi, b_Thi, None, t - 1, (par + 1) % 2, D)
                if live(2):
                    exp_group(t - 2, par, 1)
                    exp_group(t - 2, par, 2)

            into_b(act, step_a, step_b)
            stage_b(act, step_b, value_hi)

            def step_c(t, par, live):
                if live(0):
                    g, q = t, par
                    wait(act, c_T, g - 1)
                    sc.activation(q_t[:, q, :], block(xs, g), ACT.Identity, scale=a_all[:, bass.ds(g, 1)],
                                  bias=b_all[:, bass.ds(g, 1)]).then_inc(c_qt, 1)
                if live(2):
                    g, q = t - 2, par
                    act.wait_ge(c_scales, 2 * g + 2)
                    wait(act, c_h, 2 * (g - 1))
                    for half in range(2):
                        act.wait_ge(c_gu, 4 * g + 2 * half + 1)
                        sc.activation(silu[:, q, half * BANK:(half + 1) * BANK], bank[1 + 2 * half][:, :], ACT.Silu,
                                      scale=s_gate[:, slot4(t, 2), :]).then_inc(c_silu, 1)
                if live(4):
                    g, q = t - 4, par
                    wait(act, c_dn, g - 1)
                    act.wait_ge(c_hT, g + 1)
                    sc.activation(hqT[:, q, :, :].rearrange("p c n -> p (c n)"), bank[5 + q][:, :].bitcast(F16),
                                  ACT.Copy, bias=-OFFSET_16).then_inc(c_hqT, 1)
                if live(0):
                    g, q = t, par
                    if isinstance(g, int) and g == 0:
                        act.wait_ge(w_ready, 1)
                    wait(act, c_sh, g - 3)
                    for s_, w in ((s_gate, 0), (s_up, 1)):
                        sc.activation(s_[:, slot4(t, 0), :], c1_all[:, bass.ds(g, 1)], ACT.Copy,
                                      scale=w_mean[:, w:w + 1]).then_inc(c_scales, 1)
                if live(3):
                    g, q = t - 3, (par + 1) % 2
                    act.wait_ge(c_c2, g + 1)
                    wait(act, c_y, g - 3)
                    sc.activation(s_y[:, slot4(t, 3), :], c2[:, q, :], ACT.Copy, scale=w_mean[:, 3:4]).then_inc(c_sy, 1)

            into_c(act, step_b, step_c)
            pipeline4(act, step_c, 6)

        @blk.vector
        def _(dve):
            v = nc.vector
            seq = [0]

            def chain(ins):
                seq[0] += 1
                ins.then_inc(dve_seq, 1)
                dve.wait_ge(dve_seq, seq[0])

            dve.wait_ge(ld_c, 16)
            v.tensor_scalar(nonzero[:, :, :], cT[:, :, :], 0.0, None, ALU.not_equal).then_inc(nz_ok, 1)

            def split_low(first, last):
                for i in range(first, last):
                    dve.wait_ge(split_hi, i + 1)
                    v.tensor_tensor(SPLITS[i][1], SPLITS[i][2], SPLITS[i][0].bitcast(F32), ALU.subtract).then_inc(split_lo, 1)

            split_low(0, OF_K)
            v.memset(gate_hi[:, :, :, KEYS:KEYS + 1].bitcast(F32), 0.0)
            v.memset(gate_lo[:, :, :, KEYS:KEYS + 1].bitcast(F32), 0.0)
            dve.wait_ge(ld_pick, 32)
            chain(v.tensor_reduce(pick[:, 5, 0:1], logit[:, :], axis=AX, op=ALU.max))
            v.tensor_scalar(pick[:, 2, :], logit[:, :], pick[:, 5, 0:1], None, ALU.subtract).then_inc(pick_z, 1)
            dve.wait_ge(pick_ln, 4)
            chain(v.tensor_scalar(pick[:, 6, :], pick[:, 2, :], pick[:, 4, 1:2], None, ALU.subtract))
            chain(v.tensor_tensor(pick[:, 6, :], pick[:, 6, :], pick[:, 1, :], ALU.subtract))
            chain(v.max(pick[:, 7, :], pick[:, 6, :]))
            v.max_index(picked[:, :], pick[:, 7, :], pick[:, 6, :]).then_inc(picked_ok, 1)
            dve.wait_ge(cnt_ok, 1)
            v.tensor_scalar(mask_row[:, :, :].rearrange("p b k -> p (b k)"), bank[7][0:1, 0:B * KEYS], 0.0, MASKED,
                            ALU.is_equal, ALU.mult).then_inc(mask_ok, 1)

            n = 0
            for eo in range(DC):
                dve.wait_ge(k_gate, eo + 1)
                v.tensor_tensor(gate_lo[:, :, eo, 0:KEYS], gate[:, eo, :].rearrange("p (b k) -> p b k", b=B),
                                gate_hi[:, :, eo, 0:KEYS].bitcast(F32), ALU.subtract).then_inc(prep_lo, 1)
                n += 1
            dve.wait_ge(ld_a, 64)
            split_low(OF_K, OF_V)
            for b in range(B):
                dve.wait_ge(prep_mm, n + 1)
                v.tensor_tensor(cwo[:, :], bank[n % PREP_BANKS][0:KEYS, 0:D], bo[:, :], ALU.add).then_inc(cwo_ok, 1)
                dve.wait_ge(cwo_ok, b + 1)
                dve.wait_ge(prep_hi, n + 1)
                v.tensor_tensor(cwo_lo[:, b, :], cwo[:, :], cwo_hi[:, b, :].bitcast(F32), ALU.subtract).then_inc(prep_lo, 1)
                dve.wait_ge(prep_lo, n + 1)
                n += 1
            for p in range(PAIRS):
                if p == 1:
                    split_low(OF_V, OF_Q)
                dve.wait_ge(prep_hi, n + 1)
                v.tensor_tensor(kT_lo[:, p, :], bank[n % PREP_BANKS][:, 0:B * KEYS], kT_hi[:, p, :].bitcast(F32),
                                ALU.subtract).then_inc(prep_lo, 1)
                n += 1
            split_low(OF_Q, len(SPLITS))
            n += PAIRS
            for hh in range(H):
                for io in range(DC):
                    dve.wait_ge(prep_hi, n + 1)
                    v.scalar_tensor_tensor(out=m_lo[:, :, io, hh * KEYS:(hh + 1) * KEYS],
                                           in0=bank[n % PREP_BANKS][:, 0:B * KEYS].rearrange("p (b k) -> p b k", b=B),
                                           scalar=HD ** -0.5, in1=m_hi[:, :, io, hh * KEYS:(hh + 1) * KEYS].bitcast(F32),
                                           op0=ALU.mult, op1=ALU.subtract).then_inc(prep_lo, 1)
                    n += 1
            dve.wait_ge(sel_hi, 1)
            v.tensor_tensor(wsel_lo[:, :, :], wsel[:, :, :], wsel_hi[:, :, :].bitcast(F32), ALU.subtract).then_inc(sel_hi, 1)

            def normed(dst, src, mv, rs, rstd_sem, T_sem, done, g, q):
                dve.wait_ge(rstd_sem, g + 1)
                wait(dve, T_sem, g - 1)
                return v.tensor_scalar(dst[:, q, :], src, mv[:, q, 0:1], rs[:, q, :], ALU.subtract, ALU.mult).then_inc(done, 1)

            def take_lo(hi_sem, bank_, hi, lo, done, g, q):
                dve.wait_ge(hi_sem, g + 1)
                v.tensor_tensor(lo[:, q, :, :].rearrange("p c n -> p (c n)"), bank_[:, 0:D],
                                hi[:, q, :, :].rearrange("p c n -> p (c n)").bitcast(F32), ALU.subtract).then_inc(done, 1)

            def value_lo(b, chunks=range(NCH), banks=(4, 5, 6)):
                for j in chunks:
                    if j == 0:
                        wait(dve, b_pv, BPB * b)
                    dve.wait_ge(vw_hi, NCH * b + j + 1)
                    v.tensor_tensor(vwo_lo[:, j, :], bank[banks[j % 3]][:, 0:D], vwo_hi[:, j, :].bitcast(F32),
                                    ALU.subtract).then_inc(vw_lo, 1)

            def step_a(t, par, live):
                if live(3):
                    g, q = t - 3, (par + 1) % 2
                    dve.wait_ge(a_sc, g + 1)
                    wait(dve, a_exp, g - 1)
                    v.tensor_reduce(nmax0[:, q, :], bank[1][:, 0:KEYS], axis=AX, op=ALU.max, negate=True).then_inc(a_nmax, 1)
                if live(4):
                    g, q = t - 4, par
                    dve.wait_ge(a_eThi, g + 1)
                    wait(dve, a_pv, g - 1)
                    v.tensor_tensor(e0T_lo[:, q, :], bank[2][0:KEYS, 0:P], e0T_hi[:, q, :].bitcast(F32),
                                    ALU.subtract).then_inc(a_eTlo, 1)
                if live(9):
                    g = t - 9
                    dve.wait_ge(f_mm, g + 1)
                    dve.wait_ge(f_bias, g + 1)
                    v.tensor_tensor(block(xs, g), bank[5][:, 0:D], block(xs, g), ALU.add).then_inc(f_x2, 1)
                if live(8):
                    g, q = t - 8, par
                    wait(dve, f_mm, g - 1)
                    take_lo(f_Thi, bank[(4, 7)[q]], x2T_hi, x2T_lo, f_Tlo, g, q)
                if live(5):
                    g, q = t - 5, (par + 1) % 2
                    dve.wait_ge(a_pv, g + 1)
                    dve.wait_ge(a_rden, g + 1)
                    v.scalar_tensor_tensor(out=block(xs, g), in0=bank[3][:, 0:D], scalar=rden0[:, q, :], in1=block(xs, g),
                                           op0=ALU.mult, op1=ALU.add).then_inc(f_x1, 1)
                if live(2):
                    g, q = t - 2, par
                    wait(dve, a_sc, g - 1)
                    take_lo(a_Thi, bank[(0, 6)[q]], xT_hi, xT_lo, a_Tlo, g, q)
                if live(5):
                    g, q = t - 5, (par + 1) % 2
                    wait_apart(dve, (f_x1, g + 1))
                    v.bn_stats(stats2[:, q, :], block(xs, g)).then_inc(f_stats, 1)
                if live(-1):
                    g, q = t + 1, (par + 1) % 2
                    if isinstance(g, int) and g in (0, BPB, BPB + 3):
                        for b in {0: (0,), BPB: (1,), BPB + 3: range(2, B)}[g]:
                            dve.wait_ge(ld_x[b], 16)
                    v.bn_stats(stats[:, q, :], block(xs, g)).then_inc(a_stats, 1)
                if live(5):
                    g, q = t - 5, (par + 1) % 2
                    wait_apart(dve, (f_stats, g + 1), (f_shift, g - 1))
                    v.bn_aggr(meanvar2[:, q, :], stats2[:, q, :]).then_inc(f_mv, 1)
                if live(-1):
                    g, q = t + 1, (par + 1) % 2
                    wait_apart(dve, (a_stats, g + 1), (a_shift, g - 1))
                    v.bn_aggr(meanvar[:, q, :], stats[:, q, :]).then_inc(a_mv, 1)
                if live(4):
                    g, q = t - 4, par
                    dve.wait_ge(a_exp, g + 1)
                    wait(dve, f_x1, g - 1)
                    v.reciprocal(rden0[:, q, :], den0[:, q, :]).then_inc(a_rden, 1)
                if isinstance(t, int) and t in FIRST_VALUES:
                    value_lo(0, FIRST_VALUES[t], (4, 5, 7))

            pipeline(dve, step_a, 9, NB + 2, lead=1)

            names = ("g", "u", "d")

            def weights(t):
                i = t - (T_SUM - 3)
                if 0 <= i < 3:
                    if i == 0:
                        dve.wait_ge(ld_ffn, 48)
                    v.tensor_reduce(abs_sum[:, i:i + 1], raw[names[i]][:, :], axis=AX, op=ALU.add, apply_absolute_value=True)
                    if i == 2:
                        v.memset(abs_sum[:, 3:4], 1.0).then_inc(w_abs, 1)
                for i in range(2 * (t - T_SUM - 1), 2 * (t - T_SUM)) if T_SUM < t <= T_SUM + 3 else ():
                    if i == 0:
                        dve.wait_ge(w_summed, 1)
                        chain(v.tensor_scalar(w_mean[:, :], w_sum[:, :], 1.0 / (D * INNER), CLIP, ALU.mult, ALU.max))
                        chain(v.reciprocal(w_inv[:, :], w_mean[:, :]))
                        chain(v.tensor_scalar(w_mean[:, 3:4], w_mean[:, 2:3], 1.0 / QMAX, None, ALU.mult))
                    n, cols = i // 2, slice(i % 2 * INNER, i % 2 * INNER + INNER)
                    chain(v.tensor_scalar(wtmp[:, :], raw[names[n]][:, cols], w_inv[:, n:n + 1], MAGIC, ALU.mult, ALU.add))
                    chain(v.tensor_scalar(wtmp_b[:, :], wtmp[:, :], MAGIC, 1.0, ALU.subtract, ALU.min))
                    v.tensor_scalar(wq_b[names[n]][:, cols], wtmp_b[:, :], -1.0, None, ALU.max).then_inc(w_ready, 1)

            def head_max(g, q, i):
                h0, h1 = HEAD_GROUPS[i]
                dve.wait_ge(b_sc, 3 * g + i + 1)
                v.tensor_reduce(nmax[:, q, h0:h1], bank[1 + i][:, 0:(h1 - h0) * KEYS].rearrange("p (h k) -> p h k", k=KEYS),
                                axis=AX, op=ALU.max, negate=True).then_inc(b_nmax, 1)

            def head_reciprocal(g, q, i):
                h0, h1 = HEAD_GROUPS[i]
                dve.wait_ge(b_exp, 3 * g + i + 1)
                v.reciprocal(rden[:, q, h0:h1], den[:, q, h0:h1]).then_inc(b_rden, 1)

            def step_b(t, par, live):
                g2, q2 = t - 2, par
                if live(5):
                    g, q = t - 5, (par + 1) % 2
                    dve.wait_ge(n_xn, g + 1)
                    v.tensor_reduce(amax[:, q, :], xn3[:, q, :], axis=AX, op=ALU.max, apply_absolute_value=True).then_inc(n_amax, 1)
                if live(2):
                    wait(dve, b_exp, 3 * (g2 - 1))
                    head_max(g2, q2, 0)
                if live(5):
                    g, q = t - 5, (par + 1) % 2
                    dve.wait_ge(n_amax, g + 1)
                    v.tensor_scalar(c1_all[:, bass.ds(g, 1)], amax[:, q, :], 1.0 / QMAX, CLIP / QMAX, ALU.mult, ALU.max).then_inc(n_c1, 1)
                if live(3):
                    g = t - 3
                    wait(dve, b_pv, g)
                    for i, (j0, j1) in enumerate(T_GROUPS):
                        dve.wait_ge(b_pThi, 3 * g + i + 1)
                        v.tensor_tensor(pT_lo[:, j0:j1, :].rearrange("p c n -> p (c n)"), bank[4 + i][:, 0:(j1 - j0) * P],
                                        pT_hi[:, j0:j1, :].rearrange("p c n -> p (c n)").bitcast(F32),
                                        ALU.subtract).then_inc(b_pTlo, 1)
                if live(5):
                    g, q = t - 5, (par + 1) % 2
                    wait_apart(dve, (n_c1, g + 1))
                    v.reciprocal(r1[:, q, :], c1_all[:, bass.ds(g, 1)]).then_inc(n_r1, 1)
                if live(0):
                    v.bn_stats(stats[:, par, :], block(xs, t)).then_inc(b_stats, 1)
                if live(4):
                    wait_apart(dve, (b_x3, t - 3))
                    v.bn_stats(stats3[:, par, :], block(xs, t - 4)).then_inc(n_stats, 1)
                if live(2):
                    head_max(g2, q2, 1)
                if live(0):
                    wait_apart(dve, (b_stats, t + 1), (b_rstd, t - 1))
                    v.bn_aggr(meanvar[:, par, :], stats[:, par, :]).then_inc(b_mv, 1)
                if live(2):
                    head_max(g2, q2, 2)
                if live(4):
                    wait_apart(dve, (n_stats, t - 3), (n_shift, t - 5))
                    v.bn_aggr(meanvar3[:, par, :], stats3[:, par, :]).then_inc(n_mv, 1)
                if live(1):
                    g, q = t - 1, (par + 1) % 2
                    wait(dve, b_sc, 3 * (g - 1))
                    take_lo(b_Thi, bank[0], xT_hi, xT_lo, b_Tlo, g, q)
                if live(2):
                    wait(dve, b_norm, 3 * (g2 - 1))
                    head_reciprocal(g2, q2, 0)
                if live(5):
                    g, q = t - 5, (par + 1) % 2
                    dve.wait_ge(n_r1, g + 1)
                    v.tensor_tensor(a_all[:, bass.ds(g, 1)], rstd3[:, q, :], r1[:, q, :], ALU.mult)
                    v.tensor_tensor(b_all[:, bass.ds(g, 1)], shift3[:, q, :], r1[:, q, :], ALU.mult).then_inc(n_ab, 1)
                if live(2):
                    head_reciprocal(g2, q2, 1)
                if live(0):
                    normed(xn, block(xs, t), meanvar, rstd, b_rstd, b_T, b_xn, t, par)
                if live(2):
                    head_reciprocal(g2, q2, 2)
                if isinstance(t, int):
                    weights(t)
                if live(3):
                    g = t - 3
                    dve.wait_ge(b_pv, g + 1)
                    v.tensor_tensor(block(xs, g), bank[7][:, 0:D], block(xs, g), ALU.add).then_inc(b_x3, 1)

            into_b(dve, step_a, step_b)
            stage_b(dve, step_b, value_lo)

            def step_c(t, par, live):
                if live(3):
                    g, q = t - 3, (par + 1) % 2
                    dve.wait_ge(c_hmax, g + 1)
                    dve.wait_ge(c_scales, 2 * g + 2)
                    wait(dve, c_sh, g - 1)
                    wait(dve, c_sy, g - 1)
                    v.tensor_scalar(c2[:, q, :], hmax[:, q, :], s_up[:, slot4(t, 3), :], CLIP, ALU.mult, ALU.max).then_inc(c_c2, 1)
                if live(1):
                    g, q = t - 1, (par + 1) % 2
                    dve.wait_ge(c_T, g + 1)
                    wait(dve, c_gu, 4 * (g - 1))
                    v.tensor_scalar(qT[:, q, :, :].rearrange("p c n -> p (c n)"), bank[0][:, 0:D], MAGIC, MAGIC,
                                    ALU.add, ALU.subtract).then_inc(c_qT, 1)
                if live(3):
                    g, q = t - 3, (par + 1) % 2
                    dve.wait_ge(c_c2, g + 1)
                    v.reciprocal(r2[:, q, :], c2[:, q, :]).then_inc(c_r2, 1)
                if live(6):
                    g, q = t - 6, par
                    dve.wait_ge(c_dn, g + 1)
                    dve.wait_ge(c_sy, g + 1)
                    if not isinstance(g, int) or g >= 2:
                        dve.wait_ge(st_out[q], 8 * (g - q))
                    v.scalar_tensor_tensor(out=y[:, q, :], in0=bank[7][:, 0:D], scalar=s_y[:, slot4(t, 6), :], in1=block(xs, g),
                                           op0=ALU.mult, op1=ALU.add).then_inc(c_y, 1)
                if live(2):
                    g, q = t - 2, par
                    wait(dve, c_hqf, g - 1)
                    for half in range(2):
                        cols = slice(half * BANK, (half + 1) * BANK)
                        dve.wait_ge(c_gu, 4 * g + 2 * half + 2)
                        dve.wait_ge(c_silu, 2 * g + half + 1)
                        v.tensor_tensor(h[:, q, cols], bank[2 + 2 * half][:, :], silu[:, q, cols], ALU.mult).then_inc(c_h, 1)
                    dve.wait_ge(c_h, 2 * g + 2)
                    v.tensor_reduce(hmax[:, q, :], h[:, q, :], axis=AX, op=ALU.max, apply_absolute_value=True).then_inc(c_hmax, 1)

            into_c(dve, step_b, step_c)
            pipeline4(dve, step_c, 6)


def kernel(**inputs):
    import numpy as np
    import concourse.bacc as bacc
    from concourse.bass_utils import run_bass_kernel_spmd

    def arr(name):
        return np.asarray(inputs[name])

    def head_major(w):
        return w.reshape(D, HD, H).transpose(0, 2, 1).reshape(D, H * HD)

    layout = {
        "x": arr("x"),
        "cT": arr("ctx_1024").reshape(B * KEYS, D).T,
        "a_wg": arr("L0_xattn_Wg"), "a_bg": arr("L0_xattn_bg"), "a_wo": arr("L0_xattn_Wo"), "a_bo": arr("L0_xattn_bo"),
        "f_w": arr("L0_ffn_W"), "f_b": arr("L0_ffn_b"), "f_logits": arr("L0_ffn_logits"), "f_u": arr("L0_ffn_u"),
        "b_wqT": arr("L1_xattn_Wq").T, "b_wk": head_major(arr("L1_xattn_Wk")), "b_wv": head_major(arr("L1_xattn_Wv")),
        "b_wo": arr("L1_xattn_Wo"),
        "w_gateT": arr("L1_ffn_w_gate").T, "w_upT": arr("L1_ffn_w_up").T, "w_downT": arr("L1_ffn_w_down").T,
    }
    arrays = {"in_" + n: np.ascontiguousarray(a) for n, a in layout.items()}
    nc = bacc.Bacc("TRN2", target_bir_lowering=False, num_devices=1)
    aps = [nc.dram_tensor(n, a.shape, F32, kind="ExternalInput").ap() for n, a in arrays.items()]
    out = nc.dram_tensor("out_0", (B, S, D), F32, kind="ExternalOutput").ap()
    build(nc, *aps, out)
    return run_bass_kernel_spmd(nc, [arrays], core_ids=[0]).results[0]["out_0"]
```
